# Optimizing a Trainium2 kernel written in Bass

```python
import numpy as np
import jax
import jax.numpy as jnp

def _softmax(x, axis=-1):
    return jax.nn.softmax(x, axis=axis)

def _gelu(x):
    return jax.nn.gelu(x, approximate=True)

def _silu(x):
    return jax.nn.silu(x)

def _sigmoid(x):
    return jax.nn.sigmoid(x)

def _layernorm(x, axis=-1, eps=1e-05):
    m = jnp.mean(x, axis=axis, keepdims=True)
    v = jnp.var(x, axis=axis, keepdims=True)
    return (x - m) / jnp.sqrt(v + eps)

def _scatter_add(tgt, idx, src, axis=0):
    return tgt.at[idx].add(src)

def _segment_sum(src, seg, n):
    return jax.ops.segment_sum(src, seg, n)
kernel_name = 'mk_adaln_d1_jaxref_r4_b07c2d'

def setup_inputs(seed: int=0):
    np.random.seed(seed)
    _w = jnp.asarray

    def _L0_attn_setup():
        import jax, jax.numpy as jnp
        import numpy as np
        B, P, D = (8, 256, 256)
        H, N = (16, 64)
        key = jax.random.key(seed)
        k1, k2, k3 = jax.random.split(key, 3)
        inputs = jax.random.normal(k1, (B, P, D), dtype=jnp.float32)
        w_qkv = jax.random.normal(k2, (H, 3, D, N), dtype=jnp.float32) * 0.05
        w_o = jax.random.normal(k3, (N * H, D), dtype=jnp.float32) * 0.05
        return {'inputs': inputs, 'w_qkv': w_qkv, 'w_o': w_o}
    _L0_attn_in = _L0_attn_setup()

    def _L0_ffn_setup():
        import jax, jax.numpy as jnp
        import numpy as np
        B, S, HID, DFF, E, K = (4, 512, 256, 1024, 8, 512)
        key = jax.random.key(seed)
        ks = jax.random.split(key, 4)
        sc_h = 1.0 / np.sqrt(HID)
        sc_f = 1.0 / np.sqrt(DFF)
        return {'x': jax.random.normal(ks[0], (B, S, HID), jnp.float32), 'router_w': jax.random.normal(ks[1], (HID, E), jnp.float32) * sc_h, 'router_b': jnp.zeros((E,), jnp.float32), 'w1': jax.random.normal(ks[2], (E, HID, DFF), jnp.float32) * sc_h, 'b1': jnp.zeros((E, DFF), jnp.float32), 'w2': jax.random.normal(ks[3], (E, DFF, HID), jnp.float32) * sc_f, 'b2': jnp.zeros((E, HID), jnp.float32)}
    _L0_ffn_in = _L0_ffn_setup()
    _L0_c = _w((lambda *s: np.random.randn(*s).astype(np.float32) * 0.05)(8, 256))
    _L0_wmod = _w((lambda *s: np.random.randn(*s).astype(np.float32) * 0.05)(256, 6 * 256) * 256 ** (-0.5))
    _d = {'L0_attn_inputs': _L0_attn_in['inputs'], 'L0_attn_w_qkv': _L0_attn_in['w_qkv'], 'L0_attn_w_o': _L0_attn_in['w_o'], 'L0_ffn_router_w': _L0_ffn_in['router_w'], 'L0_ffn_router_b': _L0_ffn_in['router_b'], 'L0_ffn_w1': _L0_ffn_in['w1'], 'L0_ffn_b1': _L0_ffn_in['b1'], 'L0_ffn_w2': _L0_ffn_in['w2'], 'L0_ffn_b2': _L0_ffn_in['b2'], 'L0_c': _L0_c, 'L0_wmod': _L0_wmod}
    _x0 = _d['L0_attn_inputs']
    _d['L0_attn_inputs'] = jax.random.normal(jax.random.fold_in(jax.random.key(seed), 1), (8, 1024, 256), dtype=_x0.dtype)
    del _x0
    return _d

def reference(L0_attn_inputs, L0_attn_w_qkv, L0_attn_w_o, L0_ffn_router_w, L0_ffn_router_b, L0_ffn_w1, L0_ffn_b1, L0_ffn_w2, L0_ffn_b2, L0_c, L0_wmod):

    def _L0_attn_ref(inputs, w_qkv, w_o):
        import jax, jax.numpy as jnp
        import numpy as np
        B, P, D = (8, 256, 256)
        H, N = (16, 64)
        proj = jnp.einsum('bpv,havn->bhapn', inputs, w_qkv)
        q = proj[:, :, 0]
        k = proj[:, :, 1]
        v = proj[:, :, 2]
        head_dim = q.shape[-1]
        scale = 1.0 / jnp.sqrt(jnp.asarray(head_dim, dtype=jnp.float32))
        scores = jnp.einsum('bhqn,bhkn->bhqk', q, k) * scale
        attn = jax.nn.softmax(scores, axis=-1)
        out = jnp.einsum('bhqk,bhkn->bhqn', attn, v)
        b, h, p, n = out.shape
        concat = out.transpose(0, 2, 1, 3).reshape(b, p, h * n)
        return jnp.einsum('bpi,ij->bpj', concat, w_o)

    def _L0_ffn_ref(x, router_w, router_b, w1, b1, w2, b2):
        import jax, jax.numpy as jnp
        import numpy as np
        B, S, HID, DFF, E, K = (4, 512, 256, 1024, 8, 512)
        b, s, h = x.shape
        xf = x.reshape(-1, h)
        logits = xf @ router_w + router_b
        scores = jax.nn.softmax(logits, axis=-1)
        G, idx = jax.lax.top_k(scores.T, K)
        toks = xf[idx]
        h1 = jax.nn.relu(jnp.einsum('ekh,ehf->ekf', toks, w1) + b1[:, None, :])
        eo = jnp.einsum('ekf,efh->ekh', h1, w2) + b2[:, None, :]
        contrib = (eo * G[..., None]).reshape(-1, h)
        y = jnp.zeros_like(xf).at[idx.reshape(-1)].add(contrib)
        return y.reshape(b, s, h)
    x = L0_attn_inputs
    mod = (_silu(L0_c) @ L0_wmod).reshape(L0_c.shape[0], 6, 1, -1)
    sa, ca, ga, sb, cb, gb = (mod[:, 0], mod[:, 1], mod[:, 2], mod[:, 3], mod[:, 4], mod[:, 5])
    ga = (2 * (ga >= 0) - 1) * jnp.maximum(jnp.abs(ga), 0.25)
    gb = (2 * (gb >= 0) - 1) * jnp.maximum(jnp.abs(gb), 0.25)
    h = _layernorm(x, axis=-1) * (1 + ca) + sa
    x = x + ga * _L0_attn_ref(h, L0_attn_w_qkv, L0_attn_w_o)
    h = _layernorm(x, axis=-1) * (1 + cb) + sb
    x = x + gb * _L0_ffn_ref(h, L0_ffn_router_w, L0_ffn_router_b, L0_ffn_w1, L0_ffn_b1, L0_ffn_w2, L0_ffn_b2)
    return x

_drawn_inputs = setup_inputs


def setup_inputs(seed=0):
    import zlib

    import numpy as np

    out = dict(_drawn_inputs(seed))
    spreads = {'L0_ffn_router_b': (0.0, 2.0), 'L0_ffn_b1': (0.0, 2.0), 'L0_ffn_b2': (0.0, 2.0)}
    factors = {'L0_attn_w_qkv': 3.036, 'L0_attn_w_o': 3.014}
    for name, (base, spread) in spreads.items():
        noise = np.random.default_rng([zlib.crc32(name.encode()), seed]).standard_normal(out[name].shape)
        drawn = base * np.exp(spread * noise) if base else spread * noise
        out[name] = jnp.asarray(drawn.astype(out[name].dtype))
    for name, factor in factors.items():
        out[name] = (out[name] * factor).astype(out[name].dtype)
    return out
```

```python
from contextlib import ExitStack

import concourse.bass as bass
from concourse import mybir

F32 = mybir.dt.float32
F32R = mybir.dt.float32r
BF16 = mybir.dt.bfloat16
F16 = mybir.dt.float16
I32 = mybir.dt.int32
U32 = mybir.dt.uint32
ALU = mybir.AluOpType
ACT = mybir.ActivationFunctionType
AX = mybir.AxisListType

LN_EPS = 1e-5
GATE_FLOOR = 0.25
PART = 128
HALF = 512

LOW_ON_DVE = (0, 3, 6)
LOW_ON_POOL = (1, 2, 4, 5, 7)
MAX_BEFORE = {3: 0, 4: 1, 5: 3, 6: 5, 7: 7}
MAX_AFTER = {4: 2, 5: 4, 6: 6}


def count_upto(tiles, j):
    return sum(1 for t in tiles if t <= j)


def build_kernel(nc, x, w_qkv, w_o, router_w, router_b, w1, b1, w2, b2, c, wmod, out, topk):
    B, P, D = x.shape
    H, _, _, N = w_qkv.shape
    E, _, F = w1.shape
    NQ = P // PART
    KT = D // PART
    HT = H * N // PART
    NB = B * P // PART
    SCALE = float(N) ** -0.5
    VW = 3 * (N + 1)
    VHI = 3 * N + 2
    VLO = 2 * N + 1
    ST = topk // PART
    FT = F // PART
    ROW = D + E
    SLOT_LO = 32
    SLOT_HI = topk // SLOT_LO
    assert NQ == 8 and KT == 2 and N == 64 and D == 256 and E == 8 and HALF == E * N

    x_t = x.rearrange("b (q p) d -> b p q d", p=PART)
    out_t = out.rearrange("b (q p) d -> b p q d", p=PART)
    out_rows = out.rearrange("b p d -> (b p) d")
    rows_dram = nc.dram_tensor("rows_dram", (B * P, ROW), F32, kind="Internal").ap()
    rows_t = rows_dram.rearrange("(b q p) r -> b p q r", p=PART, q=NQ)
    rows_blk = rows_dram.rearrange("(n p) r -> p n r", p=PART)
    mods_dram = nc.dram_tensor("mods_dram", (B, 4 * D), F32, kind="Internal").ap()
    gate_dram = nc.dram_tensor("gate_dram", (B, D), F32, kind="Internal").ap()
    slots_dram = nc.dram_tensor("slots_dram", (E, topk), U32, kind="Internal").ap()

    with ExitStack() as outer:
        def keep(name, shape, dt):
            return outer.enter_context(nc.sbuf_tensor(name, shape, dt))

        ident = keep("ident", [PART, PART], F32)
        ident_bf = keep("ident_bf", [PART, PART], BF16)
        logits = keep("logits", [PART, NB, E], F32)
        minus_half = keep("minus_half", [PART, NQ], F32)

        attention_phase(nc, locals())
        ffn_phase(nc, locals())


def attention_phase(nc, k):
    B, P, D, H, N, E = k["B"], k["P"], k["D"], k["H"], k["N"], k["E"]
    NQ, KT, HT, SCALE, VW, VHI, VLO = k["NQ"], k["KT"], k["HT"], k["SCALE"], k["VW"], k["VHI"], k["VLO"]
    ident, ident_bf, logits, minus_half = k["ident"], k["ident_bf"], k["logits"], k["minus_half"]
    x_t, out_t, rows_t, mods_dram, gate_dram = k["x_t"], k["out_t"], k["rows_t"], k["mods_dram"], k["gate_dram"]
    w_qkv, w_o, router_w, router_b, c, wmod = k["w_qkv"], k["w_o"], k["router_w"], k["router_b"], k["c"], k["wmod"]
    HG = HALF // N
    NG = H // HG
    LD, LP = len(LOW_ON_DVE), len(LOW_ON_POOL)
    NM = 6 * KT

    with ExitStack() as ctx:
        def sb(name, shape, dt):
            return ctx.enter_context(nc.sbuf_tensor(name, shape, dt))

        def ps(name, shape):
            return ctx.enter_context(nc.psum_tensor(name, shape, F32))

        def sem(name):
            return ctx.enter_context(nc.semaphore(name))

        silu_t = sb("silu_t", [PART, KT, B], F32)
        sig_t = sb("sig_t", [PART, KT, B], F32)
        c_t = sb("c_t", [PART, KT, B], F32)
        mod_t = sb("mod_t", [PART, 2 * KT, B], F32)
        mod_b = sb("mod_b", [PART, 2 * KT], F32)
        stats = sb("stats", [PART, NQ, 6], F32)
        mean = sb("mean", [PART, NQ], F32)
        mean_d = sb("mean_d", [PART, NQ], F32)
        var_eps = sb("var_eps", [PART, NQ], F32)
        rstd = sb("rstd", [PART, NQ], F32)
        h_t = sb("h_t", [PART, KT, P], F32)
        rw_sb = sb("rw_sb", [PART, KT, E], F32)
        rb_bc = sb("rb_bc", [PART, E], F32)
        wqk = [sb(f"wqk{u}", [PART, KT, 2, N], F32) for u in range(2)]
        q_hh = [sb(f"q_hh{u}", [PART, P], F32R) for u in range(2)]
        q_lc = [sb(f"q_lc{u}", [PART, P], F32R) for u in range(2)]
        k_hl = [sb(f"k_hl{u}", [PART, P], F32R) for u in range(2)]
        k_h1 = [sb(f"k_h1{u}", [PART, P], F32R) for u in range(2)]
        row_max = sb("row_max", [PART, NQ], F32)
        neg_max = sb("neg_max", [PART, NQ], BF16)
        prob = sb("prob", [PART, 4, P], F32)
        p_hi = [sb(f"p_hi{u}", [PART, NQ, P], F16) for u in range(2)]
        p_lo = [sb(f"p_lo{u}", [PART, NQ, P], F16) for u in range(2)]
        v_all = sb("v_all", [PART, NQ, H, VW], BF16)
        pv_sum = sb("pv_sum", [PART, 2, 2, N], F32)
        pv_inv = sb("pv_inv", [PART, 2, 2], F32)
        heads = sb("heads", [PART, NQ, H * N], F32)

        def view(tensor, first, n):
            return tensor[:].rearrange("p q k -> p (q k)")[:, 2 * first:2 * (first + n)].bitcast(F32)

        x_sb = view(p_hi[0], 0, NQ * D).rearrange("p (q d) -> p q d", q=NQ)
        norm = view(p_hi[0], NQ * D, NQ * D).rearrange("p (q d) -> p q d", q=NQ)
        wv_sb = view(p_hi[1], 0, KT * H * N).rearrange("p (t h n) -> p t h n", t=KT, h=H)
        mod_rows = view(p_hi[1], KT * H * N, 3 * D).rearrange("p (m d) -> p m d", m=3)
        v_rest = view(p_hi[1], KT * H * N + 3 * D, 2 * HALF).rearrange("p (u n) -> p u n", u=2)
        wo_sb = view(p_lo[0], 0, HT * D).rearrange("p (t d) -> p t d", t=HT)
        heads_t = [view(p_lo[0], HT * (D + u * PART), HT * PART).rearrange("p (t n) -> p t n", t=HT) for u in range(2)]
        x1_sb = view(p_lo[1], 0, NQ * D).rearrange("p (q d) -> p q d", q=NQ)
        wmod_sb = view(p_lo[1], 0, KT * 6 * D).rearrange("p (t m) -> p t m", t=KT)
        mods = view(p_lo[1], KT * 6 * D, 4 * D).rearrange("p (m d) -> p m d", m=4)[0:B]
        mods_s = prob[0:B, 0, 0:4 * D].rearrange("p (m d) -> p m d", m=4)

        st_ps = [ps(f"st_ps{u}", [PART, P]) for u in range(2)]
        max_ps = ps("max_ps", [PART, P])
        pv_ps = ps("pv_ps", [PART, HALF])
        ms_ps = ps("ms_ps", [PART, HALF])

        const_ld = sem("const_ld")
        ident_z = sem("ident_z")
        ident_ok = sem("ident_ok")
        fill_ok = sem("fill_ok")
        c_exp = sem("c_exp")
        c_silu = sem("c_silu")
        mod_mm = sem("mod_mm")
        mod_ok = sem("mod_ok")
        x_ld = sem("x_ld")
        ln = sem("ln")
        ln_pow = sem("ln_pow")
        tr_mm = sem("tr_mm")
        tr_ev = sem("tr_ev")
        v_mm = sem("v_mm")
        v1_ok = sem("v1_ok")
        v_sub = sem("v_sub")
        v2_ok = sem("v2_ok")
        v3_ok = sem("v3_ok")
        wqk_ld = [sem(f"wqk_ld{u}") for u in range(2)]
        proj_mm = sem("proj_mm")
        high_ok = sem("high_ok")
        low_ok = sem("low_ok")
        dup_ok = [sem(f"dup_ok{u}") for u in range(2)]
        max_mm = sem("max_mm")
        max_red = sem("max_red")
        neg_ok = sem("neg_ok")
        crow_mm = sem("crow_mm")
        crow_ok = sem("crow_ok")
        st_mm = sem("st_mm")
        exp_ok = sem("exp_ok")
        phi_ok = sem("phi_ok")
        plo_dve = sem("plo_dve")
        plo_pool = sem("plo_pool")
        pv_mm = sem("pv_mm")
        pv_red = sem("pv_red")
        pv_ev = sem("pv_ev")
        head_ok = sem("head_ok")
        ht_mm = sem("ht_mm")
        ht_ev = sem("ht_ev")
        o_mm = sem("o_mm")
        gated = sem("gated")
        x1_ok = sem("x1_ok")
        h2n_ok = sem("h2n_ok")
        h2m_ok = sem("h2m_ok")
        h2_ok = sem("h2_ok")
        lg_mm = sem("lg_mm")
        lg_ok = sem("lg_ok")
        st_rows = sem("st_rows")

        EXP_CREDIT, PV_CREDIT, VSUB_CREDIT, V3_CREDIT, HEAD_CREDIT = 2, 5, 4, 2, 2
        LN_STEPS = 1 + (NQ + 6 + NQ - 1) + (NQ - 1) + (6 + NQ - 1)
        N_CONST = 5

        wv_ld = sem("wv_ld")
        wo_ld = sem("wo_ld")
        mods_st = sem("mods_st")
        mods_ld = sem("mods_ld")
        ln_ok = sem("ln_ok")
        ln_pow_in = sem("ln_pow_in")
        x1_row = sem("x1_row")

        block = ctx.enter_context(nc.Block())

        def run_heads(eng, head):
            head(0, 0, True)
            head(1, 1, False)
            with eng.Fori(1, H // 2 - 1) as hp:
                head(hp * 2, 0, False)
                head(hp * 2 + 1, 1, False)
            head(H - 2, 0, False)
            head(H - 1, 1, False)

        def pair_dmas(b, t, u):
            return b * (H * 16) + (t - u) * 16 + 32

        def tile_cols(j):
            return slice(j * PART, (j + 1) * PART)

        def half_cols(h):
            return slice(h * HALF, (h + 1) * HALF)

        @block.sync
        def _(sp):
            for t in range(KT):
                sp.dma_start(c_t[:, t, :], c[:, t * PART:(t + 1) * PART].rearrange("b p -> p b"),
                             allow_slow_non_contiguous=True).then_inc(const_ld, 16)
            sp.dma_start(wmod_sb[:], wmod.rearrange("(t p) m -> p t m", p=PART)).then_inc(const_ld, 16)
            sp.dma_start(rw_sb[:], router_w.rearrange("(t p) e -> p t e", p=PART)).then_inc(const_ld, 16)
            sp.dma_start(rb_bc[:], router_b.partition_broadcast(PART)).then_inc(const_ld, 16)
            sp.wait_ge(mod_ok, 14)
            sp.dma_start(mods_dram, mods.rearrange("b m d -> b (m d)")).then_inc(mods_st, 16)
            sp.dma_start(gate_dram, mods[:, 3, :]).then_inc(mods_st, 16)
            sp.wait_ge(mods_st, 32)

            def load_wqk(t, u):
                for a in range(2):
                    sp.dma_start(wqk[u][:, :, a, :],
                                 w_qkv[bass.ds(t, 1), a].rearrange("o (t p) n -> p (o t) n", p=PART)).then_inc(wqk_ld[u], 16)

            sp.sem_inc(st_rows, 32)
            load_wqk(0, 0)
            with sp.Fori(0, B) as b:
                sp.wait_ge(st_rows, b * 32 + 32)
                sp.dma_start(x_sb, x_t[bass.ds(b, 1)].rearrange("o p q d -> p (o q) d")).then_inc(x_ld, 16)
                for t in range(KT):
                    sp.dma_start(wv_sb[:, t], w_qkv[:, 2, t * PART:(t + 1) * PART, :].rearrange("h p n -> p h n")).then_inc(wv_ld, 16)

                def head(t, u, nxt):
                    g = b * H + t
                    sp.wait_ge(proj_mm, g * 2 + 1)
                    load_wqk(nxt, 1 - u)
                    sp.wait_ge(high_ok, g * 4 + 4)
                    sp.dma_start(q_hh[u][N:2 * N, :].bitcast(F32), q_hh[u][0:N, :].bitcast(F32)).then_inc(dup_ok[u], 16)
                    sp.dma_start(k_h1[u][0:N, :].bitcast(F32), k_hl[u][0:N, :].bitcast(F32)).then_inc(dup_ok[u], 16)

                with sp.Fori(0, H // 2 - 1) as hp:
                    head(hp * 2, 0, hp * 2 + 1)
                    head(hp * 2 + 1, 1, hp * 2 + 2)
                head(H - 2, 0, H - 1)
                head(H - 1, 1, 0)
                sp.wait_ge(pv_mm, (b + 1) * (H * 4) + PV_CREDIT)
                sp.dma_start(wo_sb, w_o.rearrange("(t p) d -> p t d", p=PART)).then_inc(wo_ld, 16)
                sp.dma_start(mod_rows.rearrange("p m d -> p (m d)"),
                             mods_dram[bass.ds(b, 1), 0:3 * D].rearrange("o m -> (o m)").partition_broadcast(PART)).then_inc(mods_ld, 16)
                sp.dma_start(x_sb, x_t[bass.ds(b, 1)].rearrange("o p q d -> p (o q) d")).then_inc(x_ld, 16)
                sp.wait_ge(x1_ok, b + 1)
                sp.dma_start(out_t[bass.ds(b, 1)].rearrange("o p q d -> p (o q) d"), x1_sb).then_inc(st_rows, 16)
                sp.wait_ge(h2_ok, b + 1)
                sp.dma_start(rows_t[bass.ds(b, 1), :, :, 0:D].rearrange("o p q d -> p (o q) d"), norm).then_inc(st_rows, 16)
            sp.wait_ge(st_rows, 32 * B + 32)
            sp.wait_ge(wqk_ld[0], 32 * (B * H // 2 + 1))

        @block.gpsimd
        def _(pool):
            nc.gpsimd.memset(ident[:], 0.0).then_inc(ident_z, 1)
            nc.gpsimd.memset(minus_half[:], -0.5).then_inc(ident_z, 1)
            pool.wait_ge(ident_z, 2)
            nc.gpsimd.affine_select(out=ident[:], in_=ident[:], compare_op=ALU.not_equal, fill=1.0, base=0,
                                    pattern=[[-1, PART]], channel_multiplier=1).then_inc(ident_z, 1)
            pool.wait_ge(ident_z, 3)
            nc.gpsimd.tensor_copy(ident_bf[:], ident[:]).then_inc(ident_ok, 1)
            pool.sem_inc(plo_pool, LP)
            pool.sem_inc(v3_ok, V3_CREDIT)
            pool.sem_inc(head_ok, HEAD_CREDIT)

            with pool.Fori(0, B) as b:
                def inv_std(n):
                    pool.wait_ge(ln_pow_in, b * 2 + n + 1)
                    nc.gpsimd.tensor_tensor(rstd[:], var_eps[:], minus_half[:], ALU.pow).then_inc(ln_pow, 1)

                inv_std(0)
                for i in range(NQ * NG):
                    kb, hg = i // NG, i % NG
                    n = b * (NQ * NG) + i
                    rest = v_rest[:, i % 2, :].rearrange("p (h n) -> p h n", n=N)
                    v2 = v_all[:, kb, hg * HG:(hg + 1) * HG, N + 1:2 * N + 1]
                    v3 = v_all[:, kb, hg * HG:(hg + 1) * HG, 2 * N + 2:3 * N + 2]
                    pool.wait_ge(v2_ok, n + 1)
                    nc.gpsimd.tensor_tensor(v3, rest, v2, ALU.subtract).then_inc(v3_ok, 1)

                def low(g, u, j):
                    pool.wait_ge(phi_ok, g * NQ + j + 1)
                    nc.gpsimd.tensor_tensor(p_lo[u][:, j, :], prob[:, j % 4, :], p_hi[u][:, j, :],
                                            ALU.subtract).then_inc(plo_pool, 1)

                def scale_pair(g, t, p):
                    m = g * 4 + p
                    pool.wait_ge(pv_ev, m + 2)
                    nc.gpsimd.tensor_tensor(heads[:, 2 * p:2 * p + 2, bass.ds(t * N, N)], pv_sum[:, p % 2],
                                            pv_inv[:, p % 2, :].unsqueeze(2).to_broadcast([PART, 2, N]),
                                            ALU.mult).then_inc(head_ok, 1)

                def head(t, u, first):
                    g = b * H + t
                    for j in range(NQ):
                        if not first and j % 2 == 1:
                            scale_pair(g - 1, t - 1, j // 2)
                        if j in LOW_ON_POOL:
                            low(g, u, j)

                run_heads(pool, head)
                for p in range(NQ // 2):
                    scale_pair(b * H + H - 1, H - 1, p)

                inv_std(1)
                pool.wait_ge(h2n_ok, b + 1)
                pool.wait_ge(mods_ld, b * 16 + 16)
                nc.gpsimd.tensor_tensor(norm, norm, mod_rows[:, 2].unsqueeze(1).to_broadcast([PART, NQ, D]), ALU.mult).then_inc(h2m_ok, 1)
                pool.wait_ge(h2m_ok, b + 1)
                nc.gpsimd.tensor_tensor(norm, norm, mod_rows[:, 1].unsqueeze(1).to_broadcast([PART, NQ, D]), ALU.add).then_inc(h2_ok, 1)

        @block.scalar
        def _(act):
            act.sem_inc(exp_ok, EXP_CREDIT)
            act.wait_ge(const_ld, 16 * N_CONST)
            nc.scalar.activation(sig_t[:], c_t[:], ACT.Exp, scale=-1.0).then_inc(c_exp, 1)

            with act.Fori(0, B) as b:
                def second_part(i):
                    kb, hg = i // NG, i % NG
                    act.wait_ge(v_sub, b * (NQ * NG) + i + VSUB_CREDIT + 1)
                    nc.scalar.activation(v_all[:, kb, hg * HG:(hg + 1) * HG, N + 1:2 * N + 1],
                                         v_rest[:, i % 2, :].rearrange("p (h n) -> p h n", n=N), ACT.Copy).then_inc(v2_ok, 1)

                for i in range(NQ * NG):
                    kb, hg = i // NG, i % NG
                    n = b * (NQ * NG) + i
                    act.wait_ge(v_mm, n + 1)
                    src = st_ps[(i % 4) // 2][:, half_cols(i % 2)].rearrange("p (h n) -> p h n", n=N)
                    nc.scalar.activation(v_all[:, kb, hg * HG:(hg + 1) * HG, 0:N], src, ACT.Copy).then_inc(v1_ok, 1)
                    if i:
                        second_part(i - 1)
                second_part(NQ * NG - 1)

                def high(g, u, h):
                    act.wait_ge(proj_mm, g * 2 + h + 2)
                    nc.scalar.activation(q_hh[u][0:N, half_cols(h)], ms_ps[0:N, :], ACT.Copy).then_inc(high_ok, 1)
                    nc.scalar.activation(k_hl[u][0:N, half_cols(h)], ms_ps[N:2 * N, :], ACT.Copy).then_inc(high_ok, 1)

                def prob_tile(g, u, j):
                    act.wait_ge(st_mm, g * NQ + j + 1)
                    if j >= 4:
                        if (j - 4) in LOW_ON_DVE:
                            act.wait_ge(plo_dve, g * LD + LD + count_upto(LOW_ON_DVE, j - 4))
                        else:
                            act.wait_ge(plo_pool, g * LP + LP + count_upto(LOW_ON_POOL, j - 4))
                    elif (j + 4) in LOW_ON_DVE:
                        act.wait_ge(plo_dve, g * LD + count_upto(LOW_ON_DVE, j + 4))
                    else:
                        act.wait_ge(plo_pool, g * LP + count_upto(LOW_ON_POOL, j + 4))
                    nc.scalar.activation(prob[:, j % 4, :], st_ps[j % 2][:], ACT.Exp, scale=SCALE).then_inc(exp_ok, 1)
                    if j == 0:
                        act.wait_ge(pv_mm, g * 4 + PV_CREDIT - 4)
                    act.wait_ge(exp_ok, EXP_CREDIT + g * NQ + j + 1)
                    nc.scalar.activation(p_hi[u][:, j, :], prob[:, j % 4, :], ACT.Copy).then_inc(phi_ok, 1)

                def crow(g, u):
                    act.wait_ge(crow_mm, g + 1)
                    nc.scalar.activation(q_lc[u][N:N + 1, :], max_ps[0:1, :], ACT.Copy).then_inc(crow_ok, 1)

                high(b * H, 0, 0)
                high(b * H, 0, 1)
                crow(b * H, 0)

                def head(t, u, first):
                    g = b * H + t
                    last = isinstance(t, int) and t == H - 1
                    for j in range(NQ):
                        if j < 2 and not last:
                            high(g + 1, 1 - u, j)
                        prob_tile(g, u, j)
                    if not last:
                        crow(g + 1, 1 - u)

                run_heads(act, head)

                for q in range(NQ):
                    act.wait_ge(ht_mm, b * NQ + q + 1)
                    if q >= 2:
                        act.wait_ge(o_mm, b * NQ + q - 1)
                    nc.scalar.activation(heads_t[q % 2], st_ps[q % 2][:, 0:HT * PART].rearrange("p (t n) -> p t n", n=PART), ACT.Copy).then_inc(ht_ev, 1)
                for i in range(2 * KT):
                    kt, h = i // 2, i % 2
                    act.wait_ge(tr_mm, b * 4 * KT + 2 * KT + i + 1)
                    nc.scalar.activation(h_t[:, kt, half_cols(h)], st_ps[kt][:, half_cols(h)], ACT.Copy).then_inc(tr_ev, 1)

        @block.vector
        def _(dve):
            dve.sem_inc(plo_dve, LD)
            dve.sem_inc(v_sub, VSUB_CREDIT)
            for s_one in (low_ok, max_red, pv_ev, tr_ev):
                dve.sem_inc(s_one, 1)
            for u in range(2):
                nc.vector.memset(k_h1[u][N:2 * N, :].bitcast(F32), 0.0).then_inc(fill_ok, 1)
                nc.vector.memset(q_lc[u][N:2 * N, :].bitcast(F32), 0.0).then_inc(fill_ok, 1)
            nc.vector.memset(v_all[:, :, :, N:N + 1], 1.0).then_inc(fill_ok, 1)
            nc.vector.memset(v_all[:, :, :, 2 * N + 1:2 * N + 2], 0.0).then_inc(fill_ok, 1)
            dve.wait_ge(fill_ok, 6)
            for u in range(2):
                nc.vector.memset(k_h1[u][N:N + 1, :].bitcast(F32), 1.0).then_inc(fill_ok, 1)
            dve.wait_ge(c_exp, 1)
            nc.vector.tensor_scalar(sig_t[:], sig_t[:], 1.0, None, ALU.add).then_inc(c_silu, 1)
            dve.wait_ge(c_silu, 1)
            nc.vector.reciprocal(sig_t[:], sig_t[:]).then_inc(c_silu, 1)
            dve.wait_ge(c_silu, 2)
            nc.vector.tensor_tensor(silu_t[:], c_t[:], sig_t[:], ALU.mult).then_inc(c_silu, 1)
            dve.wait_ge(mod_mm, 1)
            md = ms_ps[:, 0:2 * KT * B].rearrange("p (m b) -> p m b", b=B)
            nc.vector.tensor_copy(mod_t[:, 0:KT, :], md[:, 0:KT]).then_inc(mod_ok, 1)
            nc.vector.tensor_scalar(mod_t[:, KT:2 * KT, :], md[:, KT:2 * KT], 1.0, None, ALU.add).then_inc(mod_ok, 1)
            raw = st_ps[0][0:B, :].rearrange("b (m d) -> b m d", m=4)
            nc.vector.tensor_copy(mods[:, 1, :], raw[:, 1]).then_inc(mod_ok, 1)
            nc.vector.tensor_scalar(mods[:, 2, :], raw[:, 2], 1.0, None, ALU.add).then_inc(mod_ok, 1)
            for i, m in enumerate((0, 3)):
                nc.vector.tensor_scalar(mods_s[:, 2 * i], raw[:, m], 0.0, None, ALU.is_ge).then_inc(mod_ok, 1)
                nc.vector.tensor_scalar(mods_s[:, 2 * i + 1], raw[:, m], 0.0, None, ALU.is_lt).then_inc(mod_ok, 1)
            dve.wait_ge(mod_ok, 8)
            for i, m in enumerate((0, 3)):
                nc.vector.scalar_tensor_tensor(out=mods_s[:, 2 * i], in0=raw[:, m], scalar=GATE_FLOOR, in1=mods_s[:, 2 * i],
                                               op0=ALU.max, op1=ALU.mult).then_inc(mod_ok, 1)
                nc.vector.scalar_tensor_tensor(out=mods_s[:, 2 * i + 1], in0=raw[:, m], scalar=-GATE_FLOOR,
                                               in1=mods_s[:, 2 * i + 1], op0=ALU.min, op1=ALU.mult).then_inc(mod_ok, 1)
            dve.wait_ge(mod_ok, 12)
            for i, m in enumerate((0, 3)):
                nc.vector.tensor_tensor(mods[:, m, :], mods_s[:, 2 * i], mods_s[:, 2 * i + 1], ALU.add).then_inc(mod_ok, 1)

            with dve.Fori(0, B) as b:
                ln_n = [0]

                def step(ins, wait=True):
                    ins.then_inc(ln, 1)
                    ln_n[0] += 1
                    if wait:
                        dve.wait_ge(ln, b * LN_STEPS + ln_n[0])

                def normalise(src, n):
                    for q in range(NQ):
                        if n == 0:
                            step(nc.vector.bn_stats(stats[:, q, :], src[:, q, :]), q == NQ - 1)
                    mean_e, mean_o, m2_e, m2_o = stats[:, :, 1], stats[:, :, 4], stats[:, :, 2], stats[:, :, 5]
                    step(nc.vector.tensor_tensor(mean[:], mean_e, mean_o, ALU.add), False)
                    step(nc.vector.tensor_tensor(mean_d[:], mean_e, mean_o, ALU.subtract), False)
                    step(nc.vector.tensor_tensor(var_eps[:], m2_e, m2_o, ALU.add))
                    step(nc.vector.tensor_scalar(mean[:], mean[:], 0.5, None, ALU.mult), False)
                    step(nc.vector.scalar_tensor_tensor(out=mean_d[:], in0=mean_d[:], scalar=0.25, in1=mean_d[:],
                                                        op0=ALU.mult, op1=ALU.mult), False)
                    step(nc.vector.tensor_scalar(var_eps[:], var_eps[:], 1.0 / D, LN_EPS, ALU.mult, ALU.add))
                    nc.vector.tensor_tensor(var_eps[:], var_eps[:], mean_d[:], ALU.add).then_inc(ln_pow_in, 1)
                    dve.wait_ge(ln_pow, b * 2 + n + 1)
                    for q in range(NQ):
                        ins = nc.vector.tensor_scalar(norm[:, q, :], src[:, q, :], mean[:, q:q + 1], rstd[:, q:q + 1],
                                                      ALU.subtract, ALU.mult)
                        if q < NQ - 1:
                            step(ins, False)
                        else:
                            ins.then_inc(ln_ok if n == 0 else h2n_ok, 1)

                step(nc.vector.tensor_copy(mod_b[:], mod_t[:, :, bass.ds(b, 1)].rearrange("p m o -> p (m o)")), False)
                dve.wait_ge(x_ld, b * 32 + 16)
                normalise(x_sb, 0)
                for i in range(2 * KT):
                    kt, h = i // 2, i % 2
                    dve.wait_ge(tr_mm, b * 4 * KT + i + 1)
                    nc.vector.tensor_scalar(h_t[:, kt, half_cols(h)], st_ps[kt][:, half_cols(h)], mod_b[:, KT + kt:KT + kt + 1],
                                            mod_b[:, kt:kt + 1], ALU.mult, ALU.add).then_inc(tr_ev, 1)
                for i in range(NQ * NG):
                    kb, hg = i // NG, i % NG
                    n = b * (NQ * NG) + i
                    dve.wait_ge(v1_ok, n + 1)
                    dve.wait_ge(v3_ok, n + 1)
                    src = st_ps[(i % 4) // 2][:, half_cols(i % 2)].rearrange("p (h n) -> p h n", n=N)
                    nc.vector.tensor_tensor(v_rest[:, i % 2, :].rearrange("p (h n) -> p h n", n=N), src,
                                            v_all[:, kb, hg * HG:(hg + 1) * HG, 0:N], ALU.subtract).then_inc(v_sub, 1)

                def lows(g, u, h):
                    dve.wait_ge(high_ok, g * 4 + 2 * h + 2)
                    nc.vector.tensor_tensor(q_lc[u][0:N, half_cols(h)], ms_ps[0:N, :],
                                            q_hh[u][0:N, half_cols(h)].bitcast(F32), ALU.subtract).then_inc(low_ok, 1)
                    nc.vector.tensor_tensor(k_hl[u][N:2 * N, half_cols(h)], ms_ps[N:2 * N, :],
                                            k_hl[u][0:N, half_cols(h)].bitcast(F32), ALU.subtract).then_inc(low_ok, 1)

                def reduce_max(g, i):
                    dve.wait_ge(max_mm, g * NQ + i + 1)
                    nc.vector.tensor_reduce(row_max[:, i:i + 1], max_ps[:], AX.X, ALU.max).then_inc(max_red, 1)

                def negate(g):
                    dve.wait_ge(max_red, g * NQ + NQ + 1)
                    nc.vector.tensor_scalar(neg_max[:], row_max[:], -1.0, None, ALU.mult).then_inc(neg_ok, 1)

                def low(g, u, j):
                    dve.wait_ge(phi_ok, g * NQ + j + 1)
                    nc.vector.tensor_tensor(p_lo[u][:, j, :], prob[:, j % 4, :], p_hi[u][:, j, :],
                                            ALU.subtract).then_inc(plo_dve, 1)

                def collect(g, p):
                    m = g * 4 + p
                    dve.wait_ge(pv_mm, PV_CREDIT + m + 1)
                    dve.wait_ge(head_ok, m + 1)
                    src = pv_ps[:, 0:2 * VW].rearrange("p (q w) -> p q w", q=2)
                    nc.vector.tensor_reduce(pv_sum[:, p % 2], src.rearrange("p q (v n) -> p q n v", v=3)[:, :, 0:N, :],
                                            AX.X, ALU.add).then_inc(pv_red, 1)
                    dve.wait_ge(pv_red, m + 1)
                    nc.vector.reciprocal(pv_inv[:, p % 2, :], src[:, :, N]).then_inc(pv_ev, 1)

                lows(b * H, 0, 0)
                lows(b * H, 0, 1)
                for i in range(NQ):
                    reduce_max(b * H, i)
                negate(b * H)

                def head(t, u, first):
                    g = b * H + t
                    last = isinstance(t, int) and t == H - 1
                    for j in range(NQ):
                        if j < 2 and not last:
                            lows(g + 1, 1 - u, j)
                        if j in MAX_BEFORE and not last:
                            reduce_max(g + 1, MAX_BEFORE[j])
                        if j % 2 == 1 and not first:
                            collect(g - 1, j // 2)
                        if j in MAX_AFTER and not last:
                            reduce_max(g + 1, MAX_AFTER[j])
                        if j in LOW_ON_DVE:
                            low(g, u, j)
                    if not last:
                        negate(g + 1)

                run_heads(dve, head)
                for p in range(NQ // 2):
                    collect(b * H + H - 1, p)

                dve.wait_ge(mods_ld, b * 16 + 16)
                dve.wait_ge(x_ld, b * 32 + 32)
                for q in range(NQ):
                    dve.wait_ge(o_mm, b * NQ + q + 1)
                    o_ps = (pv_ps if q % 2 == 0 else ms_ps)[:, 0:D]
                    nc.vector.tensor_tensor(x1_sb[:, q, :], o_ps, mod_rows[:, 0], ALU.mult).then_inc(gated, 1)
                    dve.wait_ge(gated, b * NQ + q + 1)
                    nc.vector.tensor_tensor(x1_sb[:, q, :], x1_sb[:, q, :], x_sb[:, q, :], ALU.add).then_inc(x1_row, 1)
                    dve.wait_ge(x1_row, b * NQ + q + 1)
                    ins = nc.vector.bn_stats(stats[:, q, :], x1_sb[:, q, :])
                    if q < NQ - 1:
                        step(ins, False)
                    else:
                        ins.then_inc(x1_ok, 1)
                        dve.wait_ge(x1_ok, b + 1)
                normalise(x1_sb, 1)
                dve.wait_ge(lg_mm, b + 1)
                nc.vector.tensor_tensor(logits[:, bass.ds(b * NQ, NQ), :], max_ps[:, 0:NQ * E].rearrange("p (q e) -> p q e", e=E),
                                        rb_bc[:].unsqueeze(1).to_broadcast([PART, NQ, E]), ALU.add).then_inc(lg_ok, 1)
                assert ln_n[0] == LN_STEPS, (ln_n[0], LN_STEPS)

        @block.tensor
        def _(pe):
            pe.sem_inc(pv_mm, PV_CREDIT)
            pe.sem_inc(proj_mm, 1)
            pe.wait_ge(const_ld, 16 * N_CONST)
            pe.wait_ge(c_silu, 3)
            for m in range(2 * KT):
                for kt in range(KT):
                    nc.tensor.matmul(ms_ps[:, m * B:(m + 1) * B], wmod_sb[:, kt, tile_cols(m)], silu_t[:, kt, :],
                                     start=(kt == 0), stop=(kt == KT - 1))
            for h in range(2):
                for kt in range(KT):
                    mm = nc.tensor.matmul(st_ps[0][0:B, half_cols(h)], silu_t[:, kt, :], wmod_sb[:, kt, 2 * D + h * HALF:2 * D + (h + 1) * HALF],
                                          start=(kt == 0), stop=(kt == KT - 1))
            mm.then_inc(mod_mm, 1)
            pe.wait_ge(ident_ok, 1)
            pe.wait_ge(fill_ok, 8)
            pe.wait_ge(mod_ok, 14)

            with pe.Fori(0, B) as b:
                def transpose_rows(n):
                    for i in range(2 * KT):
                        kt, h = i // 2, i % 2
                        for q in range(4):
                            mm = nc.tensor.transpose(st_ps[kt][:, h * HALF + q * PART:h * HALF + (q + 1) * PART],
                                                     norm[:, h * 4 + q, tile_cols(kt)], ident[:])
                        mm.then_inc(tr_mm, 1)

                pe.wait_ge(ln_ok, b + 1)
                pe.wait_ge(tr_ev, b * 4 * KT + 1)
                transpose_rows(0)
                pe.wait_ge(tr_ev, b * 4 * KT + 2 * KT + 1)
                pe.wait_ge(wv_ld, b * (16 * KT) + 16 * KT)
                for i in range(NQ * NG):
                    kb, hg = i // NG, i % NG
                    pe.wait_ge(v_sub, b * (NQ * NG) + i + 1)
                    for kt in range(KT):
                        mm = nc.tensor.matmul(st_ps[(i % 4) // 2][:, half_cols(i % 2)], h_t[:, kt, tile_cols(kb)],
                                              wv_sb[:, kt, hg * HG:(hg + 1) * HG, :].rearrange("p h n -> p (h n)"),
                                              start=(kt == 0), stop=(kt == KT - 1))
                    mm.then_inc(v_mm, 1)

                def project(g, t, u, h):
                    pe.wait_ge(low_ok, g * 4 + 2 * h + 1)
                    if h == 0:
                        pe.wait_ge(wqk_ld[u], pair_dmas(b, t, u))
                    for kt in range(KT):
                        mm = nc.tensor.matmul(ms_ps[:], wqk[u][:, kt].rearrange("p a n -> p (a n)"), h_t[:, kt, half_cols(h)],
                                              start=(kt == 0), stop=(kt == KT - 1))
                    mm.then_inc(proj_mm, 1)

                def max_tile(g, t, u, i):
                    if i == 0:
                        pe.wait_ge(low_ok, g * 4 + 4 + 1)
                        pe.wait_ge(dup_ok[u], pair_dmas(b, t, u))
                    pe.wait_ge(max_red, g * NQ + i + 1)
                    for h in range(2):
                        mm = nc.tensor.matmul(max_ps[:, half_cols(h)], q_hh[u][:, tile_cols(i)], k_hl[u][:, half_cols(h)],
                                              start=True, stop=True)
                    mm.then_inc(max_mm, 1)

                def max_row(g):
                    pe.wait_ge(neg_ok, g + 1)
                    for q in range(NQ):
                        mm = nc.tensor.matmul(max_ps[0:1, tile_cols(q)], neg_max[:, q:q + 1], ident_bf[:], start=True, stop=True)
                    mm.then_inc(crow_mm, 1)

                def scores(g, u, j):
                    if j == 0:
                        pe.wait_ge(crow_ok, g + 1)
                    pe.wait_ge(exp_ok, g * NQ + j - 1 + EXP_CREDIT)
                    for h in range(2):
                        nc.tensor.matmul(st_ps[j % 2][:, half_cols(h)], k_hl[u][:, tile_cols(j)], q_hh[u][:, half_cols(h)],
                                         start=True, stop=False)
                    for h in range(2):
                        mm = nc.tensor.matmul(st_ps[j % 2][:, half_cols(h)], k_h1[u][:, tile_cols(j)], q_lc[u][:, half_cols(h)],
                                              start=False, stop=True)
                    mm.then_inc(st_mm, 1)

                def weighted(g, t, u, q):
                    if q == 0:
                        pe.wait_ge(plo_dve, g * LD + 2 * LD)
                        pe.wait_ge(plo_pool, g * LP + 2 * LP)
                        pe.wait_ge(v3_ok, b * (NQ * NG) + NQ * NG + V3_CREDIT)
                    if q % 2 == 0:
                        pe.wait_ge(pv_ev, g * 4 + q // 2 + 1)
                    o = pv_ps[:, (q % 2) * VW:(q % 2) * VW + VHI]
                    for kb in range(NQ):
                        v = v_all[:, kb, bass.ds(t, 1), :].rearrange("p o w -> p (o w)")
                        nc.tensor.matmul(o, p_hi[u][:, kb, tile_cols(q)], v[:, 0:VHI], start=(kb == 0), stop=False)
                        mm = nc.tensor.matmul(o[:, 0:VLO], p_lo[u][:, kb, tile_cols(q)], v[:, 0:VLO],
                                              start=False, stop=(kb == NQ - 1))
                    if q % 2 == 1:
                        mm.then_inc(pv_mm, 1)

                project(b * H, 0, 0, 0)
                project(b * H, 0, 0, 1)
                for i in range(NQ):
                    max_tile(b * H, 0, 0, i)
                max_row(b * H)

                def head(t, u, first):
                    g = b * H + t
                    last = isinstance(t, int) and t == H - 1
                    for j in range(NQ):
                        if j < 2 and not last:
                            project(g + 1, t + 1, 1 - u, j)
                        scores(g, u, j)
                        if j in MAX_BEFORE and not last:
                            max_tile(g + 1, t + 1, 1 - u, MAX_BEFORE[j])
                        if not first:
                            weighted(g - 1, t - 1, 1 - u, j)
                        if j in MAX_AFTER and not last:
                            max_tile(g + 1, t + 1, 1 - u, MAX_AFTER[j])
                    if not last:
                        max_row(g + 1)

                run_heads(pe, head)
                for q in range(NQ):
                    weighted(b * H + H - 1, H - 1, 1, q)

                def turn(q):
                    if q >= 2:
                        pe.wait_ge(ht_ev, b * NQ + q - 1)
                    if q == 0:
                        pe.wait_ge(exp_ok, (b + 1) * (H * NQ) + EXP_CREDIT)
                        pe.wait_ge(head_ok, (b + 1) * (H * 4) + HEAD_CREDIT)
                    for t in range(HT):
                        mm = nc.tensor.transpose(st_ps[q % 2][:, tile_cols(t)], heads[:, q, tile_cols(t)], ident[:])
                    mm.then_inc(ht_mm, 1)

                pe.wait_ge(wo_ld, b * 16 + 16)
                turn(0)
                for q in range(NQ):
                    if q < NQ - 1:
                        turn(q + 1)
                    pe.wait_ge(ht_ev, b * NQ + q + 1)
                    if q >= 2:
                        pe.wait_ge(gated, b * NQ + q - 1)
                    else:
                        pe.wait_ge(pv_ev, (b + 1) * (H * 4) + 1)
                        pe.wait_ge(low_ok, (b + 1) * (H * 4) + 1)
                    o_ps = (pv_ps if q % 2 == 0 else ms_ps)[:, 0:D]
                    for t in range(HT):
                        mm = nc.tensor.matmul(o_ps, heads_t[q % 2][:, t, :], wo_sb[:, t, :], start=(t == 0), stop=(t == HT - 1))
                    mm.then_inc(o_mm, 1)

                pe.wait_ge(h2_ok, b + 1)
                pe.wait_ge(ht_ev, b * NQ + NQ)
                transpose_rows(1)
                pe.wait_ge(tr_ev, b * 4 * KT + 4 * KT + 1)
                pe.wait_ge(crow_ok, (b + 1) * H)
                for q in range(NQ):
                    for kt in range(KT):
                        mm = nc.tensor.matmul(max_ps[:, q * E:(q + 1) * E], h_t[:, kt, tile_cols(q)], rw_sb[:, kt, :],
                                              start=(kt == 0), stop=(kt == KT - 1))
                mm.then_inc(lg_mm, 1)
                pe.wait_ge(gated, (b + 1) * NQ)


def ffn_phase(nc, k):
    B, P, D, E, F, NB = k["B"], k["P"], k["D"], k["E"], k["F"], k["NB"]
    KT, ST, FT, ROW, TK = k["KT"], k["ST"], k["FT"], k["ROW"], k["topk"]
    SLOT_LO, SLOT_HI = k["SLOT_LO"], k["SLOT_HI"]
    ident, logits = k["ident"], k["logits"]
    rows_dram, rows_blk, gate_dram, slots_dram, out_rows = k["rows_dram"], k["rows_blk"], k["gate_dram"], k["slots_dram"], k["out_rows"]
    w1, b1, w2, b2 = k["w1"], k["b1"], k["w2"], k["b2"]
    EB = E * NB
    TOP_BIT = 29
    NOWHERE = 4096.0
    LO_BITS = SLOT_LO.bit_length() - 1
    assert TK % PART == 0 and SLOT_HI * SLOT_LO == TK and SLOT_HI <= PART and 2 * TK < NOWHERE

    with ExitStack() as ctx:
        def sb(name, shape, dt):
            return ctx.enter_context(nc.sbuf_tensor(name, shape, dt))

        def ps(name, shape):
            return ctx.enter_context(nc.psum_tensor(name, shape, F32))

        def sem(name):
            return ctx.enter_context(nc.semaphore(name))

        token_max = sb("token_max", [PART, NB], F32)
        token_sum = sb("token_sum", [PART, NB], F32)
        scores = sb("scores", [PART, E, NB], F32)
        ones_bf = sb("ones_bf", [PART, PART], BF16)
        before_bf = sb("before_bf", [PART, PART], BF16)
        thr = sb("thr", [PART, E], I32)
        cand = sb("cand", [PART, E], I32)
        bit = sb("bit", [PART, E], I32)
        flag = sb("flag", [PART, E], I32)
        cnt = sb("cnt", [PART, E], F32)
        mask = sb("mask", [PART, 2, E, NB], BF16)
        tot = sb("tot", [PART, 2, EB], F32)
        incl = sb("incl", [PART, 2, EB], F32)
        carry = sb("carry", [PART, E, NB], F32)
        need = sb("need", [PART, E], F32)
        place = sb("place", [PART, EB], F32)
        take = sb("take", [PART, EB], F32)
        place_i = sb("place_i", [PART, EB], I32)
        part_i = sb("part_i", [PART, EB], I32)
        place_hi = sb("place_hi", [PART, EB], BF16)
        place_lo = sb("place_lo", [PART, EB], BF16)
        iota_i = sb("iota_i", [PART, NB + SLOT_LO], I32)
        iota_bf = sb("iota_bf", [PART, NB + SLOT_LO], BF16)
        row_i = sb("row_i", [PART, 1], I32)
        row_f = sb("row_f", [PART, 1], F32)
        hot_hi = sb("hot_hi", [PART, NB, SLOT_HI], BF16)
        hot_lo = sb("hot_lo", [PART, NB, SLOT_LO], BF16)
        hot_id = sb("hot_id", [PART, NB, 2, SLOT_LO], BF16)
        id_f = sb("id_f", [SLOT_HI, 2, SLOT_LO], F32)
        id_i = sb("id_i", [SLOT_HI, SLOT_LO], U32)
        slots = [sb(f"slots{u}", [PART, ST], U32) for u in range(2)]
        slot_batch = [sb(f"slot_batch{u}", [PART, ST], U32) for u in range(2)]
        w1_sb = [sb(f"w1_sb{u}", [PART, KT, F], F32) for u in range(2)]
        w2_sb = [sb(f"w2_sb{u}", [PART, FT, D], F32) for u in range(2)]
        b1_sb = [sb(f"b1_sb{u}", [PART, FT], F32) for u in range(2)]
        b2_sb = [sb(f"b2_sb{u}", [PART, D], F32) for u in range(2)]
        rows = [sb(f"rows{u}", [PART, ST, ROW], F32) for u in range(2)]
        gates = [sb(f"gates{u}", [PART, ST, D], F32) for u in range(2)]
        weight = [sb(f"weight{u}", [PART, ST], F32) for u in range(2)]
        rows_tr = sb("rows_tr", [PART, KT, TK], F32)
        hid = sb("hid", [PART, FT, TK], F32)
        contrib = [sb(f"contrib{u}", [PART, ST, D], F32) for u in range(2)]

        a_ps = [ps(f"a_ps{i}", [PART, HALF]) for i in range(4)]
        y_ps = [ps(f"y_ps{i}", [PART, HALF]) for i in range(2)]
        c_ps = ps("c_ps", [PART, HALF])

        rt = sem("rt")
        sm_exp = sem("sm_exp")
        sc_ok = sem("sc_ok")
        sc_st = sem("sc_st")
        cst = sem("cst")
        bs = sem("bs")
        cnt_in = sem("cnt_in")
        cnt_mm = sem("cnt_mm")
        mask_ok = sem("mask_ok")
        rank_mm = sem("rank_mm")
        hot = sem("hot")
        hot_ok = sem("hot_ok")
        id_mm = sem("id_mm")
        id_cp = sem("id_cp")
        id_ok = sem("id_ok")
        id_st = sem("id_st")
        id_ld = [sem(f"id_ld{u}") for u in range(2)]
        sb_ok = sem("sb_ok")
        w_ld = [sem(f"w_ld{u}") for u in range(2)]
        got = [sem(f"got{u}") for u in range(2)]
        g_cp = sem("g_cp")
        rt_mm = sem("rt_mm")
        rt_ev = sem("rt_ev")
        hid_mm = sem("hid_mm")
        hid_ok = sem("hid_ok")
        y_mm = sem("y_mm")
        y_b = sem("y_b")
        y_ok = sem("y_ok")
        added = sem("added")

        STEP_BS, STEP_HOT, W_DMAS = 5, 3, 4
        block = ctx.enter_context(nc.Block())

        @block.sync
        def _(sp):
            def load_weights(e, u):
                sp.dma_start(w1_sb[u][:], w1[bass.ds(e, 1)].rearrange("o (t p) f -> p (o t) f", p=PART)).then_inc(w_ld[u], 16)
                sp.dma_start(w2_sb[u][:], w2[bass.ds(e, 1)].rearrange("o (t p) d -> p (o t) d", p=PART)).then_inc(w_ld[u], 16)
                sp.dma_start(b1_sb[u][:], b1[bass.ds(e, 1)].rearrange("o (t p) -> p (o t)", p=PART),
                             allow_slow_non_contiguous=True).then_inc(w_ld[u], 16)
                sp.dma_start(b2_sb[u][:], b2[bass.ds(e, 1)].rearrange("o d -> (o d)").partition_broadcast(PART)).then_inc(w_ld[u], 16)

            load_weights(0, 0)
            load_weights(1, 1)
            sp.wait_ge(sc_ok, 1)
            sp.dma_start(rows_blk[:, :, D:D + E], logits[:]).then_inc(sc_st, 16)
            with sp.Fori(0, E) as e:
                sp.wait_ge(id_ok, e + 1)
                sp.dma_start(slots_dram[bass.ds(e, 1)].rearrange("o (h l) -> (o h) l", l=SLOT_LO), id_i[:]).then_inc(id_st, 16)

            def load_slots(e, u):
                sp.dma_start(slots[u][:], slots_dram[bass.ds(e, 1)].rearrange("o (s p) -> p (o s)", p=PART),
                             allow_slow_non_contiguous=True).then_inc(id_ld[u], 16)

            sp.wait_ge(id_st, 16 * E + 1)
            load_slots(0, 0)
            load_slots(1, 1)
            with sp.Fori(0, E // 2 - 1) as ep:
                for u in range(2):
                    sp.wait_ge(y_ok, (ep * 2 + u + 1) * ST)
                    load_weights(ep * 2 + u + 2, u)
                    sp.wait_ge(added, (ep * 2 + u + 1) * (16 * ST))
                    load_slots(ep * 2 + u + 2, u)
            sp.wait_ge(sc_st, 16)

        @block.gpsimd
        def _(pool):
            nc.gpsimd.iota(iota_i[:, 0:NB], [[1, NB]], base=0, channel_multiplier=0).then_inc(cst, 1)
            nc.gpsimd.iota(iota_i[:, NB:], [[1, SLOT_LO]], base=0, channel_multiplier=0).then_inc(cst, 1)
            nc.gpsimd.iota(row_i[:], [[0, 1]], base=0, channel_multiplier=1).then_inc(cst, 1)
            nc.gpsimd.memset(ones_bf[:], 1.0).then_inc(cst, 1)
            pool.wait_ge(cst, 4)
            nc.gpsimd.affine_select(out=before_bf[:], in_=ones_bf[:], compare_op=ALU.is_gt, fill=0.0, base=0,
                                    pattern=[[1, PART]], channel_multiplier=-1).then_inc(cst, 1)

            def gather(e, u):
                for s in range(ST):
                    nc.gpsimd.indirect_dma_start(
                        out=rows[u][:, s, :], out_offset=None, in_=rows_dram,
                        in_offset=bass.IndirectOffsetOnAxis(ap=slots[u][:, s:s + 1], axis=0)).then_inc(got[u], 16)
                    nc.gpsimd.indirect_dma_start(
                        out=gates[u][:, s, :], out_offset=None, in_=gate_dram,
                        in_offset=bass.IndirectOffsetOnAxis(ap=slot_batch[u][:, s:s + 1], axis=0)).then_inc(got[u], 16)

            def scatter(e, u):
                for s in range(ST):
                    pool.wait_ge(y_ok, e * ST + s + 1)
                    nc.gpsimd.indirect_dma_start(
                        out=out_rows, out_offset=bass.IndirectOffsetOnAxis(ap=slots[u][:, s:s + 1], axis=0),
                        in_=contrib[u][:, s, :], in_offset=None, compute_op=ALU.add).then_inc(added, 16)
                pool.wait_ge(added, (e + 1) * (16 * ST))

            pool.wait_ge(sc_st, 16)
            pool.wait_ge(sb_ok, 2)
            gather(0, 0)
            gather(1, 1)
            for e in range(E):
                scatter(e, e % 2)
                if e + 2 < E:
                    pool.wait_ge(sb_ok, e + 3)
                    gather(e + 2, e % 2)

        @block.scalar
        def _(act):
            act.wait_ge(rt, 2)
            nc.scalar.activation(logits[:], logits[:], ACT.Exp).then_inc(sm_exp, 1)
            with act.Fori(0, E // 2) as ep:
                for u in range(2):
                    e = ep * 2 + u
                    for t in range(KT):
                        act.wait_ge(rt_mm, e * KT + t + 1)
                        nc.scalar.activation(rows_tr[:, t, :], a_ps[t][:, 0:TK], ACT.Copy).then_inc(rt_ev, 1)
                    for f in range(FT):
                        act.wait_ge(hid_mm, e * FT + f + 1)
                        nc.scalar.activation(hid[:, f, :], a_ps[f % 4][:, 0:TK], ACT.Relu, bias=b1_sb[u][:, f:f + 1]).then_inc(hid_ok, 1)

        @block.vector
        def _(dve):
            n_rt = [0]

            def step(ins, wait=True):
                ins.then_inc(rt, 1)
                n_rt[0] += 1
                if wait:
                    dve.wait_ge(rt, n_rt[0])

            dve.sem_inc(rt_ev, 1)
            dve.sem_inc(hid_ok, 1)
            dve.sem_inc(y_b, 2)
            dve.sem_inc(id_st, 1)
            step(nc.vector.tensor_reduce(token_max[:], logits[:], AX.X, ALU.max))
            step(nc.vector.tensor_tensor(logits[:], logits[:], token_max[:].unsqueeze(2).to_broadcast([PART, NB, E]), ALU.subtract), False)
            dve.wait_ge(sm_exp, 1)
            step(nc.vector.tensor_reduce(token_sum[:], logits[:], AX.X, ALU.add))
            step(nc.vector.reciprocal(token_sum[:], token_sum[:]))
            nc.vector.tensor_tensor(logits[:], logits[:], token_sum[:].unsqueeze(2).to_broadcast([PART, NB, E]), ALU.mult).then_inc(sc_ok, 1)
            dve.wait_ge(sc_ok, 1)
            step(nc.vector.tensor_copy(scores[:], logits[:].rearrange("p n e -> p e n")), False)
            dve.wait_ge(cst, 5)
            step(nc.vector.tensor_copy(iota_bf[:], iota_i[:]), False)
            step(nc.vector.tensor_copy(row_f[:], row_i[:]), False)
            step(nc.vector.memset(carry[:], 1.0))
            step(nc.vector.memset(carry[:, :, 0:1], 0.0), False)
            step(nc.vector.memset(thr[:], 0), False)
            step(nc.vector.memset(bit[:], 1 << TOP_BIT), False)
            step(nc.vector.memset(cand[:], 1 << TOP_BIT))

            with dve.Fori(0, TOP_BIT + 1) as i:
                nc.vector.tensor_tensor(mask[:, 0], scores[:], cand[:].bitcast(F32).unsqueeze(2).to_broadcast([PART, E, NB]),
                                        ALU.is_ge).then_inc(cnt_in, 1)
                dve.wait_ge(cnt_mm, i + 1)
                nc.vector.tensor_reduce(cnt[:], c_ps[:, 0:EB].rearrange("p (e n) -> p e n", n=NB), AX.X, ALU.add).then_inc(bs, 1)
                dve.wait_ge(bs, i * STEP_BS + 1)
                nc.vector.tensor_scalar(flag[:], cnt[:], float(TK), None, ALU.is_ge).then_inc(bs, 1)
                dve.wait_ge(bs, i * STEP_BS + 2)
                nc.vector.tensor_scalar(bit[:], bit[:], 1, None, ALU.logical_shift_right).then_inc(bs, 1)
                nc.vector.copy_predicated(thr[:], flag[:], cand[:]).then_inc(bs, 1)
                dve.wait_ge(bs, i * STEP_BS + 4)
                nc.vector.tensor_tensor(cand[:], thr[:], bit[:], ALU.bitwise_or).then_inc(bs, 1)
                dve.wait_ge(bs, i * STEP_BS + 5)

            thr_bc = thr[:].bitcast(F32).unsqueeze(2).to_broadcast([PART, E, NB])
            nc.vector.tensor_tensor(mask[:, 0], scores[:], thr_bc, ALU.is_gt).then_inc(mask_ok, 1)
            nc.vector.tensor_tensor(mask[:, 1], scores[:], thr_bc, ALU.is_equal).then_inc(mask_ok, 1)
            dve.wait_ge(rank_mm, 1)
            carry_f = carry[:].rearrange("p e n -> p (e n)")
            for m in range(2):
                step(nc.vector.tensor_copy(tot[:, m], a_ps[2 + m][:, 0:EB]), m == 1)
            for m in range(2):
                step(nc.vector.tensor_tensor_scan(incl[:, m], carry_f, tot[:, m], 0.0, ALU.mult, ALU.add), m == 1)
            step(nc.vector.tensor_scalar(need[:], incl[:, 0].rearrange("p (e n) -> p e n", n=NB)[:, :, NB - 1], -1.0, float(TK), ALU.mult, ALU.add), False)
            step(nc.vector.tensor_tensor(tot[:], incl[:], tot[:], ALU.subtract))
            for m in range(2):
                step(nc.vector.tensor_tensor(tot[:, m], tot[:, m], a_ps[m][:, 0:EB], ALU.add), m == 1)
            need_bc = need[:].unsqueeze(2).to_broadcast([PART, E, NB])

            def by_expert(ap):
                return ap.rearrange("p (e n) -> p e n", n=NB)

            step(nc.vector.tensor_tensor(by_expert(place[:]), by_expert(tot[:, 1]), need_bc, ALU.min), False)
            step(nc.vector.tensor_tensor(by_expert(take[:]), by_expert(tot[:, 1]), need_bc, ALU.is_lt))
            step(nc.vector.tensor_tensor(place[:], place[:], tot[:, 0], ALU.add), False)
            step(nc.vector.tensor_tensor(take[:], take[:], mask[:, 1].rearrange("p e n -> p (e n)"), ALU.mult))
            step(nc.vector.tensor_tensor(take[:], take[:], mask[:, 0].rearrange("p e n -> p (e n)"), ALU.add))
            step(nc.vector.scalar_tensor_tensor(out=place[:], in0=take[:], scalar=-NOWHERE, in1=place[:], op0=ALU.mult, op1=ALU.add))
            step(nc.vector.tensor_scalar(place_i[:], place[:], NOWHERE, None, ALU.add))
            step(nc.vector.tensor_scalar(part_i[:], place_i[:], LO_BITS, None, ALU.logical_shift_right))
            step(nc.vector.tensor_copy(place_hi[:], part_i[:]))
            step(nc.vector.tensor_scalar(part_i[:], place_i[:], SLOT_LO - 1, None, ALU.bitwise_and))
            step(nc.vector.tensor_copy(place_lo[:], part_i[:]))

            with dve.Fori(0, E) as e:
                hi_e = place_hi[:, bass.ds(e * NB, NB)].unsqueeze(2).to_broadcast([PART, NB, SLOT_HI])
                lo_e = place_lo[:, bass.ds(e * NB, NB)].unsqueeze(2).to_broadcast([PART, NB, SLOT_LO])
                nc.vector.tensor_tensor(hot_hi[:], hi_e, iota_bf[:, NB:NB + SLOT_HI].unsqueeze(1).to_broadcast([PART, NB, SLOT_HI]),
                                        ALU.is_equal).then_inc(hot, 1)
                nc.vector.tensor_tensor(hot_lo[:], lo_e, iota_bf[:, NB:NB + SLOT_LO].unsqueeze(1).to_broadcast([PART, NB, SLOT_LO]),
                                        ALU.is_equal).then_inc(hot, 1)
                dve.wait_ge(hot, e * STEP_HOT + 2)
                nc.vector.tensor_tensor(hot_id[:, :, 0, :], hot_lo[:], iota_bf[:, 0:NB].unsqueeze(2).to_broadcast([PART, NB, SLOT_LO]),
                                        ALU.mult).then_inc(hot, 1)
                nc.vector.tensor_scalar(hot_id[:, :, 1, :], hot_lo[:], row_f[:, 0:1], None, ALU.mult).then_inc(hot_ok, 1)
                dve.wait_ge(id_mm, e + 1)
                nc.vector.tensor_copy(id_f[:], c_ps[0:SLOT_HI, 0:2 * SLOT_LO].rearrange("p (m l) -> p m l", m=2)).then_inc(id_cp, 1)
                dve.wait_ge(id_cp, e + 1)
                dve.wait_ge(id_st, e * 16 + 1)
                nc.vector.scalar_tensor_tensor(out=id_i[:], in0=id_f[:, 0], scalar=float(PART), in1=id_f[:, 1],
                                               op0=ALU.mult, op1=ALU.add).then_inc(id_ok, 1)

            def batch_of_slots(n, u):
                dve.wait_ge(id_ld[u], n * 16 + 16)
                nc.vector.tensor_scalar(slot_batch[u][:], slots[u][:], P.bit_length() - 1, None, ALU.logical_shift_right).then_inc(sb_ok, 1)

            batch_of_slots(0, 0)
            batch_of_slots(0, 1)

            def experts(ep, more):
                for u in range(2):
                    e = ep * 2 + u
                    dve.wait_ge(got[u], (ep + 1) * (32 * ST))
                    nc.vector.tensor_copy(weight[u][:], rows[u][:, :, bass.ds(e + D, 1)].rearrange("p s o -> p (s o)")).then_inc(g_cp, 1)
                    dve.wait_ge(g_cp, e + 1)
                    for s in range(ST):
                        n = e * ST + s
                        dve.wait_ge(y_mm, n + 1)
                        nc.vector.tensor_tensor(contrib[u][:, s, :], y_ps[s % 2][:, 0:D], b2_sb[u][:], ALU.add).then_inc(y_b, 1)
                        dve.wait_ge(y_b, n + 3)
                        nc.vector.scalar_tensor_tensor(out=contrib[u][:, s, :], in0=contrib[u][:, s, :], scalar=weight[u][:, s:s + 1],
                                                       in1=gates[u][:, s, :], op0=ALU.mult, op1=ALU.mult).then_inc(y_ok, 1)
                    if more:
                        batch_of_slots(ep + 1, u)

            with dve.Fori(0, E // 2 - 1) as ep:
                experts(ep, True)
            experts(E // 2 - 1, False)

        @block.tensor
        def _(pe):
            pe.wait_ge(cst, 5)
            with pe.Fori(0, TOP_BIT + 1) as i:
                pe.wait_ge(cnt_in, i + 1)
                nc.tensor.matmul(c_ps[:, 0:EB], ones_bf[:], mask[:, 0].rearrange("p e n -> p (e n)"), start=True, stop=True).then_inc(cnt_mm, 1)
            pe.wait_ge(mask_ok, 2)
            for m in range(2):
                src = mask[:, m].rearrange("p e n -> p (e n)")
                nc.tensor.matmul(a_ps[m][:, 0:EB], before_bf[:], src, start=True, stop=True)
                mm = nc.tensor.matmul(a_ps[2 + m][:, 0:EB], ones_bf[:], src, start=True, stop=True)
            mm.then_inc(rank_mm, 1)
            with pe.Fori(0, E) as e:
                pe.wait_ge(hot_ok, e + 1)
                for n in range(NB):
                    mm = nc.tensor.matmul(c_ps[0:SLOT_HI, 0:2 * SLOT_LO], hot_hi[:, n, :], hot_id[:, n].rearrange("p m l -> p (m l)"),
                                          start=(n == 0), stop=(n == NB - 1))
                mm.then_inc(id_mm, 1)

            with pe.Fori(0, E // 2) as ep:
                for u in range(2):
                    e = ep * 2 + u
                    pe.wait_ge(got[u], (ep + 1) * (32 * ST))
                    pe.wait_ge(hid_ok, e * FT + 1)
                    for t in range(KT):
                        for s in range(ST):
                            mm = nc.tensor.transpose(a_ps[t][:, s * PART:(s + 1) * PART], rows[u][:, s, t * PART:(t + 1) * PART], ident[:])
                        mm.then_inc(rt_mm, 1)
                    pe.wait_ge(w_ld[u], (ep + 1) * (16 * W_DMAS))
                    pe.wait_ge(rt_ev, e * KT + KT + 1)
                    for f in range(FT):
                        if f >= 4:
                            pe.wait_ge(hid_ok, e * FT + f - 4 + 2)
                        for t in range(KT):
                            mm = nc.tensor.matmul(a_ps[f % 4][:, 0:TK], w1_sb[u][:, t, f * PART:(f + 1) * PART], rows_tr[:, t, :],
                                                  start=(t == 0), stop=(t == KT - 1))
                        mm.then_inc(hid_mm, 1)
                    pe.wait_ge(hid_ok, e * FT + FT + 1)
                    for s in range(ST):
                        pe.wait_ge(y_b, e * ST + s + 1)
                        for f in range(FT):
                            mm = nc.tensor.matmul(y_ps[s % 2][:, 0:D], hid[:, f, s * PART:(s + 1) * PART], w2_sb[u][:, f, :],
                                                  start=(f == 0), stop=(f == FT - 1))
                        mm.then_inc(y_mm, 1)


_INS = ['L0_attn_inputs', 'L0_attn_w_qkv', 'L0_attn_w_o', 'L0_ffn_router_w', 'L0_ffn_router_b', 'L0_ffn_w1', 'L0_ffn_b1', 'L0_ffn_w2', 'L0_ffn_b2', 'L0_c', 'L0_wmod']
TOPK = 512


def kernel(**inputs):
    import numpy as _np
    import concourse.bacc as _bacc
    from concourse import mybir as _mybir
    from concourse.bass_utils import run_bass_kernel_spmd as _run

    nc = _bacc.Bacc("TRN2", target_bir_lowering=False, num_devices=1)
    arrays, args = {}, []
    for name in _INS:
        a = _np.ascontiguousarray(inputs[name])
        arrays[f"in_{name}_dram"] = a
        args.append(nc.dram_tensor(f"in_{name}_dram", a.shape, _mybir.dt.from_np(a.dtype), kind="ExternalInput").ap())
    shape = tuple(inputs['L0_attn_inputs'].shape)
    out = nc.dram_tensor("out_0_dram", shape, _mybir.dt.from_np(_np.dtype('float32')), kind="ExternalOutput").ap()
    build_kernel(nc, *args, out, TOPK)
    r = _run(nc, [arrays], core_ids=[0])
    return r.results[0]["out_0_dram"]
```

```python
from contextlib import ExitStack

import concourse.bass as bass
from concourse import mybir

F32 = mybir.dt.float32
F32R = mybir.dt.float32r
BF16 = mybir.dt.bfloat16
F16 = mybir.dt.float16
I32 = mybir.dt.int32
U32 = mybir.dt.uint32
ALU = mybir.AluOpType
ACT = mybir.ActivationFunctionType
AX = mybir.AxisListType

LN_EPS = 1e-5
GATE_FLOOR = 0.25
PART = 128
HALF = 512

LOW_ON_DVE = (0, 7)
LOW_ON_POOL = (1, 2, 3, 4, 5, 6)
MAX_BEFORE = {4: 2, 5: 3, 6: 5, 7: 7}
MAX_AFTER = {2: 0, 3: 1, 5: 4, 6: 6}

PROJECT_AT = {1: 0, 4: 1}
NORM_TURN_AT = {4: (0, 1), 6: (2, 3)}
FIRST_MAX_AT = {8: 0, 9: 1, 10: 2, 11: 3, 12: 4, 13: 5, 14: 6, 15: 7}
TURN_AT = {9: 0, 10: 1, 11: 2, 12: 3}
LOGITS_AT = 14


def count_upto(tiles, j):
    return sum(1 for t in tiles if t <= j)


def build_kernel(nc, x, w_qkv, w_o, router_w, router_b, w1, b1, w2, b2, c, wmod, out, topk):
    B, P, D = x.shape
    H, _, _, N = w_qkv.shape
    E, _, F = w1.shape
    NQ = P // PART
    KT = D // PART
    HT = H * N // PART
    NB = B * P // PART
    SCALE = float(N) ** -0.5
    VW = 3 * (N + 1)
    VHI = 3 * N + 2
    VLO = 2 * N + 1
    ST = topk // PART
    FT = F // PART
    ROW = D + E
    SLOT_LO = 32
    SLOT_HI = topk // SLOT_LO
    assert NQ == 8 and KT == 2 and N == 64 and D == 256 and E == 8 and HALF == E * N

    x_t = x.rearrange("b (q p) d -> b p q d", p=PART)
    out_t = out.rearrange("b (q p) d -> b p q d", p=PART)
    out_rows = out.rearrange("b p d -> (b p) d")
    rows_dram = nc.dram_tensor("rows_dram", (B * P, ROW), F32, kind="Internal").ap()
    rows_t = rows_dram.rearrange("(b q p) r -> b p q r", p=PART, q=NQ)
    rows_blk = rows_dram.rearrange("(n p) r -> p n r", p=PART)
    mods_dram = nc.dram_tensor("mods_dram", (B, 4 * D), F32, kind="Internal").ap()
    gate_dram = nc.dram_tensor("gate_dram", (B, D), F32, kind="Internal").ap()
    slots_dram = nc.dram_tensor("slots_dram", (E, topk), U32, kind="Internal").ap()

    with ExitStack() as outer:
        def keep(name, shape, dt):
            return outer.enter_context(nc.sbuf_tensor(name, shape, dt))

        ident = keep("ident", [PART, PART], F32)
        ident_bf = keep("ident_bf", [PART, PART], BF16)
        logits = keep("logits", [PART, NB, E], F32)
        minus_half = keep("minus_half", [PART, NQ], F32)

        attention_phase(nc, locals())
        ffn_phase(nc, locals())


def attention_phase(nc, k):
    B, P, D, H, N, E = k["B"], k["P"], k["D"], k["H"], k["N"], k["E"]
    NQ, KT, HT, SCALE, VW, VHI, VLO = k["NQ"], k["KT"], k["HT"], k["SCALE"], k["VW"], k["VHI"], k["VLO"]
    ident, ident_bf, logits, minus_half = k["ident"], k["ident_bf"], k["logits"], k["minus_half"]
    x_t, out_t, rows_t, mods_dram, gate_dram = k["x_t"], k["out_t"], k["rows_t"], k["mods_dram"], k["gate_dram"]
    w_qkv, w_o, router_w, router_b, c, wmod = k["w_qkv"], k["w_o"], k["router_w"], k["router_b"], k["c"], k["wmod"]
    HG = HALF // N
    NG = H // HG
    LD, LP = len(LOW_ON_DVE), len(LOW_ON_POOL)
    NV = NQ * NG
    V_BUFS = 4
    assert NV == 16

    with ExitStack() as ctx:
        def sb(name, shape, dt):
            return ctx.enter_context(nc.sbuf_tensor(name, shape, dt))

        def ps(name, shape):
            return ctx.enter_context(nc.psum_tensor(name, shape, F32))

        def sem(name):
            return ctx.enter_context(nc.semaphore(name))

        silu_t = sb("silu_t", [PART, KT, B], F32)
        sig_t = sb("sig_t", [PART, KT, B], F32)
        c_t = sb("c_t", [PART, KT, B], F32)
        mod_t = sb("mod_t", [PART, 2 * KT, B], F32)
        mod_b = sb("mod_b", [PART, 2 * KT], F32)
        stats = sb("stats", [PART, NQ, 6], F32)
        mean = sb("mean", [PART, NQ], F32)
        mean_d = sb("mean_d", [PART, NQ], F32)
        var_eps = sb("var_eps", [PART, NQ], F32)
        rstd = sb("rstd", [PART, NQ], F32)
        h_t = sb("h_t", [PART, KT, P], F32)
        rw_sb = sb("rw_sb", [PART, KT, E], F32)
        rb_bc = sb("rb_bc", [PART, E], F32)
        wqk = [sb(f"wqk{u}", [PART, KT, 2, N], F32) for u in range(2)]
        q_hh = [sb(f"q_hh{u}", [PART, P], F32R) for u in range(2)]
        q_lc = [sb(f"q_lc{u}", [PART, P], F32R) for u in range(2)]
        k_hl = [sb(f"k_hl{u}", [PART, P], F32R) for u in range(2)]
        k_h1 = [sb(f"k_h1{u}", [PART, P], F32R) for u in range(2)]
        row_max = sb("row_max", [PART, NQ, 2], F32)
        neg_max = sb("neg_max", [PART, NQ], BF16)
        prob = sb("prob", [PART, 4, P], F32)
        p_hi = [sb(f"p_hi{u}", [PART, NQ, P], F16) for u in range(2)]
        p_lo = [sb(f"p_lo{u}", [PART, NQ, P], F16) for u in range(2)]
        v_all = sb("v_all", [PART, NQ, H, VW], BF16)
        pv_sum = sb("pv_sum", [PART, 2, 2, N], F32)
        pv_inv = sb("pv_inv", [PART, 2, 2], F32)
        heads = sb("heads", [PART, NQ, H * N], F32)

        def view(tensor, first, n):
            return tensor[:].rearrange("p q k -> p (q k)")[:, 2 * first:2 * (first + n)].bitcast(F32)

        x_sb = view(p_hi[0], 0, NQ * D).rearrange("p (q d) -> p q d", q=NQ)
        norm = view(p_hi[0], NQ * D, NQ * D).rearrange("p (q d) -> p q d", q=NQ)
        wv_sb = view(p_hi[1], 0, KT * H * N).rearrange("p (t h n) -> p t h n", t=KT, h=H)
        prob_flat = prob[:].rearrange("p j k -> p (j k)")
        mod_rows = prob_flat[:, 0:3 * D].rearrange("p (m d) -> p m d", m=3)
        v_rest = prob_flat[:, P:P + V_BUFS * HALF].rearrange("p (u n) -> p u n", u=V_BUFS)
        wo_sb = view(p_lo[0], 0, HT * D).rearrange("p (t d) -> p t d", t=HT)
        heads_t = [view(p_lo[0], HT * (D + u * PART), HT * PART).rearrange("p (t n) -> p t n", t=HT) for u in range(2)]
        h2_t = view(p_lo[0], 0, KT * P).rearrange("p (t n) -> p t n", t=KT)
        x1_sb = view(p_lo[1], 0, NQ * D).rearrange("p (q d) -> p q d", q=NQ)
        h2_sb = view(p_lo[1], NQ * D, NQ * D).rearrange("p (q d) -> p q d", q=NQ)
        wmod_sb = view(p_lo[1], 0, KT * 6 * D).rearrange("p (t m) -> p t m", t=KT)
        mods = view(p_lo[1], KT * 6 * D, 4 * D).rearrange("p (m d) -> p m d", m=4)[0:B]
        mods_s = prob[0:B, 0, 0:4 * D].rearrange("p (m d) -> p m d", m=4)

        st_ps = [ps(f"st_ps{u}", [PART, P]) for u in range(2)]
        max_ps = ps("max_ps", [PART, P])
        pv_ps = ps("pv_ps", [PART, HALF])
        ms_ps = ps("ms_ps", [PART, HALF])

        const_ld = sem("const_ld")
        ident_z = sem("ident_z")
        ident_ok = sem("ident_ok")
        fill_ok = sem("fill_ok")
        c_exp = sem("c_exp")
        c_silu = sem("c_silu")
        mod_mm = sem("mod_mm")
        mod_ok = sem("mod_ok")
        x_ld = sem("x_ld")
        x_again = sem("x_again")
        ln1 = sem("ln1")
        ln1_in = sem("ln1_in")
        ln1_pow = sem("ln1_pow")
        norm_ok = sem("norm_ok")
        ht_in_mm = sem("ht_in_mm")
        ht_in_ev = sem("ht_in_ev")
        ln2 = sem("ln2")
        ln2_in = sem("ln2_in")
        ln2_pow = sem("ln2_pow")
        h2t_mm = sem("h2t_mm")
        h2t_ev = sem("h2t_ev")
        v_mm = sem("v_mm")
        v1_ok = sem("v1_ok")
        v_sub = sem("v_sub")
        v2_ok = sem("v2_ok")
        v3_ok = sem("v3_ok")
        wqk_ld = [sem(f"wqk_ld{u}") for u in range(2)]
        proj_mm = sem("proj_mm")
        high_ok = sem("high_ok")
        low_ok = sem("low_ok")
        dup_ok = [sem(f"dup_ok{u}") for u in range(2)]
        max_mm = sem("max_mm")
        max_red = sem("max_red")
        neg_ok = sem("neg_ok")
        crow_mm = sem("crow_mm")
        crow_ok = sem("crow_ok")
        st_mm = sem("st_mm")
        exp_ok = sem("exp_ok")
        phi_ok = sem("phi_ok")
        plo_dve = sem("plo_dve")
        plo_pool = sem("plo_pool")
        pv_mm = sem("pv_mm")
        pv_red = sem("pv_red")
        pv_ev = sem("pv_ev")
        head_ok = sem("head_ok")
        ht_mm = sem("ht_mm")
        ht_ev = sem("ht_ev")
        o_mm = sem("o_mm")
        gated = sem("gated")
        x1_ok = sem("x1_ok")
        h2_scaled = sem("h2_scaled")
        h2_ok = sem("h2_ok")
        lg_mm = sem("lg_mm")
        lg_ok = sem("lg_ok")
        st_rows = sem("st_rows")

        EXP_CREDIT, PV_CREDIT, VSUB_CREDIT, V3_CREDIT, HEAD_CREDIT = 2, 5, 4, V_BUFS, 2
        RED_CREDIT = 2
        LN1_STEPS, LN2_STEPS = 1 + NQ + 6, NQ + 6
        N_CONST = 5

        wv_ld = sem("wv_ld")
        wo_ld = sem("wo_ld")
        mods_st = sem("mods_st")
        mods_ld = sem("mods_ld")
        x1_row = sem("x1_row")

        block = ctx.enter_context(nc.Block())

        def run_heads(eng, head):
            head(0, 0, True)
            head(1, 1, False)
            with eng.Fori(1, H // 2 - 1) as hp:
                head(hp * 2, 0, False)
                head(hp * 2 + 1, 1, False)
            head(H - 2, 0, False)
            head(H - 1, 1, False)

        def is_at(t, n):
            return isinstance(t, int) and t == n

        def pair_dmas(b, t, u):
            return b * (H * 16) + (t - u) * 16 + 32

        def tile_cols(j):
            return slice(j * PART, (j + 1) * PART)

        def half_cols(h):
            return slice(h * HALF, (h + 1) * HALF)

        @block.sync
        def _(sp):
            for t in range(KT):
                sp.dma_start(c_t[:, t, :], c[:, t * PART:(t + 1) * PART].rearrange("b p -> p b"),
                             allow_slow_non_contiguous=True).then_inc(const_ld, 16)
            sp.dma_start(wmod_sb[:], wmod.rearrange("(t p) m -> p t m", p=PART)).then_inc(const_ld, 16)
            sp.dma_start(rw_sb[:], router_w.rearrange("(t p) e -> p t e", p=PART)).then_inc(const_ld, 16)
            sp.dma_start(rb_bc[:], router_b.partition_broadcast(PART)).then_inc(const_ld, 16)

            def load_wv():
                for t in range(KT):
                    sp.dma_start(wv_sb[:, t], w_qkv[:, 2, t * PART:(t + 1) * PART, :].rearrange("h p n -> p h n")).then_inc(wv_ld, 16)

            def load_wqk(t, u):
                for a in range(2):
                    sp.dma_start(wqk[u][:, :, a, :],
                                 w_qkv[bass.ds(t, 1), a].rearrange("o (t p) n -> p (o t) n", p=PART)).then_inc(wqk_ld[u], 16)

            def load_x(b):
                sp.dma_start(x_sb, x_t[bass.ds(b, 1)].rearrange("o p q d -> p (o q) d")).then_inc(x_ld, 16)

            def head(b, t, u, nxt):
                g = b * H + t
                if nxt is not None:
                    sp.wait_ge(proj_mm, g * 2 + 1)
                    load_wqk(nxt, 1 - u)
                sp.wait_ge(high_ok, g * 4 + 4)
                sp.dma_start(q_hh[u][N:2 * N, :].bitcast(F32), q_hh[u][0:N, :].bitcast(F32)).then_inc(dup_ok[u], 16)
                sp.dma_start(k_h1[u][0:N, :].bitcast(F32), k_hl[u][0:N, :].bitcast(F32)).then_inc(dup_ok[u], 16)

            def other_heads(b, more):
                head(b, 1, 1, 2)
                with sp.Fori(1, H // 2 - 1) as hp:
                    head(b, hp * 2, 0, hp * 2 + 1)
                    head(b, hp * 2 + 1, 1, hp * 2 + 2)
                head(b, H - 2, 0, H - 1)
                head(b, H - 1, 1, 0 if more else None)

            def boundary(b, more):
                sp.wait_ge(pv_mm, (b + 1) * (H * 4) - 4 + PV_CREDIT)
                if more:
                    load_x(b + 1)
                sp.dma_start(wo_sb, w_o.rearrange("(t p) d -> p t d", p=PART)).then_inc(wo_ld, 16)
                sp.wait_ge(pv_mm, (b + 1) * (H * 4) - 3 + PV_CREDIT)
                sp.dma_start(mod_rows.rearrange("p m d -> p (m d)"),
                             mods_dram[bass.ds(b, 1), 0:3 * D].rearrange("o m -> (o m)").partition_broadcast(PART)).then_inc(mods_ld, 16)
                sp.wait_ge(pv_mm, (b + 1) * (H * 4) + PV_CREDIT)
                sp.dma_start(x1_sb, x_t[bass.ds(b, 1)].rearrange("o p q d -> p (o q) d")).then_inc(x_again, 16)
                if more:
                    load_wv()
                sp.wait_ge(x1_ok, b + 1)
                sp.dma_start(out_t[bass.ds(b, 1)].rearrange("o p q d -> p (o q) d"), x1_sb).then_inc(st_rows, 16)
                if more:
                    head(b + 1, 0, 0, 1)
                sp.wait_ge(h2_ok, (b + 1) * NQ)
                sp.dma_start(rows_t[bass.ds(b, 1), :, :, 0:D].rearrange("o p q d -> p (o q) d"), h2_sb).then_inc(st_rows, 16)

            load_x(0)
            load_wqk(0, 0)
            load_wv()
            sp.wait_ge(mod_ok, 14)
            sp.dma_start(mods_dram, mods.rearrange("b m d -> b (m d)")).then_inc(mods_st, 16)
            sp.dma_start(gate_dram, mods[:, 3, :]).then_inc(mods_st, 16)
            sp.wait_ge(mods_st, 32)
            sp.sem_inc(st_rows, 32)
            head(0, 0, 0, 1)
            with sp.Fori(0, B - 1) as b:
                other_heads(b, True)
                boundary(b, True)
            other_heads(B - 1, False)
            boundary(B - 1, False)
            sp.wait_ge(st_rows, 32 * B + 32)

        @block.gpsimd
        def _(pool):
            nc.gpsimd.memset(ident[:], 0.0).then_inc(ident_z, 1)
            nc.gpsimd.memset(minus_half[:], -0.5).then_inc(ident_z, 1)
            pool.wait_ge(ident_z, 2)
            nc.gpsimd.affine_select(out=ident[:], in_=ident[:], compare_op=ALU.not_equal, fill=1.0, base=0,
                                    pattern=[[-1, PART]], channel_multiplier=1).then_inc(ident_z, 1)
            pool.wait_ge(ident_z, 3)
            nc.gpsimd.tensor_copy(ident_bf[:], ident[:]).then_inc(ident_ok, 1)
            pool.sem_inc(plo_pool, LP)
            pool.sem_inc(v3_ok, V3_CREDIT)
            pool.sem_inc(head_ok, HEAD_CREDIT)

            def inv_std(ready, done, n):
                pool.wait_ge(ready, n + 1)
                nc.gpsimd.tensor_tensor(rstd[:], var_eps[:], minus_half[:], ALU.pow).then_inc(done, 1)

            def third_parts(b):
                for i in range(NV):
                    kb, hg = i // NG, i % NG
                    rest = v_rest[:, i % V_BUFS, :].rearrange("p (h n) -> p h n", n=N)
                    v2 = v_all[:, kb, hg * HG:(hg + 1) * HG, N + 1:2 * N + 1]
                    v3 = v_all[:, kb, hg * HG:(hg + 1) * HG, 2 * N + 2:3 * N + 2]
                    pool.wait_ge(v2_ok, b * NV + i + 1)
                    nc.gpsimd.tensor_tensor(v3, rest, v2, ALU.subtract).then_inc(v3_ok, 1)

            def low(b, t, u, j):
                g = b * H + t
                pool.wait_ge(phi_ok, g * NQ + j + 1)
                if is_at(t, 1) and j == LOW_ON_POOL[0]:
                    pool.wait_ge(st_rows, b * 32 + 32)
                nc.gpsimd.tensor_tensor(p_lo[u][:, j, :], prob[:, j % 4, :], p_hi[u][:, j, :],
                                        ALU.subtract).then_inc(plo_pool, 1)

            def scale_pair(b, t, p):
                m = b * (H * 4) + t * 4 + p
                pool.wait_ge(pv_ev, m + 2)
                nc.gpsimd.tensor_tensor(heads[:, 2 * p:2 * p + 2, bass.ds(t * N, N)], pv_sum[:, p % 2],
                                        pv_inv[:, p % 2, :].unsqueeze(2).to_broadcast([PART, 2, N]),
                                        ALU.mult).then_inc(head_ok, 1)

            def all_heads(b):
                def head(t, u, first):
                    for j in range(NQ):
                        if not first and j and j % 2 == 0:
                            scale_pair(b, t - 1, j // 2 - 1)
                        if j in LOW_ON_POOL:
                            low(b, t, u, j)
                    if not first:
                        scale_pair(b, t - 1, NQ // 2 - 1)

                run_heads(pool, head)

            def boundary(b, more):
                for p in range(NQ // 2):
                    scale_pair(b, H - 1, p)
                if more:
                    inv_std(ln1_in, ln1_pow, b + 1)
                inv_std(ln2_in, ln2_pow, b)
                if more:
                    third_parts(b + 1)

            inv_std(ln1_in, ln1_pow, 0)
            third_parts(0)
            with pool.Fori(0, B - 1) as b:
                all_heads(b)
                boundary(b, True)
            all_heads(B - 1)
            boundary(B - 1, False)

        @block.scalar
        def _(act):
            act.sem_inc(exp_ok, EXP_CREDIT)
            act.wait_ge(const_ld, 16 * N_CONST)
            nc.scalar.activation(sig_t[:], c_t[:], ACT.Exp, scale=-1.0).then_inc(c_exp, 1)

            def v_stage(b, before):
                def second_part(i):
                    kb, hg = i // NG, i % NG
                    act.wait_ge(v_sub, b * NV + i + VSUB_CREDIT + 1)
                    nc.scalar.activation(v_all[:, kb, hg * HG:(hg + 1) * HG, N + 1:2 * N + 1],
                                         v_rest[:, i % V_BUFS, :].rearrange("p (h n) -> p h n", n=N), ACT.Copy).then_inc(v2_ok, 1)

                for i in range(NV):
                    kb, hg = i // NG, i % NG
                    act.wait_ge(v_mm, b * NV + i + 1)
                    src = st_ps[(i % 4) // 2][:, half_cols(i % 2)].rearrange("p (h n) -> p h n", n=N)
                    nc.scalar.activation(v_all[:, kb, hg * HG:(hg + 1) * HG, 0:N], src, ACT.Copy).then_inc(v1_ok, 1)
                    if i:
                        second_part(i - 1)
                    if i - 1 in PROJECT_AT:
                        high(b * H, 0, PROJECT_AT[i - 1])
                    if before is not None and i in TURN_AT:
                        h2_turned(before, TURN_AT[i])
                second_part(NV - 1)

            def h2_turned(b, i):
                kt, h = i // 2, i % 2
                act.wait_ge(h2t_mm, b * (2 * KT) + i + 1)
                nc.scalar.activation(h2_t[:, kt, half_cols(h)], pv_ps[:], ACT.Copy).then_inc(h2t_ev, 1)

            def high(g, u, h):
                act.wait_ge(proj_mm, g * 2 + h + 2)
                nc.scalar.activation(q_hh[u][0:N, half_cols(h)], ms_ps[0:N, :], ACT.Copy).then_inc(high_ok, 1)
                nc.scalar.activation(k_hl[u][0:N, half_cols(h)], ms_ps[N:2 * N, :], ACT.Copy).then_inc(high_ok, 1)

            def all_heads(b):
                def prob_tile(g, u, j, between=None):
                    act.wait_ge(st_mm, g * NQ + j + 1)
                    if j >= 4:
                        if (j - 4) in LOW_ON_DVE:
                            act.wait_ge(plo_dve, g * LD + LD + count_upto(LOW_ON_DVE, j - 4))
                        else:
                            act.wait_ge(plo_pool, g * LP + LP + count_upto(LOW_ON_POOL, j - 4))
                    elif (j + 4) in LOW_ON_DVE:
                        act.wait_ge(plo_dve, g * LD + count_upto(LOW_ON_DVE, j + 4))
                    else:
                        act.wait_ge(plo_pool, g * LP + count_upto(LOW_ON_POOL, j + 4))
                    nc.scalar.activation(prob[:, j % 4, :], st_ps[j % 2][:], ACT.Exp, scale=SCALE).then_inc(exp_ok, 1)
                    if between:
                        between()
                    if j == 0:
                        act.wait_ge(pv_mm, g * 4 + PV_CREDIT - 4)
                    act.wait_ge(exp_ok, EXP_CREDIT + g * NQ + j + 1)
                    nc.scalar.activation(p_hi[u][:, j, :], prob[:, j % 4, :], ACT.Copy).then_inc(phi_ok, 1)

                def crow(g, u):
                    act.wait_ge(crow_mm, g + 1)
                    nc.scalar.activation(q_lc[u][N:N + 1, :], max_ps[0:1, :], ACT.Copy).then_inc(crow_ok, 1)

                high(b * H + 1, 1, 0)
                crow(b * H, 0)
                act.wait_ge(v3_ok, (b + 1) * NV + V3_CREDIT)

                def head(t, u, first):
                    g = b * H + t
                    last = is_at(t, H - 1)
                    if not last:
                        high(g + 1, 1 - u, 1)
                    for j in range(NQ - 1):
                        prob_tile(g, u, j)
                    more = not last and not is_at(t, H - 2)
                    prob_tile(g, u, NQ - 1, (lambda: high(g + 2, u, 0)) if more else None)
                    if not last:
                        crow(g + 1, 1 - u)

                run_heads(act, head)

            def boundary(b, more):
                for q in range(NQ):
                    act.wait_ge(ht_mm, b * NQ + q + 1)
                    if q >= 2:
                        act.wait_ge(o_mm, b * NQ + q - 1)
                    nc.scalar.activation(heads_t[q % 2], st_ps[q % 2][:, 0:HT * PART].rearrange("p (t n) -> p t n", n=PART), ACT.Copy).then_inc(ht_ev, 1)
                if more:
                    v_stage(b + 1, b)
                else:
                    for i in range(2 * KT):
                        h2_turned(b, i)

            v_stage(0, None)
            with act.Fori(0, B - 1) as b:
                all_heads(b)
                boundary(b, True)
            all_heads(B - 1)
            boundary(B - 1, False)

        @block.vector
        def _(dve):
            dve.sem_inc(plo_dve, LD)
            dve.sem_inc(v_sub, VSUB_CREDIT)
            dve.sem_inc(max_red, RED_CREDIT)
            for s_one in (low_ok, pv_ev, lg_ok):
                dve.sem_inc(s_one, 1)
            for u in range(2):
                nc.vector.memset(k_h1[u][N:2 * N, :].bitcast(F32), 0.0).then_inc(fill_ok, 1)
                nc.vector.memset(q_lc[u][N:2 * N, :].bitcast(F32), 0.0).then_inc(fill_ok, 1)
            nc.vector.memset(v_all[:, :, :, N:N + 1], 1.0).then_inc(fill_ok, 1)
            nc.vector.memset(v_all[:, :, :, 2 * N + 1:2 * N + 2], 0.0).then_inc(fill_ok, 1)
            dve.wait_ge(fill_ok, 6)
            for u in range(2):
                nc.vector.memset(k_h1[u][N:N + 1, :].bitcast(F32), 1.0).then_inc(fill_ok, 1)
            dve.wait_ge(c_exp, 1)
            nc.vector.tensor_scalar(sig_t[:], sig_t[:], 1.0, None, ALU.add).then_inc(c_silu, 1)
            dve.wait_ge(c_silu, 1)
            nc.vector.reciprocal(sig_t[:], sig_t[:]).then_inc(c_silu, 1)
            dve.wait_ge(c_silu, 2)
            nc.vector.tensor_tensor(silu_t[:], c_t[:], sig_t[:], ALU.mult).then_inc(c_silu, 1)
            dve.wait_ge(mod_mm, 1)
            md = ms_ps[:, 0:2 * KT * B].rearrange("p (m b) -> p m b", b=B)
            nc.vector.tensor_copy(mod_t[:, 0:KT, :], md[:, 0:KT]).then_inc(mod_ok, 1)
            nc.vector.tensor_scalar(mod_t[:, KT:2 * KT, :], md[:, KT:2 * KT], 1.0, None, ALU.add).then_inc(mod_ok, 1)
            raw = st_ps[0][0:B, :].rearrange("b (m d) -> b m d", m=4)
            nc.vector.tensor_copy(mods[:, 1, :], raw[:, 1]).then_inc(mod_ok, 1)
            nc.vector.tensor_scalar(mods[:, 2, :], raw[:, 2], 1.0, None, ALU.add).then_inc(mod_ok, 1)
            for i, m in enumerate((0, 3)):
                nc.vector.tensor_scalar(mods_s[:, 2 * i], raw[:, m], 0.0, None, ALU.is_ge).then_inc(mod_ok, 1)
                nc.vector.tensor_scalar(mods_s[:, 2 * i + 1], raw[:, m], 0.0, None, ALU.is_lt).then_inc(mod_ok, 1)
            dve.wait_ge(mod_ok, 8)
            for i, m in enumerate((0, 3)):
                nc.vector.scalar_tensor_tensor(out=mods_s[:, 2 * i], in0=raw[:, m], scalar=GATE_FLOOR, in1=mods_s[:, 2 * i],
                                               op0=ALU.max, op1=ALU.mult).then_inc(mod_ok, 1)
                nc.vector.scalar_tensor_tensor(out=mods_s[:, 2 * i + 1], in0=raw[:, m], scalar=-GATE_FLOOR,
                                               in1=mods_s[:, 2 * i + 1], op0=ALU.min, op1=ALU.mult).then_inc(mod_ok, 1)
            dve.wait_ge(mod_ok, 12)
            for i, m in enumerate((0, 3)):
                nc.vector.tensor_tensor(mods[:, m, :], mods_s[:, 2 * i], mods_s[:, 2 * i + 1], ALU.add).then_inc(mod_ok, 1)

            def steps_of(signal, base, n):
                def step(ins, wait=True):
                    ins.then_inc(signal, 1)
                    n[0] += 1
                    if wait:
                        dve.wait_ge(signal, base + n[0])

                return step

            def mean_and_var(step, ready):
                mean_e, mean_o, m2_e, m2_o = stats[:, :, 1], stats[:, :, 4], stats[:, :, 2], stats[:, :, 5]
                step(nc.vector.tensor_tensor(mean[:], mean_e, mean_o, ALU.add), False)
                step(nc.vector.tensor_tensor(mean_d[:], mean_e, mean_o, ALU.subtract), False)
                step(nc.vector.tensor_tensor(var_eps[:], m2_e, m2_o, ALU.add))
                step(nc.vector.tensor_scalar(mean[:], mean[:], 0.5, None, ALU.mult), False)
                step(nc.vector.scalar_tensor_tensor(out=mean_d[:], in0=mean_d[:], scalar=0.25, in1=mean_d[:],
                                                    op0=ALU.mult, op1=ALU.mult), False)
                step(nc.vector.tensor_scalar(var_eps[:], var_eps[:], 1.0 / D, LN_EPS, ALU.mult, ALU.add))
                nc.vector.tensor_tensor(var_eps[:], var_eps[:], mean_d[:], ALU.add).then_inc(ready, 1)

            def first_norm(b):
                n1 = [0]
                step = steps_of(ln1, b * LN1_STEPS, n1)
                step(nc.vector.tensor_copy(mod_b[:], mod_t[:, :, bass.ds(b, 1)].rearrange("p m o -> p (m o)")), False)
                dve.wait_ge(x_ld, b * 16 + 16)
                for q in range(NQ):
                    step(nc.vector.bn_stats(stats[:, q, :], x_sb[:, q, :]), q == NQ - 1)
                mean_and_var(step, ln1_in)
                assert n1[0] == LN1_STEPS
                dve.wait_ge(ln1_pow, b + 1)
                for q in range(NQ):
                    nc.vector.tensor_scalar(norm[:, q, :], x_sb[:, q, :], mean[:, q:q + 1], rstd[:, q:q + 1],
                                            ALU.subtract, ALU.mult).then_inc(norm_ok, 1)

            def modulate(b, i):
                kt, h = i // 2, i % 2
                dve.wait_ge(ht_in_mm, b * (2 * KT) + i + 1)
                nc.vector.tensor_scalar(h_t[:, kt, half_cols(h)], max_ps[:, half_cols(i % 2)], mod_b[:, KT + kt:KT + kt + 1],
                                        mod_b[:, kt:kt + 1], ALU.mult, ALU.add).then_inc(ht_in_ev, 1)

            def v_stage(b, before):
                for i in range(NV):
                    kb, hg = i // NG, i % NG
                    n = b * NV + i
                    dve.wait_ge(v1_ok, n + 1)
                    dve.wait_ge(v3_ok, n + 1)
                    src = st_ps[(i % 4) // 2][:, half_cols(i % 2)].rearrange("p (h n) -> p h n", n=N)
                    nc.vector.tensor_tensor(v_rest[:, i % V_BUFS, :].rearrange("p (h n) -> p h n", n=N), src,
                                            v_all[:, kb, hg * HG:(hg + 1) * HG, 0:N], ALU.subtract).then_inc(v_sub, 1)
                    if before is not None:
                        h2_rows(before, i)
                        if i == LOGITS_AT + 1:
                            add_bias(before)
                    if i - 2 in PROJECT_AT:
                        lows(b * H, 0, PROJECT_AT[i - 2])
                    if i in FIRST_MAX_AT:
                        reduce_max(b * H, FIRST_MAX_AT[i])
                negate(b * H)

            def h2_rows(b, i):
                if i == 0:
                    dve.wait_ge(ln2_pow, b + 1)
                if i < NQ // 2:
                    for q in (2 * i, 2 * i + 1):
                        nc.vector.scalar_tensor_tensor(out=h2_sb[:, q, :], in0=x1_sb[:, q, :], scalar=mean[:, q:q + 1], in1=mod_rows[:, 2],
                                                       op0=ALU.subtract, op1=ALU.mult).then_inc(h2_scaled, 1)
                elif i < NQ:
                    for q in (2 * i - NQ, 2 * i - NQ + 1):
                        dve.wait_ge(h2_scaled, b * NQ + q + 1)
                        nc.vector.scalar_tensor_tensor(out=h2_sb[:, q, :], in0=h2_sb[:, q, :], scalar=rstd[:, q:q + 1], in1=mod_rows[:, 1],
                                                       op0=ALU.mult, op1=ALU.add).then_inc(h2_ok, 1)

            def add_bias(b):
                dve.wait_ge(lg_mm, b + 1)
                nc.vector.tensor_tensor(logits[:, bass.ds(b * NQ, NQ), :], pv_ps[:, 0:NQ * E].rearrange("p (q e) -> p q e", e=E),
                                        rb_bc[:].unsqueeze(1).to_broadcast([PART, NQ, E]), ALU.add).then_inc(lg_ok, 1)

            def lows(g, u, h):
                dve.wait_ge(high_ok, g * 4 + 2 * h + 2)
                nc.vector.tensor_tensor(q_lc[u][0:N, half_cols(h)], ms_ps[0:N, :],
                                        q_hh[u][0:N, half_cols(h)].bitcast(F32), ALU.subtract).then_inc(low_ok, 1)
                nc.vector.tensor_tensor(k_hl[u][N:2 * N, half_cols(h)], ms_ps[N:2 * N, :],
                                        k_hl[u][0:N, half_cols(h)].bitcast(F32), ALU.subtract).then_inc(low_ok, 1)

            def reduce_max(g, i):
                for h in range(2):
                    dve.wait_ge(max_mm, g * (2 * NQ) + 2 * i + h + 1)
                    nc.vector.tensor_reduce(row_max[:, i, h:h + 1], max_ps[:, half_cols(h)], AX.X, ALU.max).then_inc(max_red, 1)

            def negate(g):
                dve.wait_ge(max_red, g * (2 * NQ) + 2 * NQ + RED_CREDIT)
                nc.vector.tensor_reduce(neg_max[:], row_max[:], AX.X, ALU.max, negate=True).then_inc(neg_ok, 1)

            def low(b, t, u, j):
                g = b * H + t
                dve.wait_ge(phi_ok, g * NQ + j + 1)
                if is_at(t, 1) and j == LOW_ON_DVE[0]:
                    dve.wait_ge(st_rows, b * 32 + 32)
                nc.vector.tensor_tensor(p_lo[u][:, j, :], prob[:, j % 4, :], p_hi[u][:, j, :],
                                        ALU.subtract).then_inc(plo_dve, 1)

            def collect(g, p, bank):
                m = g * 4 + p
                dve.wait_ge(pv_mm, PV_CREDIT + m + 1)
                dve.wait_ge(head_ok, m + 1)
                src = bank[:, 0:2 * VW].rearrange("p (q w) -> p q w", q=2)
                nc.vector.tensor_reduce(pv_sum[:, p % 2], src.rearrange("p q (v n) -> p q n v", v=3)[:, :, 0:N, :],
                                        AX.X, ALU.add).then_inc(pv_red, 1)
                dve.wait_ge(pv_red, m + 1)
                nc.vector.reciprocal(pv_inv[:, p % 2, :], src[:, :, N]).then_inc(pv_ev, 1)

            def all_heads(b):
                lows(b * H + 1, 1, 0)

                def head(t, u, first):
                    g = b * H + t
                    last = is_at(t, H - 1)
                    for j in range(NQ):
                        if j == 0 and not last:
                            lows(g + 1, 1 - u, 1)
                        if j in MAX_BEFORE and not last:
                            reduce_max(g + 1, MAX_BEFORE[j])
                        if j == NQ - 1 and not last:
                            negate(g + 1)
                            if not is_at(t, H - 2):
                                lows(g + 2, u, 0)
                        if j and j % 2 == 0 and not first:
                            collect(g - 1, j // 2 - 1, pv_ps)
                        if j in MAX_AFTER and not last:
                            reduce_max(g + 1, MAX_AFTER[j])
                        if j in LOW_ON_DVE:
                            low(b, t, u, j)
                    if not first:
                        collect(g - 1, NQ // 2 - 1, pv_ps)

                run_heads(dve, head)
            def boundary(b, more):
                for p in range(NQ // 2):
                    collect(b * H + H - 1, p, (pv_ps, ms_ps)[p % 2])
                if more:
                    first_norm(b + 1)
                n2 = [0]
                step = steps_of(ln2, b * LN2_STEPS, n2)
                dve.wait_ge(mods_ld, b * 16 + 16)
                dve.wait_ge(x_again, b * 16 + 16)
                for q in range(NQ):
                    dve.wait_ge(o_mm, b * NQ + q + 1)
                    o_ps = (pv_ps if q % 2 == 0 else ms_ps)[:, 0:D]
                    nc.vector.tensor_tensor(h2_sb[:, q, :], o_ps, mod_rows[:, 0], ALU.mult).then_inc(gated, 1)
                    dve.wait_ge(gated, b * NQ + q + 1)
                    nc.vector.tensor_tensor(x1_sb[:, q, :], h2_sb[:, q, :], x1_sb[:, q, :], ALU.add).then_inc(x1_row, 1)
                    dve.wait_ge(x1_row, b * NQ + q + 1)
                    step(nc.vector.bn_stats(stats[:, q, :], x1_sb[:, q, :]), q == NQ - 1)
                    if more and q in NORM_TURN_AT:
                        for i in NORM_TURN_AT[q]:
                            modulate(b + 1, i)
                dve.sem_inc(x1_ok, 1)
                mean_and_var(step, ln2_in)
                assert n2[0] == LN2_STEPS
                if more:
                    v_stage(b + 1, b)
                else:
                    for i in range(NQ):
                        h2_rows(b, i)
                    add_bias(b)

            first_norm(0)
            for i in range(2 * KT):
                modulate(0, i)
            v_stage(0, None)
            with dve.Fori(0, B - 1) as b:
                all_heads(b)
                boundary(b, True)
            all_heads(B - 1)
            boundary(B - 1, False)

        @block.tensor
        def _(pe):
            pe.sem_inc(pv_mm, PV_CREDIT)
            pe.sem_inc(proj_mm, 1)
            pe.wait_ge(const_ld, 16 * N_CONST)
            pe.wait_ge(c_silu, 3)
            for m in range(2 * KT):
                for kt in range(KT):
                    nc.tensor.matmul(ms_ps[:, m * B:(m + 1) * B], wmod_sb[:, kt, tile_cols(m)], silu_t[:, kt, :],
                                     start=(kt == 0), stop=(kt == KT - 1))
            for h in range(2):
                for kt in range(KT):
                    mm = nc.tensor.matmul(st_ps[0][0:B, half_cols(h)], silu_t[:, kt, :], wmod_sb[:, kt, 2 * D + h * HALF:2 * D + (h + 1) * HALF],
                                          start=(kt == 0), stop=(kt == KT - 1))
            mm.then_inc(mod_mm, 1)
            pe.wait_ge(ident_ok, 1)
            pe.wait_ge(fill_ok, 8)
            pe.wait_ge(mod_ok, 14)

            def turn_norm(b, i):
                kt, h = i // 2, i % 2
                if i == 0:
                    pe.wait_ge(norm_ok, (b + 1) * NQ)
                if i >= 2:
                    pe.wait_ge(ht_in_ev, b * (2 * KT) + i - 1)
                for q in range(4):
                    mm = nc.tensor.transpose(max_ps[:, (i % 2) * HALF + q * PART:(i % 2) * HALF + (q + 1) * PART],
                                             norm[:, h * 4 + q, tile_cols(kt)], ident[:])
                mm.then_inc(ht_in_mm, 1)

            def turn_h2(b, i):
                kt, h = i // 2, i % 2
                if i == 0:
                    pe.wait_ge(h2_ok, (b + 1) * NQ)
                else:
                    pe.wait_ge(h2t_ev, b * (2 * KT) + i)
                for q in range(4):
                    mm = nc.tensor.transpose(pv_ps[:, tile_cols(q)], h2_sb[:, h * 4 + q, tile_cols(kt)], ident[:])
                mm.then_inc(h2t_mm, 1)

            def router_logits(b):
                pe.wait_ge(h2t_ev, b * (2 * KT) + 2 * KT)
                for q in range(NQ):
                    for kt in range(KT):
                        mm = nc.tensor.matmul(pv_ps[:, q * E:(q + 1) * E], h2_t[:, kt, tile_cols(q)], rw_sb[:, kt, :],
                                              start=(kt == 0), stop=(kt == KT - 1))
                mm.then_inc(lg_mm, 1)

            def project(b, t, u, h):
                g = b * H + t
                pe.wait_ge(low_ok, g * 4 + 2 * h + 1)
                if h == 0:
                    pe.wait_ge(wqk_ld[u], pair_dmas(b, t, u))
                for kt in range(KT):
                    mm = nc.tensor.matmul(ms_ps[:], wqk[u][:, kt].rearrange("p a n -> p (a n)"), h_t[:, kt, half_cols(h)],
                                          start=(kt == 0), stop=(kt == KT - 1))
                mm.then_inc(proj_mm, 1)

            def max_tile(b, t, u, i):
                g = b * H + t
                if i == 0:
                    pe.wait_ge(low_ok, g * 4 + 4 + 1)
                    pe.wait_ge(dup_ok[u], pair_dmas(b, t, u))
                for h in range(2):
                    pe.wait_ge(max_red, g * (2 * NQ) + 2 * i + h - 1 + RED_CREDIT)
                    mm = nc.tensor.matmul(max_ps[:, half_cols(h)], q_hh[u][:, tile_cols(i)], k_hl[u][:, half_cols(h)],
                                          start=True, stop=True)
                    mm.then_inc(max_mm, 1)

            def max_row(g):
                pe.wait_ge(neg_ok, g + 1)
                for q in range(NQ):
                    mm = nc.tensor.matmul(max_ps[0:1, tile_cols(q)], neg_max[:, q:q + 1], ident_bf[:], start=True, stop=True)
                mm.then_inc(crow_mm, 1)

            def scores(g, u, j):
                if j == 0:
                    pe.wait_ge(crow_ok, g + 1)
                pe.wait_ge(exp_ok, g * NQ + j - 1 + EXP_CREDIT)
                for h in range(2):
                    nc.tensor.matmul(st_ps[j % 2][:, half_cols(h)], k_hl[u][:, tile_cols(j)], q_hh[u][:, half_cols(h)],
                                     start=True, stop=False)
                for h in range(2):
                    mm = nc.tensor.matmul(st_ps[j % 2][:, half_cols(h)], k_h1[u][:, tile_cols(j)], q_lc[u][:, half_cols(h)],
                                          start=False, stop=True)
                mm.then_inc(st_mm, 1)

            def weighted(b, t, u, q, tail=False):
                g = b * H + t
                bank = (pv_ps, ms_ps)[(q // 2) % 2] if tail else pv_ps
                if q == 0:
                    pe.wait_ge(plo_dve, g * LD + 2 * LD)
                    pe.wait_ge(plo_pool, g * LP + 2 * LP)
                    pe.wait_ge(v3_ok, b * NV + NV + V3_CREDIT)
                if is_at(t, 0) and q == 0:
                    pe.wait_ge(lg_ok, b + 1)
                if q % 2 == 0 and tail and q == 2:
                    pe.wait_ge(low_ok, (b + 1) * (H * 4) + 1)
                elif q % 2 == 0:
                    pe.wait_ge(pv_ev, g * 4 + q // 2 + (0 if tail and q else 1))
                o = bank[:, (q % 2) * VW:(q % 2) * VW + VHI]
                for kb in range(NQ):
                    v = v_all[:, kb, bass.ds(t, 1), :].rearrange("p o w -> p (o w)")
                    nc.tensor.matmul(o, p_hi[u][:, kb, tile_cols(q)], v[:, 0:VHI], start=(kb == 0), stop=False)
                    mm = nc.tensor.matmul(o[:, 0:VLO], p_lo[u][:, kb, tile_cols(q)], v[:, 0:VLO],
                                          start=False, stop=(kb == NQ - 1))
                if q % 2 == 1:
                    mm.then_inc(pv_mm, 1)

            def v_stage(b, before):
                pe.wait_ge(ht_in_ev, b * (2 * KT) + 2 * KT)
                pe.wait_ge(wv_ld, b * (16 * KT) + 16 * KT)
                if before is not None:
                    pe.wait_ge(ht_ev, before * NQ + NQ)
                for i in range(NV):
                    kb, hg = i // NG, i % NG
                    pe.wait_ge(v_sub, b * NV + i + 1)
                    for kt in range(KT):
                        mm = nc.tensor.matmul(st_ps[(i % 4) // 2][:, half_cols(i % 2)], h_t[:, kt, tile_cols(kb)],
                                              wv_sb[:, kt, hg * HG:(hg + 1) * HG, :].rearrange("p h n -> p (h n)"),
                                              start=(kt == 0), stop=(kt == KT - 1))
                    mm.then_inc(v_mm, 1)
                    if i in PROJECT_AT:
                        if before is not None and PROJECT_AT[i] == 0:
                            pe.wait_ge(gated, (before + 1) * NQ)
                        project(b, 0, 0, PROJECT_AT[i])
                    if i in FIRST_MAX_AT:
                        max_tile(b, 0, 0, FIRST_MAX_AT[i])
                    if before is not None and i in TURN_AT:
                        turn_h2(before, TURN_AT[i])
                    if before is not None and i == LOGITS_AT:
                        router_logits(before)

            def all_heads(b):
                project(b, 1, 1, 0)
                max_row(b * H)

                def head(t, u, first):
                    g = b * H + t
                    last = is_at(t, H - 1)
                    for j in range(NQ):
                        if j == 0 and not last:
                            project(b, t + 1, 1 - u, 1)
                        scores(g, u, j)
                        if j == NQ - 1 and not last and not is_at(t, H - 2):
                            project(b, t + 2, u, 0)
                        if j in MAX_BEFORE and not last:
                            max_tile(b, t + 1, 1 - u, MAX_BEFORE[j])
                        if j and not first:
                            weighted(b, t - 1, 1 - u, j - 1)
                        if j in MAX_AFTER and not last:
                            max_tile(b, t + 1, 1 - u, MAX_AFTER[j])
                    if not first:
                        weighted(b, t - 1, 1 - u, NQ - 1)
                    if not last:
                        max_row(g + 1)

                run_heads(pe, head)

            def boundary(b, more):
                for q in range(NQ):
                    weighted(b, H - 1, 1, q, True)

                def turn(q):
                    if q >= 2:
                        pe.wait_ge(ht_ev, b * NQ + q - 1)
                    if q == 0:
                        pe.wait_ge(exp_ok, (b + 1) * (H * NQ) + EXP_CREDIT)
                        pe.wait_ge(head_ok, (b + 1) * (H * 4) + HEAD_CREDIT)
                    for t in range(HT):
                        mm = nc.tensor.transpose(st_ps[q % 2][:, tile_cols(t)], heads[:, q, tile_cols(t)], ident[:])
                    mm.then_inc(ht_mm, 1)

                pe.wait_ge(wo_ld, b * 16 + 16)
                turn(0)
                pe.wait_ge(pv_ev, (b + 1) * (H * 4) + 1)
                for q in range(NQ):
                    if q < NQ - 1:
                        turn(q + 1)
                    pe.wait_ge(ht_ev, b * NQ + q + 1)
                    if q >= 2:
                        pe.wait_ge(gated, b * NQ + q - 1)
                    o_ps = (pv_ps if q % 2 == 0 else ms_ps)[:, 0:D]
                    for t in range(HT):
                        mm = nc.tensor.matmul(o_ps, heads_t[q % 2][:, t, :], wo_sb[:, t, :], start=(t == 0), stop=(t == HT - 1))
                    mm.then_inc(o_mm, 1)
                    if more and q in NORM_TURN_AT:
                        pe.wait_ge(crow_ok, (b + 1) * H)
                        for i in NORM_TURN_AT[q]:
                            turn_norm(b + 1, i)
                if more:
                    v_stage(b + 1, b)
                else:
                    pe.wait_ge(gated, (b + 1) * NQ)
                    for i in range(2 * KT):
                        turn_h2(b, i)
                    router_logits(b)

            for i in range(2 * KT):
                turn_norm(0, i)
            v_stage(0, None)
            with pe.Fori(0, B - 1) as b:
                all_heads(b)
                boundary(b, True)
            all_heads(B - 1)
            boundary(B - 1, False)


def ffn_phase(nc, k):
    B, P, D, E, F, NB = k["B"], k["P"], k["D"], k["E"], k["F"], k["NB"]
    KT, ST, FT, ROW, TK = k["KT"], k["ST"], k["FT"], k["ROW"], k["topk"]
    SLOT_LO, SLOT_HI = k["SLOT_LO"], k["SLOT_HI"]
    ident, logits = k["ident"], k["logits"]
    rows_dram, rows_blk, gate_dram, slots_dram, out_rows = k["rows_dram"], k["rows_blk"], k["gate_dram"], k["slots_dram"], k["out_rows"]
    w1, b1, w2, b2 = k["w1"], k["b1"], k["w2"], k["b2"]
    EB = E * NB
    TOP_BIT = 29
    NOWHERE = 4096.0
    LO_BITS = SLOT_LO.bit_length() - 1
    assert TK % PART == 0 and SLOT_HI * SLOT_LO == TK and SLOT_HI <= PART and 2 * TK < NOWHERE

    with ExitStack() as ctx:
        def sb(name, shape, dt):
            return ctx.enter_context(nc.sbuf_tensor(name, shape, dt))

        def ps(name, shape):
            return ctx.enter_context(nc.psum_tensor(name, shape, F32))

        def sem(name):
            return ctx.enter_context(nc.semaphore(name))

        token_max = sb("token_max", [PART, NB], F32)
        token_sum = sb("token_sum", [PART, NB], F32)
        scores = sb("scores", [PART, E, NB], F32)
        ones_bf = sb("ones_bf", [PART, PART], BF16)
        before_bf = sb("before_bf", [PART, PART], BF16)
        thr = sb("thr", [PART, E], I32)
        cand = sb("cand", [PART, E], I32)
        bit = sb("bit", [PART, E], I32)
        flag = sb("flag", [PART, E], I32)
        cnt = sb("cnt", [PART, E], F32)
        mask = sb("mask", [PART, 2, E, NB], BF16)
        tot = sb("tot", [PART, 2, EB], F32)
        incl = sb("incl", [PART, 2, EB], F32)
        carry = sb("carry", [PART, E, NB], F32)
        need = sb("need", [PART, E], F32)
        place = sb("place", [PART, EB], F32)
        take = sb("take", [PART, EB], F32)
        place_i = sb("place_i", [PART, EB], I32)
        part_i = sb("part_i", [PART, EB], I32)
        place_hi = sb("place_hi", [PART, EB], BF16)
        place_lo = sb("place_lo", [PART, EB], BF16)
        iota_i = sb("iota_i", [PART, NB + SLOT_LO], I32)
        iota_bf = sb("iota_bf", [PART, NB + SLOT_LO], BF16)
        row_i = sb("row_i", [PART, 1], I32)
        row_f = sb("row_f", [PART, 1], F32)
        hot_hi = sb("hot_hi", [PART, NB, SLOT_HI], BF16)
        hot_lo = sb("hot_lo", [PART, NB, SLOT_LO], BF16)
        hot_id = sb("hot_id", [PART, NB, 2, SLOT_LO], BF16)
        id_f = sb("id_f", [SLOT_HI, 2, SLOT_LO], F32)
        id_i = sb("id_i", [SLOT_HI, SLOT_LO], U32)
        slots = [sb(f"slots{u}", [PART, ST], U32) for u in range(2)]
        slot_batch = [sb(f"slot_batch{u}", [PART, ST], U32) for u in range(2)]
        w1_sb = [sb(f"w1_sb{u}", [PART, KT, F], F32) for u in range(2)]
        w2_sb = [sb(f"w2_sb{u}", [PART, FT, D], F32) for u in range(2)]
        b1_sb = [sb(f"b1_sb{u}", [PART, FT], F32) for u in range(2)]
        b2_sb = [sb(f"b2_sb{u}", [PART, D], F32) for u in range(2)]
        rows = [sb(f"rows{u}", [PART, ST, ROW], F32) for u in range(2)]
        gates = [sb(f"gates{u}", [PART, ST, D], F32) for u in range(2)]
        weight = [sb(f"weight{u}", [PART, ST], F32) for u in range(2)]
        rows_tr = sb("rows_tr", [PART, KT, TK], F32)
        hid = sb("hid", [PART, FT, TK], F32)
        contrib = [sb(f"contrib{u}", [PART, ST, D], F32) for u in range(2)]

        a_ps = [ps(f"a_ps{i}", [PART, HALF]) for i in range(4)]
        y_ps = [ps(f"y_ps{i}", [PART, HALF]) for i in range(2)]
        c_ps = ps("c_ps", [PART, HALF])

        rt = sem("rt")
        sm_exp = sem("sm_exp")
        sc_ok = sem("sc_ok")
        sc_st = sem("sc_st")
        cst = sem("cst")
        bs = sem("bs")
        cnt_in = sem("cnt_in")
        cnt_mm = sem("cnt_mm")
        mask_ok = sem("mask_ok")
        rank_mm = sem("rank_mm")
        hot = sem("hot")
        hot_ok = sem("hot_ok")
        id_mm = sem("id_mm")
        id_cp = sem("id_cp")
        id_ok = sem("id_ok")
        id_st = sem("id_st")
        id_ld = [sem(f"id_ld{u}") for u in range(2)]
        sb_ok = sem("sb_ok")
        w_ld = [sem(f"w_ld{u}") for u in range(2)]
        got = [sem(f"got{u}") for u in range(2)]
        g_cp = sem("g_cp")
        rt_mm = sem("rt_mm")
        rt_ev = sem("rt_ev")
        hid_mm = sem("hid_mm")
        hid_ok = sem("hid_ok")
        y_mm = sem("y_mm")
        y_b = sem("y_b")
        y_ok = sem("y_ok")
        added = sem("added")

        STEP_BS, STEP_HOT, W_DMAS = 5, 3, 4
        block = ctx.enter_context(nc.Block())

        @block.sync
        def _(sp):
            def load_weights(e, u):
                sp.dma_start(w1_sb[u][:], w1[bass.ds(e, 1)].rearrange("o (t p) f -> p (o t) f", p=PART)).then_inc(w_ld[u], 16)
                sp.dma_start(w2_sb[u][:], w2[bass.ds(e, 1)].rearrange("o (t p) d -> p (o t) d", p=PART)).then_inc(w_ld[u], 16)
                sp.dma_start(b1_sb[u][:], b1[bass.ds(e, 1)].rearrange("o (t p) -> p (o t)", p=PART),
                             allow_slow_non_contiguous=True).then_inc(w_ld[u], 16)
                sp.dma_start(b2_sb[u][:], b2[bass.ds(e, 1)].rearrange("o d -> (o d)").partition_broadcast(PART)).then_inc(w_ld[u], 16)

            load_weights(0, 0)
            load_weights(1, 1)
            sp.wait_ge(sc_ok, 1)
            sp.dma_start(rows_blk[:, :, D:D + E], logits[:]).then_inc(sc_st, 16)
            with sp.Fori(0, E) as e:
                sp.wait_ge(id_ok, e + 1)
                sp.dma_start(slots_dram[bass.ds(e, 1)].rearrange("o (h l) -> (o h) l", l=SLOT_LO), id_i[:]).then_inc(id_st, 16)

            def load_slots(e, u):
                sp.dma_start(slots[u][:], slots_dram[bass.ds(e, 1)].rearrange("o (s p) -> p (o s)", p=PART),
                             allow_slow_non_contiguous=True).then_inc(id_ld[u], 16)

            sp.wait_ge(id_st, 16 * E + 1)
            load_slots(0, 0)
            load_slots(1, 1)
            with sp.Fori(0, E // 2 - 1) as ep:
                for u in range(2):
                    sp.wait_ge(y_ok, (ep * 2 + u + 1) * ST)
                    load_weights(ep * 2 + u + 2, u)
                    sp.wait_ge(added, (ep * 2 + u + 1) * (16 * ST))
                    load_slots(ep * 2 + u + 2, u)
            sp.wait_ge(sc_st, 16)

        @block.gpsimd
        def _(pool):
            nc.gpsimd.iota(iota_i[:, 0:NB], [[1, NB]], base=0, channel_multiplier=0).then_inc(cst, 1)
            nc.gpsimd.iota(iota_i[:, NB:], [[1, SLOT_LO]], base=0, channel_multiplier=0).then_inc(cst, 1)
            nc.gpsimd.iota(row_i[:], [[0, 1]], base=0, channel_multiplier=1).then_inc(cst, 1)
            nc.gpsimd.memset(ones_bf[:], 1.0).then_inc(cst, 1)
            pool.wait_ge(cst, 4)
            nc.gpsimd.affine_select(out=before_bf[:], in_=ones_bf[:], compare_op=ALU.is_gt, fill=0.0, base=0,
                                    pattern=[[1, PART]], channel_multiplier=-1).then_inc(cst, 1)

            def gather(e, u):
                for s in range(ST):
                    nc.gpsimd.indirect_dma_start(
                        out=rows[u][:, s, :], out_offset=None, in_=rows_dram,
                        in_offset=bass.IndirectOffsetOnAxis(ap=slots[u][:, s:s + 1], axis=0)).then_inc(got[u], 16)
                    nc.gpsimd.indirect_dma_start(
                        out=gates[u][:, s, :], out_offset=None, in_=gate_dram,
                        in_offset=bass.IndirectOffsetOnAxis(ap=slot_batch[u][:, s:s + 1], axis=0)).then_inc(got[u], 16)

            def scatter(e, u):
                for s in range(ST):
                    pool.wait_ge(y_ok, e * ST + s + 1)
                    nc.gpsimd.indirect_dma_start(
                        out=out_rows, out_offset=bass.IndirectOffsetOnAxis(ap=slots[u][:, s:s + 1], axis=0),
                        in_=contrib[u][:, s, :], in_offset=None, compute_op=ALU.add).then_inc(added, 16)
                pool.wait_ge(added, (e + 1) * (16 * ST))

            pool.wait_ge(sc_st, 16)
            pool.wait_ge(sb_ok, 2)
            gather(0, 0)
            gather(1, 1)
            for e in range(E):
                scatter(e, e % 2)
                if e + 2 < E:
                    pool.wait_ge(sb_ok, e + 3)
                    gather(e + 2, e % 2)

        @block.scalar
        def _(act):
            act.wait_ge(rt, 2)
            nc.scalar.activation(logits[:], logits[:], ACT.Exp).then_inc(sm_exp, 1)
            with act.Fori(0, E // 2) as ep:
                for u in range(2):
                    e = ep * 2 + u
                    for t in range(KT):
                        act.wait_ge(rt_mm, e * KT + t + 1)
                        nc.scalar.activation(rows_tr[:, t, :], a_ps[t][:, 0:TK], ACT.Copy).then_inc(rt_ev, 1)
                    for f in range(FT):
                        act.wait_ge(hid_mm, e * FT + f + 1)
                        nc.scalar.activation(hid[:, f, :], a_ps[f % 4][:, 0:TK], ACT.Relu, bias=b1_sb[u][:, f:f + 1]).then_inc(hid_ok, 1)

        @block.vector
        def _(dve):
            n_rt = [0]

            def step(ins, wait=True):
                ins.then_inc(rt, 1)
                n_rt[0] += 1
                if wait:
                    dve.wait_ge(rt, n_rt[0])

            dve.sem_inc(rt_ev, 1)
            dve.sem_inc(hid_ok, 1)
            dve.sem_inc(y_b, 2)
            dve.sem_inc(id_st, 1)
            step(nc.vector.tensor_reduce(token_max[:], logits[:], AX.X, ALU.max))
            step(nc.vector.tensor_tensor(logits[:], logits[:], token_max[:].unsqueeze(2).to_broadcast([PART, NB, E]), ALU.subtract), False)
            dve.wait_ge(sm_exp, 1)
            step(nc.vector.tensor_reduce(token_sum[:], logits[:], AX.X, ALU.add))
            step(nc.vector.reciprocal(token_sum[:], token_sum[:]))
            nc.vector.tensor_tensor(logits[:], logits[:], token_sum[:].unsqueeze(2).to_broadcast([PART, NB, E]), ALU.mult).then_inc(sc_ok, 1)
            dve.wait_ge(sc_ok, 1)
            step(nc.vector.tensor_copy(scores[:], logits[:].rearrange("p n e -> p e n")), False)
            dve.wait_ge(cst, 5)
            step(nc.vector.tensor_copy(iota_bf[:], iota_i[:]), False)
            step(nc.vector.tensor_copy(row_f[:], row_i[:]), False)
            step(nc.vector.memset(carry[:], 1.0))
            step(nc.vector.memset(carry[:, :, 0:1], 0.0), False)
            step(nc.vector.memset(thr[:], 0), False)
            step(nc.vector.memset(bit[:], 1 << TOP_BIT), False)
            step(nc.vector.memset(cand[:], 1 << TOP_BIT))

            with dve.Fori(0, TOP_BIT + 1) as i:
                nc.vector.tensor_tensor(mask[:, 0], scores[:], cand[:].bitcast(F32).unsqueeze(2).to_broadcast([PART, E, NB]),
                                        ALU.is_ge).then_inc(cnt_in, 1)
                dve.wait_ge(cnt_mm, i + 1)
                nc.vector.tensor_reduce(cnt[:], c_ps[:, 0:EB].rearrange("p (e n) -> p e n", n=NB), AX.X, ALU.add).then_inc(bs, 1)
                dve.wait_ge(bs, i * STEP_BS + 1)
                nc.vector.tensor_scalar(flag[:], cnt[:], float(TK), None, ALU.is_ge).then_inc(bs, 1)
                dve.wait_ge(bs, i * STEP_BS + 2)
                nc.vector.tensor_scalar(bit[:], bit[:], 1, None, ALU.logical_shift_right).then_inc(bs, 1)
                nc.vector.copy_predicated(thr[:], flag[:], cand[:]).then_inc(bs, 1)
                dve.wait_ge(bs, i * STEP_BS + 4)
                nc.vector.tensor_tensor(cand[:], thr[:], bit[:], ALU.bitwise_or).then_inc(bs, 1)
                dve.wait_ge(bs, i * STEP_BS + 5)

            thr_bc = thr[:].bitcast(F32).unsqueeze(2).to_broadcast([PART, E, NB])
            nc.vector.tensor_tensor(mask[:, 0], scores[:], thr_bc, ALU.is_gt).then_inc(mask_ok, 1)
            nc.vector.tensor_tensor(mask[:, 1], scores[:], thr_bc, ALU.is_equal).then_inc(mask_ok, 1)
            dve.wait_ge(rank_mm, 1)
            carry_f = carry[:].rearrange("p e n -> p (e n)")
            for m in range(2):
                step(nc.vector.tensor_copy(tot[:, m], a_ps[2 + m][:, 0:EB]), m == 1)
            for m in range(2):
                step(nc.vector.tensor_tensor_scan(incl[:, m], carry_f, tot[:, m], 0.0, ALU.mult, ALU.add), m == 1)
            step(nc.vector.tensor_scalar(need[:], incl[:, 0].rearrange("p (e n) -> p e n", n=NB)[:, :, NB - 1], -1.0, float(TK), ALU.mult, ALU.add), False)
            step(nc.vector.tensor_tensor(tot[:], incl[:], tot[:], ALU.subtract))
            for m in range(2):
                step(nc.vector.tensor_tensor(tot[:, m], tot[:, m], a_ps[m][:, 0:EB], ALU.add), m == 1)
            need_bc = need[:].unsqueeze(2).to_broadcast([PART, E, NB])

            def by_expert(ap):
                return ap.rearrange("p (e n) -> p e n", n=NB)

            step(nc.vector.tensor_tensor(by_expert(place[:]), by_expert(tot[:, 1]), need_bc, ALU.min), False)
            step(nc.vector.tensor_tensor(by_expert(take[:]), by_expert(tot[:, 1]), need_bc, ALU.is_lt))
            step(nc.vector.tensor_tensor(place[:], place[:], tot[:, 0], ALU.add), False)
            step(nc.vector.tensor_tensor(take[:], take[:], mask[:, 1].rearrange("p e n -> p (e n)"), ALU.mult))
            step(nc.vector.tensor_tensor(take[:], take[:], mask[:, 0].rearrange("p e n -> p (e n)"), ALU.add))
            step(nc.vector.scalar_tensor_tensor(out=place[:], in0=take[:], scalar=-NOWHERE, in1=place[:], op0=ALU.mult, op1=ALU.add))
            step(nc.vector.tensor_scalar(place_i[:], place[:], NOWHERE, None, ALU.add))
            step(nc.vector.tensor_scalar(part_i[:], place_i[:], LO_BITS, None, ALU.logical_shift_right))
            step(nc.vector.tensor_copy(place_hi[:], part_i[:]))
            step(nc.vector.tensor_scalar(part_i[:], place_i[:], SLOT_LO - 1, None, ALU.bitwise_and))
            step(nc.vector.tensor_copy(place_lo[:], part_i[:]))

            with dve.Fori(0, E) as e:
                hi_e = place_hi[:, bass.ds(e * NB, NB)].unsqueeze(2).to_broadcast([PART, NB, SLOT_HI])
                lo_e = place_lo[:, bass.ds(e * NB, NB)].unsqueeze(2).to_broadcast([PART, NB, SLOT_LO])
                nc.vector.tensor_tensor(hot_hi[:], hi_e, iota_bf[:, NB:NB + SLOT_HI].unsqueeze(1).to_broadcast([PART, NB, SLOT_HI]),
                                        ALU.is_equal).then_inc(hot, 1)
                nc.vector.tensor_tensor(hot_lo[:], lo_e, iota_bf[:, NB:NB + SLOT_LO].unsqueeze(1).to_broadcast([PART, NB, SLOT_LO]),
                                        ALU.is_equal).then_inc(hot, 1)
                dve.wait_ge(hot, e * STEP_HOT + 2)
                nc.vector.tensor_tensor(hot_id[:, :, 0, :], hot_lo[:], iota_bf[:, 0:NB].unsqueeze(2).to_broadcast([PART, NB, SLOT_LO]),
                                        ALU.mult).then_inc(hot, 1)
                nc.vector.tensor_scalar(hot_id[:, :, 1, :], hot_lo[:], row_f[:, 0:1], None, ALU.mult).then_inc(hot_ok, 1)
                dve.wait_ge(id_mm, e + 1)
                nc.vector.tensor_copy(id_f[:], c_ps[0:SLOT_HI, 0:2 * SLOT_LO].rearrange("p (m l) -> p m l", m=2)).then_inc(id_cp, 1)
                dve.wait_ge(id_cp, e + 1)
                dve.wait_ge(id_st, e * 16 + 1)
                nc.vector.scalar_tensor_tensor(out=id_i[:], in0=id_f[:, 0], scalar=float(PART), in1=id_f[:, 1],
                                               op0=ALU.mult, op1=ALU.add).then_inc(id_ok, 1)

            def batch_of_slots(n, u):
                dve.wait_ge(id_ld[u], n * 16 + 16)
                nc.vector.tensor_scalar(slot_batch[u][:], slots[u][:], P.bit_length() - 1, None, ALU.logical_shift_right).then_inc(sb_ok, 1)

            batch_of_slots(0, 0)
            batch_of_slots(0, 1)

            def experts(ep, more):
                for u in range(2):
                    e = ep * 2 + u
                    dve.wait_ge(got[u], (ep + 1) * (32 * ST))
                    nc.vector.tensor_copy(weight[u][:], rows[u][:, :, bass.ds(e + D, 1)].rearrange("p s o -> p (s o)")).then_inc(g_cp, 1)
                    dve.wait_ge(g_cp, e + 1)
                    for s in range(ST):
                        n = e * ST + s
                        dve.wait_ge(y_mm, n + 1)
                        nc.vector.tensor_tensor(contrib[u][:, s, :], y_ps[s % 2][:, 0:D], b2_sb[u][:], ALU.add).then_inc(y_b, 1)
                        dve.wait_ge(y_b, n + 3)
                        nc.vector.scalar_tensor_tensor(out=contrib[u][:, s, :], in0=contrib[u][:, s, :], scalar=weight[u][:, s:s + 1],
                                                       in1=gates[u][:, s, :], op0=ALU.mult, op1=ALU.mult).then_inc(y_ok, 1)
                    if more:
                        batch_of_slots(ep + 1, u)

            with dve.Fori(0, E // 2 - 1) as ep:
                experts(ep, True)
            experts(E // 2 - 1, False)

        @block.tensor
        def _(pe):
            pe.wait_ge(cst, 5)
            with pe.Fori(0, TOP_BIT + 1) as i:
                pe.wait_ge(cnt_in, i + 1)
                nc.tensor.matmul(c_ps[:, 0:EB], ones_bf[:], mask[:, 0].rearrange("p e n -> p (e n)"), start=True, stop=True).then_inc(cnt_mm, 1)
            pe.wait_ge(mask_ok, 2)
            for m in range(2):
                src = mask[:, m].rearrange("p e n -> p (e n)")
                nc.tensor.matmul(a_ps[m][:, 0:EB], before_bf[:], src, start=True, stop=True)
                mm = nc.tensor.matmul(a_ps[2 + m][:, 0:EB], ones_bf[:], src, start=True, stop=True)
            mm.then_inc(rank_mm, 1)
            with pe.Fori(0, E) as e:
                pe.wait_ge(hot_ok, e + 1)
                for n in range(NB):
                    mm = nc.tensor.matmul(c_ps[0:SLOT_HI, 0:2 * SLOT_LO], hot_hi[:, n, :], hot_id[:, n].rearrange("p m l -> p (m l)"),
                                          start=(n == 0), stop=(n == NB - 1))
                mm.then_inc(id_mm, 1)

            with pe.Fori(0, E // 2) as ep:
                for u in range(2):
                    e = ep * 2 + u
                    pe.wait_ge(got[u], (ep + 1) * (32 * ST))
                    pe.wait_ge(hid_ok, e * FT + 1)
                    for t in range(KT):
                        for s in range(ST):
                            mm = nc.tensor.transpose(a_ps[t][:, s * PART:(s + 1) * PART], rows[u][:, s, t * PART:(t + 1) * PART], ident[:])
                        mm.then_inc(rt_mm, 1)
                    pe.wait_ge(w_ld[u], (ep + 1) * (16 * W_DMAS))
                    pe.wait_ge(rt_ev, e * KT + KT + 1)
                    for f in range(FT):
                        if f >= 4:
                            pe.wait_ge(hid_ok, e * FT + f - 4 + 2)
                        for t in range(KT):
                            mm = nc.tensor.matmul(a_ps[f % 4][:, 0:TK], w1_sb[u][:, t, f * PART:(f + 1) * PART], rows_tr[:, t, :],
                                                  start=(t == 0), stop=(t == KT - 1))
                        mm.then_inc(hid_mm, 1)
                    pe.wait_ge(hid_ok, e * FT + FT + 1)
                    for s in range(ST):
                        pe.wait_ge(y_b, e * ST + s + 1)
                        for f in range(FT):
                            mm = nc.tensor.matmul(y_ps[s % 2][:, 0:D], hid[:, f, s * PART:(s + 1) * PART], w2_sb[u][:, f, :],
                                                  start=(f == 0), stop=(f == FT - 1))
                        mm.then_inc(y_mm, 1)


_INS = ['L0_attn_inputs', 'L0_attn_w_qkv', 'L0_attn_w_o', 'L0_ffn_router_w', 'L0_ffn_router_b', 'L0_ffn_w1', 'L0_ffn_b1', 'L0_ffn_w2', 'L0_ffn_b2', 'L0_c', 'L0_wmod']
TOPK = 512


def kernel(**inputs):
    import numpy as _np
    import concourse.bacc as _bacc
    from concourse import mybir as _mybir
    from concourse.bass_utils import run_bass_kernel_spmd as _run

    nc = _bacc.Bacc("TRN2", target_bir_lowering=False, num_devices=1)
    arrays, args = {}, []
    for name in _INS:
        a = _np.ascontiguousarray(inputs[name])
        arrays[f"in_{name}_dram"] = a
        args.append(nc.dram_tensor(f"in_{name}_dram", a.shape, _mybir.dt.from_np(a.dtype), kind="ExternalInput").ap())
    shape = tuple(inputs['L0_attn_inputs'].shape)
    out = nc.dram_tensor("out_0_dram", shape, _mybir.dt.from_np(_np.dtype('float32')), kind="ExternalOutput").ap()
    build_kernel(nc, *args, out, TOPK)
    r = _run(nc, [arrays], core_ids=[0])
    return r.results[0]["out_0_dram"]
```

```python
from contextlib import ExitStack

import concourse.bass as bass
from concourse import mybir

F32 = mybir.dt.float32
F32R = mybir.dt.float32r
BF16 = mybir.dt.bfloat16
F16 = mybir.dt.float16
I32 = mybir.dt.int32
U32 = mybir.dt.uint32
ALU = mybir.AluOpType
ACT = mybir.ActivationFunctionType
AX = mybir.AxisListType

LN_EPS = 1e-5
GATE_FLOOR = 0.25
PART = 128
HALF = 512

LOW_ON_DVE = (0, 7)
LOW_ON_POOL = (1, 2, 3, 4, 5, 6)
LAST_ON_DVE = (0, 2, 4, 5, 7)
LAST_ON_POOL = (1, 3, 6)
MAX_BEFORE = {4: 2, 5: 3, 6: 5, 7: 7}
MAX_AFTER = {2: 0, 3: 1, 5: 4, 6: 6}

NORM_TURN_AT = {4: (0, 1), 6: (2, 3)}
PROJECT_AT = {1: 0, 4: 1}
FIRST_MAX_AT = {8: 0, 9: 1, 10: 2, 11: 3, 12: 4, 13: 5, 14: 6, 15: 7}
TURN_AT = {9: 0, 10: 1, 11: 2, 12: 3}
LOGITS_AT = 14


def count_upto(tiles, j):
    return sum(1 for t in tiles if t <= j)


def build_kernel(nc, x, w_qkv, w_o, router_w, router_b, w1, b1, w2, b2, c, wmod, out, topk):
    B, P, D = x.shape
    H, _, _, N = w_qkv.shape
    E, _, F = w1.shape
    NQ = P // PART
    KT = D // PART
    HT = H * N // PART
    NB = B * P // PART
    SCALE = float(N) ** -0.5
    VW = 3 * (N + 1)
    VHI = 3 * N + 2
    VLO = 2 * N + 1
    ST = topk // PART
    FT = F // PART
    ROW = D + E
    SLOT_LO = 32
    SLOT_HI = topk // SLOT_LO
    assert NQ == 8 and KT == 2 and N == 64 and D == 256 and E == 8 and HALF == E * N

    x_t = x.rearrange("b (q p) d -> b p q d", p=PART)
    out_t = out.rearrange("b (q p) d -> b p q d", p=PART)
    out_rows = out.rearrange("b p d -> (b p) d")
    rows_dram = nc.dram_tensor("rows_dram", (B * P, ROW), F32, kind="Internal").ap()
    rows_t = rows_dram.rearrange("(b q p) r -> b p q r", p=PART, q=NQ)
    rows_blk = rows_dram.rearrange("(n p) r -> p n r", p=PART)
    mods_dram = nc.dram_tensor("mods_dram", (B, 4 * D), F32, kind="Internal").ap()
    gate_dram = nc.dram_tensor("gate_dram", (B, D), F32, kind="Internal").ap()
    slots_dram = nc.dram_tensor("slots_dram", (E, topk), U32, kind="Internal").ap()

    with ExitStack() as outer:
        def keep(name, shape, dt):
            return outer.enter_context(nc.sbuf_tensor(name, shape, dt))

        ident = keep("ident", [PART, PART], F32)
        ident_bf = keep("ident_bf", [PART, PART], BF16)
        logits = keep("logits", [PART, NB, E], F32)
        minus_half = keep("minus_half", [PART, NQ], F32)

        attention_phase(nc, locals())
        ffn_phase(nc, locals())


def attention_phase(nc, k):
    B, P, D, H, N, E = k["B"], k["P"], k["D"], k["H"], k["N"], k["E"]
    NQ, KT, HT, SCALE, VW, VHI, VLO = k["NQ"], k["KT"], k["HT"], k["SCALE"], k["VW"], k["VHI"], k["VLO"]
    ident, ident_bf, logits, minus_half = k["ident"], k["ident_bf"], k["logits"], k["minus_half"]
    x_t, out_t, rows_t, mods_dram, gate_dram = k["x_t"], k["out_t"], k["rows_t"], k["mods_dram"], k["gate_dram"]
    w_qkv, w_o, router_w, router_b, c, wmod = k["w_qkv"], k["w_o"], k["router_w"], k["router_b"], k["c"], k["wmod"]
    HG = HALF // N
    NG = H // HG
    LD, LP = len(LOW_ON_DVE), len(LOW_ON_POOL)
    BD, BP = (H - 1) * LD + len(LAST_ON_DVE), (H - 1) * LP + len(LAST_ON_POOL)
    NV = NQ * NG
    V_BUFS = 4
    assert NV == 16

    with ExitStack() as ctx:
        def sb(name, shape, dt):
            return ctx.enter_context(nc.sbuf_tensor(name, shape, dt))

        def ps(name, shape):
            return ctx.enter_context(nc.psum_tensor(name, shape, F32))

        def sem(name):
            return ctx.enter_context(nc.semaphore(name))

        silu_t = sb("silu_t", [PART, KT, B], F32)
        sig_t = sb("sig_t", [PART, KT, B], F32)
        c_t = sb("c_t", [PART, KT, B], F32)
        mod_t = sb("mod_t", [PART, 2 * KT, B], F32)
        mod_b = sb("mod_b", [PART, 2 * KT], F32)
        stats = sb("stats", [PART, NQ, 6], F32)
        mean = sb("mean", [PART, NQ], F32)
        mean_d = sb("mean_d", [PART, NQ], F32)
        var_eps = sb("var_eps", [PART, NQ], F32)
        rstd = sb("rstd", [PART, NQ], F32)
        h_t = sb("h_t", [PART, KT, P], F32)
        rw_sb = sb("rw_sb", [PART, KT, E], F32)
        rb_bc = sb("rb_bc", [PART, E], F32)
        wqk = [sb(f"wqk{u}", [PART, KT, 2, N], F32) for u in range(2)]
        q_hh = [sb(f"q_hh{u}", [PART, P], F32R) for u in range(2)]
        q_lc = [sb(f"q_lc{u}", [PART, P], F32R) for u in range(2)]
        k_hl = [sb(f"k_hl{u}", [PART, P], F32R) for u in range(2)]
        k_h1 = [sb(f"k_h1{u}", [PART, P], F32R) for u in range(2)]
        row_max = sb("row_max", [PART, NQ, 2], F32)
        neg_max = sb("neg_max", [PART, NQ], BF16)
        prob = sb("prob", [PART, 4, P], F32)
        p_hi = [sb(f"p_hi{u}", [PART, NQ, P], F16) for u in range(2)]
        p_lo = [sb(f"p_lo{u}", [PART, NQ, P], F16) for u in range(2)]
        v_all = sb("v_all", [PART, NQ, H, VW], BF16)
        pv_sum = sb("pv_sum", [PART, 2, 2, N], F32)
        pv_inv = sb("pv_inv", [PART, 2, 2], F32)
        heads = sb("heads", [PART, NQ, H * N], F32)

        def view(tensor, first, n):
            return tensor[:].rearrange("p q k -> p (q k)")[:, 2 * first:2 * (first + n)].bitcast(F32)

        x_sb = view(p_hi[0], 0, NQ * D).rearrange("p (q d) -> p q d", q=NQ)
        norm = view(p_hi[0], NQ * D, NQ * D).rearrange("p (q d) -> p q d", q=NQ)
        wv_sb = view(p_hi[1], 0, KT * H * N).rearrange("p (t h n) -> p t h n", t=KT, h=H)
        prob_flat = prob[:].rearrange("p j k -> p (j k)")
        mod_rows = prob_flat[:, 0:3 * D].rearrange("p (m d) -> p m d", m=3)
        v_rest = prob_flat[:, P:P + V_BUFS * HALF].rearrange("p (u n) -> p u n", u=V_BUFS)
        wo_sb = view(p_lo[0], 0, HT * D).rearrange("p (t d) -> p t d", t=HT)
        heads_t = [view(p_lo[0], HT * (D + u * PART), HT * PART).rearrange("p (t n) -> p t n", t=HT) for u in range(2)]
        h2_t = view(p_lo[0], 0, KT * P).rearrange("p (t n) -> p t n", t=KT)
        x1_sb = view(p_lo[1], 0, NQ * D).rearrange("p (q d) -> p q d", q=NQ)
        h2_sb = view(p_lo[1], NQ * D, NQ * D).rearrange("p (q d) -> p q d", q=NQ)
        wmod_sb = view(p_lo[1], 0, KT * 6 * D).rearrange("p (t m) -> p t m", t=KT)
        mods = view(p_lo[1], KT * 6 * D, 4 * D).rearrange("p (m d) -> p m d", m=4)[0:B]
        mods_s = prob[0:B, 0, 0:4 * D].rearrange("p (m d) -> p m d", m=4)

        st_ps = [ps(f"st_ps{u}", [PART, P]) for u in range(2)]
        max_ps = ps("max_ps", [PART, P])
        pv_ps = ps("pv_ps", [PART, HALF])
        ms_ps = ps("ms_ps", [PART, HALF])

        const_ld = sem("const_ld")
        ident_z = sem("ident_z")
        ident_ok = sem("ident_ok")
        fill_ok = sem("fill_ok")
        c_exp = sem("c_exp")
        c_silu = sem("c_silu")
        mod_mm = sem("mod_mm")
        mod_ok = sem("mod_ok")
        x_ld = sem("x_ld")
        x_again = sem("x_again")
        ln1 = sem("ln1")
        ln1_in = sem("ln1_in")
        ln1_pow = sem("ln1_pow")
        norm_ok = sem("norm_ok")
        mod_b_ok = sem("mod_b_ok")
        ht_in_mm = sem("ht_in_mm")
        ht_in_ev = sem("ht_in_ev")
        ln2 = sem("ln2")
        ln2_in = sem("ln2_in")
        ln2_pow = sem("ln2_pow")
        h2t_mm = sem("h2t_mm")
        h2t_ev = sem("h2t_ev")
        v_mm = sem("v_mm")
        v1_ok = sem("v1_ok")
        v_sub = sem("v_sub")
        v2_ok = sem("v2_ok")
        v3_ok = sem("v3_ok")
        wqk_ld = [sem(f"wqk_ld{u}") for u in range(2)]
        proj_mm = sem("proj_mm")
        high_ok = sem("high_ok")
        low_ok = sem("low_ok")
        dup_ok = [sem(f"dup_ok{u}") for u in range(2)]
        max_mm = sem("max_mm")
        max_red = sem("max_red")
        neg_ok = sem("neg_ok")
        crow_mm = sem("crow_mm")
        crow_ok = sem("crow_ok")
        st_mm = sem("st_mm")
        exp_ok = sem("exp_ok")
        phi_ok = sem("phi_ok")
        plo_dve = sem("plo_dve")
        plo_pool = sem("plo_pool")
        pv_mm = sem("pv_mm")
        pv_red = sem("pv_red")
        pv_ev = sem("pv_ev")
        head_ok = sem("head_ok")
        ht_mm = sem("ht_mm")
        ht_ev = sem("ht_ev")
        o_mm = sem("o_mm")
        gated = sem("gated")
        x1_ok = sem("x1_ok")
        h2_scaled = sem("h2_scaled")
        h2_ok = sem("h2_ok")
        lg_mm = sem("lg_mm")
        lg_ok = sem("lg_ok")
        st_rows = sem("st_rows")

        EXP_CREDIT, PV_CREDIT, VSUB_CREDIT, V3_CREDIT, HEAD_CREDIT = 2, 5, 4, V_BUFS, 2
        RED_CREDIT = 2
        LN1_STEPS, LN2_STEPS = NQ + 6, NQ + 6
        N_CONST = 5

        wv_ld = sem("wv_ld")
        wo_ld = sem("wo_ld")
        mods_st = sem("mods_st")
        mods_ld = sem("mods_ld")
        x1_row = sem("x1_row")

        block = ctx.enter_context(nc.Block())

        def run_heads(eng, head):
            head(0, 0, True)
            head(1, 1, False)
            with eng.Fori(1, H // 2 - 1) as hp:
                head(hp * 2, 0, False)
                head(hp * 2 + 1, 1, False)
            head(H - 2, 0, False)
            head(H - 1, 1, False)

        def is_at(t, n):
            return isinstance(t, int) and t == n

        def lows_of(t):
            return (LAST_ON_DVE, LAST_ON_POOL) if is_at(t, H - 1) else (LOW_ON_DVE, LOW_ON_POOL)

        def pair_dmas(b, t, u):
            return b * (H * 16) + (t - u) * 16 + 32

        def tile_cols(j):
            return slice(j * PART, (j + 1) * PART)

        def half_cols(h):
            return slice(h * HALF, (h + 1) * HALF)

        @block.sync
        def _(sp):
            for t in range(KT):
                sp.dma_start(c_t[:, t, :], c[:, t * PART:(t + 1) * PART].rearrange("b p -> p b"),
                             allow_slow_non_contiguous=True).then_inc(const_ld, 16)
            sp.dma_start(wmod_sb[:], wmod.rearrange("(t p) m -> p t m", p=PART)).then_inc(const_ld, 16)
            sp.dma_start(rw_sb[:], router_w.rearrange("(t p) e -> p t e", p=PART)).then_inc(const_ld, 16)
            sp.dma_start(rb_bc[:], router_b.partition_broadcast(PART)).then_inc(const_ld, 16)

            def load_wv():
                for t in range(KT):
                    sp.dma_start(wv_sb[:, t], w_qkv[:, 2, t * PART:(t + 1) * PART, :].rearrange("h p n -> p h n")).then_inc(wv_ld, 16)

            def load_wqk(t, u):
                for a in range(2):
                    sp.dma_start(wqk[u][:, :, a, :],
                                 w_qkv[bass.ds(t, 1), a].rearrange("o (t p) n -> p (o t) n", p=PART)).then_inc(wqk_ld[u], 16)

            def load_x(b):
                sp.dma_start(x_sb, x_t[bass.ds(b, 1)].rearrange("o p q d -> p (o q) d")).then_inc(x_ld, 16)

            def head(b, t, u, nxt):
                g = b * H + t
                if nxt is not None:
                    sp.wait_ge(proj_mm, g * 2 + 1)
                    load_wqk(nxt, 1 - u)
                sp.wait_ge(high_ok, g * 4 + 4)
                sp.dma_start(q_hh[u][N:2 * N, :].bitcast(F32), q_hh[u][0:N, :].bitcast(F32)).then_inc(dup_ok[u], 16)
                sp.dma_start(k_h1[u][0:N, :].bitcast(F32), k_hl[u][0:N, :].bitcast(F32)).then_inc(dup_ok[u], 16)

            def other_heads(b, more):
                head(b, 1, 1, 2)
                with sp.Fori(1, H // 2 - 1) as hp:
                    head(b, hp * 2, 0, hp * 2 + 1)
                    head(b, hp * 2 + 1, 1, hp * 2 + 2)
                head(b, H - 2, 0, H - 1)
                head(b, H - 1, 1, 0 if more else None)

            def boundary(b, more):
                sp.wait_ge(pv_mm, (b + 1) * (H * 4) - 4 + PV_CREDIT)
                if more:
                    load_x(b + 1)
                sp.dma_start(wo_sb, w_o.rearrange("(t p) d -> p t d", p=PART)).then_inc(wo_ld, 16)
                sp.wait_ge(pv_mm, (b + 1) * (H * 4) - 3 + PV_CREDIT)
                sp.dma_start(mod_rows.rearrange("p m d -> p (m d)"),
                             mods_dram[bass.ds(b, 1), 0:3 * D].rearrange("o m -> (o m)").partition_broadcast(PART)).then_inc(mods_ld, 16)
                sp.wait_ge(pv_mm, (b + 1) * (H * 4) + PV_CREDIT)
                sp.dma_start(x1_sb, x_t[bass.ds(b, 1)].rearrange("o p q d -> p (o q) d")).then_inc(x_again, 16)
                if more:
                    load_wv()
                sp.wait_ge(x1_ok, b + 1)
                sp.dma_start(out_t[bass.ds(b, 1)].rearrange("o p q d -> p (o q) d"), x1_sb).then_inc(st_rows, 16)
                if more:
                    head(b + 1, 0, 0, 1)
                sp.wait_ge(h2_ok, (b + 1) * NQ)
                sp.dma_start(rows_t[bass.ds(b, 1), :, :, 0:D].rearrange("o p q d -> p (o q) d"), h2_sb).then_inc(st_rows, 16)

            load_x(0)
            load_wqk(0, 0)
            load_wv()
            sp.wait_ge(mod_ok, 14)
            sp.dma_start(mods_dram, mods.rearrange("b m d -> b (m d)")).then_inc(mods_st, 16)
            sp.dma_start(gate_dram, mods[:, 3, :]).then_inc(mods_st, 16)
            sp.wait_ge(mods_st, 32)
            sp.sem_inc(st_rows, 32)
            head(0, 0, 0, 1)
            with sp.Fori(0, B - 1) as b:
                other_heads(b, True)
                boundary(b, True)
            other_heads(B - 1, False)
            boundary(B - 1, False)
            sp.wait_ge(st_rows, 32 * B + 32)

        @block.gpsimd
        def _(pool):
            nc.gpsimd.memset(ident[:], 0.0).then_inc(ident_z, 1)
            nc.gpsimd.memset(minus_half[:], -0.5).then_inc(ident_z, 1)
            pool.wait_ge(ident_z, 2)
            nc.gpsimd.affine_select(out=ident[:], in_=ident[:], compare_op=ALU.not_equal, fill=1.0, base=0,
                                    pattern=[[-1, PART]], channel_multiplier=1).then_inc(ident_z, 1)
            pool.wait_ge(ident_z, 3)
            nc.gpsimd.tensor_copy(ident_bf[:], ident[:]).then_inc(ident_ok, 1)
            pool.sem_inc(plo_pool, LP)
            pool.sem_inc(v3_ok, V3_CREDIT)
            pool.sem_inc(head_ok, HEAD_CREDIT)

            def inv_std(ready, done, n):
                pool.wait_ge(ready, n + 1)
                nc.gpsimd.tensor_tensor(rstd[:], var_eps[:], minus_half[:], ALU.pow).then_inc(done, 1)

            def third_parts(b):
                for i in range(NV):
                    kb, hg = i // NG, i % NG
                    rest = v_rest[:, i % V_BUFS, :].rearrange("p (h n) -> p h n", n=N)
                    v2 = v_all[:, kb, hg * HG:(hg + 1) * HG, N + 1:2 * N + 1]
                    v3 = v_all[:, kb, hg * HG:(hg + 1) * HG, 2 * N + 2:3 * N + 2]
                    pool.wait_ge(v2_ok, b * NV + i + 1)
                    nc.gpsimd.tensor_tensor(v3, rest, v2, ALU.subtract).then_inc(v3_ok, 1)

            def low(b, t, u, j):
                g = b * H + t
                pool.wait_ge(phi_ok, g * NQ + j + 1)
                if is_at(t, 1) and j == LOW_ON_POOL[0]:
                    pool.wait_ge(st_rows, b * 32 + 32)
                nc.gpsimd.tensor_tensor(p_lo[u][:, j, :], prob[:, j % 4, :], p_hi[u][:, j, :],
                                        ALU.subtract).then_inc(plo_pool, 1)

            def scale_pair(b, t, p):
                m = b * (H * 4) + t * 4 + p
                pool.wait_ge(pv_ev, m + 2)
                nc.gpsimd.tensor_tensor(heads[:, 2 * p:2 * p + 2, bass.ds(t * N, N)], pv_sum[:, p % 2],
                                        pv_inv[:, p % 2, :].unsqueeze(2).to_broadcast([PART, 2, N]),
                                        ALU.mult).then_inc(head_ok, 1)

            def all_heads(b):
                def head(t, u, first):
                    for j in range(NQ):
                        if not first and j and j % 2 == 0:
                            scale_pair(b, t - 1, j // 2 - 1)
                        if j in lows_of(t)[1]:
                            low(b, t, u, j)
                    if not first:
                        scale_pair(b, t - 1, NQ // 2 - 1)

                run_heads(pool, head)

            def boundary(b, more):
                for p in range(NQ // 2):
                    scale_pair(b, H - 1, p)
                if more:
                    inv_std(ln1_in, ln1_pow, b + 1)
                inv_std(ln2_in, ln2_pow, b)
                if more:
                    third_parts(b + 1)

            inv_std(ln1_in, ln1_pow, 0)
            third_parts(0)
            with pool.Fori(0, B - 1) as b:
                all_heads(b)
                boundary(b, True)
            all_heads(B - 1)
            boundary(B - 1, False)

        @block.scalar
        def _(act):
            act.sem_inc(exp_ok, EXP_CREDIT)
            act.wait_ge(const_ld, 16 * N_CONST)
            nc.scalar.activation(sig_t[:], c_t[:], ACT.Exp, scale=-1.0).then_inc(c_exp, 1)

            def v_stage(b, before):
                def second_part(i):
                    kb, hg = i // NG, i % NG
                    act.wait_ge(v_sub, b * NV + i + VSUB_CREDIT + 1)
                    nc.scalar.activation(v_all[:, kb, hg * HG:(hg + 1) * HG, N + 1:2 * N + 1],
                                         v_rest[:, i % V_BUFS, :].rearrange("p (h n) -> p h n", n=N), ACT.Copy).then_inc(v2_ok, 1)

                for i in range(NV):
                    kb, hg = i // NG, i % NG
                    act.wait_ge(v_mm, b * NV + i + 1)
                    src = st_ps[(i % 4) // 2][:, half_cols(i % 2)].rearrange("p (h n) -> p h n", n=N)
                    nc.scalar.activation(v_all[:, kb, hg * HG:(hg + 1) * HG, 0:N], src, ACT.Copy).then_inc(v1_ok, 1)
                    if i:
                        second_part(i - 1)
                    if i - 1 in PROJECT_AT:
                        high(b * H, 0, PROJECT_AT[i - 1])
                    if before is not None and i in TURN_AT:
                        h2_turned(before, TURN_AT[i])
                second_part(NV - 1)

            def h2_turned(b, i):
                kt, h = i // 2, i % 2
                act.wait_ge(h2t_mm, b * (2 * KT) + i + 1)
                nc.scalar.activation(h2_t[:, kt, half_cols(h)], pv_ps[:], ACT.Copy).then_inc(h2t_ev, 1)

            def high(g, u, h):
                act.wait_ge(proj_mm, g * 2 + h + 2)
                nc.scalar.activation(q_hh[u][0:N, half_cols(h)], ms_ps[0:N, :], ACT.Copy).then_inc(high_ok, 1)
                nc.scalar.activation(k_hl[u][0:N, half_cols(h)], ms_ps[N:2 * N, :], ACT.Copy).then_inc(high_ok, 1)

            def all_heads(b):
                def prob_tile(t, u, j, between=None):
                    g = b * H + t
                    act.wait_ge(st_mm, g * NQ + j + 1)
                    if j >= 4:
                        on_dve, on_pool = lows_of(t)
                        if (j - 4) in on_dve:
                            act.wait_ge(plo_dve, b * BD + t * LD + LD + count_upto(on_dve, j - 4))
                        else:
                            act.wait_ge(plo_pool, b * BP + t * LP + LP + count_upto(on_pool, j - 4))
                    else:
                        on_dve, on_pool = lows_of(H - 1 if is_at(t, 0) else 1)
                        if (j + 4) in on_dve:
                            act.wait_ge(plo_dve, b * BD + t * LD + LD - (len(on_dve) - count_upto(on_dve, j + 4)))
                        else:
                            act.wait_ge(plo_pool, b * BP + t * LP + LP - (len(on_pool) - count_upto(on_pool, j + 4)))
                    nc.scalar.activation(prob[:, j % 4, :], st_ps[j % 2][:], ACT.Exp, scale=SCALE).then_inc(exp_ok, 1)
                    if between:
                        between()
                    if j == 0:
                        act.wait_ge(pv_mm, g * 4 + PV_CREDIT - 4)
                    act.wait_ge(exp_ok, EXP_CREDIT + g * NQ + j + 1)
                    nc.scalar.activation(p_hi[u][:, j, :], prob[:, j % 4, :], ACT.Copy).then_inc(phi_ok, 1)

                def crow(g, u):
                    act.wait_ge(crow_mm, g + 1)
                    nc.scalar.activation(q_lc[u][N:N + 1, :], max_ps[0:1, :], ACT.Copy).then_inc(crow_ok, 1)

                high(b * H + 1, 1, 0)
                crow(b * H, 0)
                act.wait_ge(v3_ok, (b + 1) * NV + V3_CREDIT)

                def head(t, u, first):
                    g = b * H + t
                    last = is_at(t, H - 1)
                    if not last:
                        high(g + 1, 1 - u, 1)
                    for j in range(NQ - 1):
                        prob_tile(t, u, j)
                    more = not last and not is_at(t, H - 2)
                    prob_tile(t, u, NQ - 1, (lambda: high(g + 2, u, 0)) if more else None)
                    if not last:
                        crow(g + 1, 1 - u)

                run_heads(act, head)

            def boundary(b, more):
                for q in range(NQ):
                    act.wait_ge(ht_mm, b * NQ + q + 1)
                    if q >= 2:
                        act.wait_ge(o_mm, b * NQ + q - 1)
                    nc.scalar.activation(heads_t[q % 2], st_ps[q % 2][:, 0:HT * PART].rearrange("p (t n) -> p t n", n=PART), ACT.Copy).then_inc(ht_ev, 1)
                if more:
                    v_stage(b + 1, b)
                else:
                    for i in range(2 * KT):
                        h2_turned(b, i)

            v_stage(0, None)
            with act.Fori(0, B - 1) as b:
                all_heads(b)
                boundary(b, True)
            all_heads(B - 1)
            boundary(B - 1, False)

        @block.vector
        def _(dve):
            dve.sem_inc(plo_dve, LD)
            dve.sem_inc(v_sub, VSUB_CREDIT)
            dve.sem_inc(max_red, RED_CREDIT)
            for s_one in (low_ok, pv_ev, lg_ok):
                dve.sem_inc(s_one, 1)
            for u in range(2):
                nc.vector.memset(k_h1[u][N:2 * N, :].bitcast(F32), 0.0).then_inc(fill_ok, 1)
                nc.vector.memset(q_lc[u][N:2 * N, :].bitcast(F32), 0.0).then_inc(fill_ok, 1)
            nc.vector.memset(v_all[:, :, :, N:N + 1], 1.0).then_inc(fill_ok, 1)
            nc.vector.memset(v_all[:, :, :, 2 * N + 1:2 * N + 2], 0.0).then_inc(fill_ok, 1)
            dve.wait_ge(fill_ok, 6)
            for u in range(2):
                nc.vector.memset(k_h1[u][N:N + 1, :].bitcast(F32), 1.0).then_inc(fill_ok, 1)
            dve.wait_ge(c_exp, 1)
            nc.vector.tensor_scalar(sig_t[:], sig_t[:], 1.0, None, ALU.add).then_inc(c_silu, 1)
            dve.wait_ge(c_silu, 1)
            nc.vector.reciprocal(sig_t[:], sig_t[:]).then_inc(c_silu, 1)
            dve.wait_ge(c_silu, 2)
            nc.vector.tensor_tensor(silu_t[:], c_t[:], sig_t[:], ALU.mult).then_inc(c_silu, 1)
            def steps_of(signal, base, n):
                def step(ins, wait=True):
                    ins.then_inc(signal, 1)
                    n[0] += 1
                    if wait:
                        dve.wait_ge(signal, base + n[0])

                return step

            def mean_and_var(step, ready):
                mean_e, mean_o, m2_e, m2_o = stats[:, :, 1], stats[:, :, 4], stats[:, :, 2], stats[:, :, 5]
                step(nc.vector.tensor_tensor(mean[:], mean_e, mean_o, ALU.add), False)
                step(nc.vector.tensor_tensor(mean_d[:], mean_e, mean_o, ALU.subtract), False)
                step(nc.vector.tensor_tensor(var_eps[:], m2_e, m2_o, ALU.add))
                step(nc.vector.tensor_scalar(mean[:], mean[:], 0.5, None, ALU.mult), False)
                step(nc.vector.scalar_tensor_tensor(out=mean_d[:], in0=mean_d[:], scalar=0.25, in1=mean_d[:],
                                                    op0=ALU.mult, op1=ALU.mult), False)
                step(nc.vector.tensor_scalar(var_eps[:], var_eps[:], 1.0 / D, LN_EPS, ALU.mult, ALU.add))
                nc.vector.tensor_tensor(var_eps[:], var_eps[:], mean_d[:], ALU.add).then_inc(ready, 1)

            def first_norm(b):
                n1 = [0]
                step = steps_of(ln1, b * LN1_STEPS, n1)
                dve.wait_ge(x_ld, b * 16 + 16)
                for q in range(NQ):
                    step(nc.vector.bn_stats(stats[:, q, :], x_sb[:, q, :]), q == NQ - 1)
                mean_and_var(step, ln1_in)
                assert n1[0] == LN1_STEPS
                dve.wait_ge(ln1_pow, b + 1)
                for q in range(NQ):
                    nc.vector.tensor_scalar(norm[:, q, :], x_sb[:, q, :], mean[:, q:q + 1], rstd[:, q:q + 1],
                                            ALU.subtract, ALU.mult).then_inc(norm_ok, 1)

            def modulate(b, i):
                kt, h = i // 2, i % 2
                if i == 0:
                    nc.vector.tensor_copy(mod_b[:], mod_t[:, :, bass.ds(b, 1)].rearrange("p m o -> p (m o)")).then_inc(mod_b_ok, 1)
                    dve.wait_ge(mod_b_ok, b + 1)
                dve.wait_ge(ht_in_mm, b * (2 * KT) + i + 1)
                nc.vector.tensor_scalar(h_t[:, kt, half_cols(h)], max_ps[:, half_cols(i % 2)], mod_b[:, KT + kt:KT + kt + 1],
                                        mod_b[:, kt:kt + 1], ALU.mult, ALU.add).then_inc(ht_in_ev, 1)

            def v_stage(b, before):
                for i in range(NV):
                    kb, hg = i // NG, i % NG
                    n = b * NV + i
                    dve.wait_ge(v1_ok, n + 1)
                    dve.wait_ge(v3_ok, n + 1)
                    src = st_ps[(i % 4) // 2][:, half_cols(i % 2)].rearrange("p (h n) -> p h n", n=N)
                    nc.vector.tensor_tensor(v_rest[:, i % V_BUFS, :].rearrange("p (h n) -> p h n", n=N), src,
                                            v_all[:, kb, hg * HG:(hg + 1) * HG, 0:N], ALU.subtract).then_inc(v_sub, 1)
                    if before is not None:
                        h2_rows(before, i)
                        if i == LOGITS_AT + 1:
                            add_bias(before)
                    if i - 2 in PROJECT_AT:
                        lows(b * H, 0, PROJECT_AT[i - 2])
                    if i in FIRST_MAX_AT:
                        reduce_max(b * H, FIRST_MAX_AT[i])
                negate(b * H)

            def h2_rows(b, i):
                if i == 0:
                    dve.wait_ge(ln2_pow, b + 1)
                if i < NQ // 2:
                    for q in (2 * i, 2 * i + 1):
                        nc.vector.scalar_tensor_tensor(out=h2_sb[:, q, :], in0=x1_sb[:, q, :], scalar=mean[:, q:q + 1], in1=mod_rows[:, 2],
                                                       op0=ALU.subtract, op1=ALU.mult).then_inc(h2_scaled, 1)
                elif i < NQ:
                    for q in (2 * i - NQ, 2 * i - NQ + 1):
                        dve.wait_ge(h2_scaled, b * NQ + q + 1)
                        nc.vector.scalar_tensor_tensor(out=h2_sb[:, q, :], in0=h2_sb[:, q, :], scalar=rstd[:, q:q + 1], in1=mod_rows[:, 1],
                                                       op0=ALU.mult, op1=ALU.add).then_inc(h2_ok, 1)

            def add_bias(b):
                dve.wait_ge(lg_mm, b + 1)
                nc.vector.tensor_tensor(logits[:, bass.ds(b * NQ, NQ), :], pv_ps[:, 0:NQ * E].rearrange("p (q e) -> p q e", e=E),
                                        rb_bc[:].unsqueeze(1).to_broadcast([PART, NQ, E]), ALU.add).then_inc(lg_ok, 1)

            def lows(g, u, h):
                dve.wait_ge(high_ok, g * 4 + 2 * h + 2)
                nc.vector.tensor_tensor(q_lc[u][0:N, half_cols(h)], ms_ps[0:N, :],
                                        q_hh[u][0:N, half_cols(h)].bitcast(F32), ALU.subtract).then_inc(low_ok, 1)
                nc.vector.tensor_tensor(k_hl[u][N:2 * N, half_cols(h)], ms_ps[N:2 * N, :],
                                        k_hl[u][0:N, half_cols(h)].bitcast(F32), ALU.subtract).then_inc(low_ok, 1)

            def reduce_max(g, i):
                for h in range(2):
                    dve.wait_ge(max_mm, g * (2 * NQ) + 2 * i + h + 1)
                    nc.vector.tensor_reduce(row_max[:, i, h:h + 1], max_ps[:, half_cols(h)], AX.X, ALU.max).then_inc(max_red, 1)

            def negate(g):
                dve.wait_ge(max_red, g * (2 * NQ) + 2 * NQ + RED_CREDIT)
                nc.vector.tensor_reduce(neg_max[:], row_max[:], AX.X, ALU.max, negate=True).then_inc(neg_ok, 1)

            def low(b, t, u, j):
                g = b * H + t
                dve.wait_ge(phi_ok, g * NQ + j + 1)
                if is_at(t, 1) and j == LOW_ON_DVE[0]:
                    dve.wait_ge(st_rows, b * 32 + 32)
                nc.vector.tensor_tensor(p_lo[u][:, j, :], prob[:, j % 4, :], p_hi[u][:, j, :],
                                        ALU.subtract).then_inc(plo_dve, 1)

            def collect(g, p, bank):
                m = g * 4 + p
                dve.wait_ge(pv_mm, PV_CREDIT + m + 1)
                dve.wait_ge(head_ok, m + 1)
                src = bank[:, 0:2 * VW].rearrange("p (q w) -> p q w", q=2)
                nc.vector.tensor_reduce(pv_sum[:, p % 2], src.rearrange("p q (v n) -> p q n v", v=3)[:, :, 0:N, :],
                                        AX.X, ALU.add).then_inc(pv_red, 1)
                dve.wait_ge(pv_red, m + 1)
                nc.vector.reciprocal(pv_inv[:, p % 2, :], src[:, :, N]).then_inc(pv_ev, 1)

            def all_heads(b):
                lows(b * H + 1, 1, 0)

                def head(t, u, first):
                    g = b * H + t
                    last = is_at(t, H - 1)
                    for j in range(NQ):
                        if j == 0 and not last:
                            lows(g + 1, 1 - u, 1)
                        if j in MAX_BEFORE and not last:
                            reduce_max(g + 1, MAX_BEFORE[j])
                        if j == NQ - 1 and not last:
                            negate(g + 1)
                            if not is_at(t, H - 2):
                                lows(g + 2, u, 0)
                        if j and j % 2 == 0 and not first:
                            collect(g - 1, j // 2 - 1, pv_ps)
                        if j in MAX_AFTER and not last:
                            reduce_max(g + 1, MAX_AFTER[j])
                        if j in lows_of(t)[0]:
                            low(b, t, u, j)
                    if not first:
                        collect(g - 1, NQ // 2 - 1, pv_ps)

                run_heads(dve, head)
            def boundary(b, more):
                for p in range(NQ // 2):
                    collect(b * H + H - 1, p, (pv_ps, ms_ps)[p % 2])
                if more:
                    first_norm(b + 1)
                n2 = [0]
                step = steps_of(ln2, b * LN2_STEPS, n2)
                dve.wait_ge(mods_ld, b * 16 + 16)
                dve.wait_ge(x_again, b * 16 + 16)
                for q in range(NQ):
                    dve.wait_ge(o_mm, b * NQ + q + 1)
                    o_ps = (pv_ps if q % 2 == 0 else ms_ps)[:, 0:D]
                    nc.vector.tensor_tensor(h2_sb[:, q, :], o_ps, mod_rows[:, 0], ALU.mult).then_inc(gated, 1)
                    dve.wait_ge(gated, b * NQ + q + 1)
                    nc.vector.tensor_tensor(x1_sb[:, q, :], h2_sb[:, q, :], x1_sb[:, q, :], ALU.add).then_inc(x1_row, 1)
                    dve.wait_ge(x1_row, b * NQ + q + 1)
                    step(nc.vector.bn_stats(stats[:, q, :], x1_sb[:, q, :]), q == NQ - 1)
                    if more and q in NORM_TURN_AT:
                        for i in NORM_TURN_AT[q]:
                            modulate(b + 1, i)
                dve.sem_inc(x1_ok, 1)
                mean_and_var(step, ln2_in)
                assert n2[0] == LN2_STEPS
                if more:
                    v_stage(b + 1, b)
                else:
                    for i in range(NQ):
                        h2_rows(b, i)
                    add_bias(b)

            first_norm(0)
            dve.wait_ge(mod_mm, 1)
            md = ms_ps[:, 0:2 * KT * B].rearrange("p (m b) -> p m b", b=B)
            nc.vector.tensor_copy(mod_t[:, 0:KT, :], md[:, 0:KT]).then_inc(mod_ok, 1)
            nc.vector.tensor_scalar(mod_t[:, KT:2 * KT, :], md[:, KT:2 * KT], 1.0, None, ALU.add).then_inc(mod_ok, 1)
            raw = st_ps[0][0:B, :].rearrange("b (m d) -> b m d", m=4)
            nc.vector.tensor_copy(mods[:, 1, :], raw[:, 1]).then_inc(mod_ok, 1)
            nc.vector.tensor_scalar(mods[:, 2, :], raw[:, 2], 1.0, None, ALU.add).then_inc(mod_ok, 1)
            for i, m in enumerate((0, 3)):
                nc.vector.tensor_scalar(mods_s[:, 2 * i], raw[:, m], 0.0, None, ALU.is_ge).then_inc(mod_ok, 1)
                nc.vector.tensor_scalar(mods_s[:, 2 * i + 1], raw[:, m], 0.0, None, ALU.is_lt).then_inc(mod_ok, 1)
            dve.wait_ge(mod_ok, 8)
            for i, m in enumerate((0, 3)):
                nc.vector.scalar_tensor_tensor(out=mods_s[:, 2 * i], in0=raw[:, m], scalar=GATE_FLOOR, in1=mods_s[:, 2 * i],
                                               op0=ALU.max, op1=ALU.mult).then_inc(mod_ok, 1)
                nc.vector.scalar_tensor_tensor(out=mods_s[:, 2 * i + 1], in0=raw[:, m], scalar=-GATE_FLOOR,
                                               in1=mods_s[:, 2 * i + 1], op0=ALU.min, op1=ALU.mult).then_inc(mod_ok, 1)
            dve.wait_ge(mod_ok, 12)
            for i, m in enumerate((0, 3)):
                nc.vector.tensor_tensor(mods[:, m, :], mods_s[:, 2 * i], mods_s[:, 2 * i + 1], ALU.add).then_inc(mod_ok, 1)
            for i in range(2 * KT):
                modulate(0, i)
            v_stage(0, None)
            with dve.Fori(0, B - 1) as b:
                all_heads(b)
                boundary(b, True)
            all_heads(B - 1)
            boundary(B - 1, False)

        @block.tensor
        def _(pe):
            pe.sem_inc(pv_mm, PV_CREDIT)
            pe.sem_inc(proj_mm, 1)
            pe.wait_ge(const_ld, 16 * N_CONST)
            pe.wait_ge(c_silu, 3)
            for m in range(2 * KT):
                for kt in range(KT):
                    nc.tensor.matmul(ms_ps[:, m * B:(m + 1) * B], wmod_sb[:, kt, tile_cols(m)], silu_t[:, kt, :],
                                     start=(kt == 0), stop=(kt == KT - 1))
            for h in range(2):
                for kt in range(KT):
                    mm = nc.tensor.matmul(st_ps[0][0:B, half_cols(h)], silu_t[:, kt, :], wmod_sb[:, kt, 2 * D + h * HALF:2 * D + (h + 1) * HALF],
                                          start=(kt == 0), stop=(kt == KT - 1))
            mm.then_inc(mod_mm, 1)
            pe.wait_ge(ident_ok, 1)
            pe.wait_ge(fill_ok, 8)
            def turn_norm(b, i):
                kt, h = i // 2, i % 2
                if i == 0:
                    pe.wait_ge(norm_ok, (b + 1) * NQ)
                if i >= 2:
                    pe.wait_ge(ht_in_ev, b * (2 * KT) + i - 1)
                for q in range(4):
                    mm = nc.tensor.transpose(max_ps[:, (i % 2) * HALF + q * PART:(i % 2) * HALF + (q + 1) * PART],
                                             norm[:, h * 4 + q, tile_cols(kt)], ident[:])
                mm.then_inc(ht_in_mm, 1)

            def turn_h2(b, i):
                kt, h = i // 2, i % 2
                if i == 0:
                    pe.wait_ge(h2_ok, (b + 1) * NQ)
                else:
                    pe.wait_ge(h2t_ev, b * (2 * KT) + i)
                for q in range(4):
                    mm = nc.tensor.transpose(pv_ps[:, tile_cols(q)], h2_sb[:, h * 4 + q, tile_cols(kt)], ident[:])
                mm.then_inc(h2t_mm, 1)

            def router_logits(b):
                pe.wait_ge(h2t_ev, b * (2 * KT) + 2 * KT)
                for q in range(NQ):
                    for kt in range(KT):
                        mm = nc.tensor.matmul(pv_ps[:, q * E:(q + 1) * E], h2_t[:, kt, tile_cols(q)], rw_sb[:, kt, :],
                                              start=(kt == 0), stop=(kt == KT - 1))
                mm.then_inc(lg_mm, 1)

            def project(b, t, u, h):
                g = b * H + t
                pe.wait_ge(low_ok, g * 4 + 2 * h + 1)
                if h == 0:
                    pe.wait_ge(wqk_ld[u], pair_dmas(b, t, u))
                for kt in range(KT):
                    mm = nc.tensor.matmul(ms_ps[:], wqk[u][:, kt].rearrange("p a n -> p (a n)"), h_t[:, kt, half_cols(h)],
                                          start=(kt == 0), stop=(kt == KT - 1))
                mm.then_inc(proj_mm, 1)

            def max_tile(b, t, u, i):
                g = b * H + t
                if i == 0:
                    pe.wait_ge(low_ok, g * 4 + 4 + 1)
                    pe.wait_ge(dup_ok[u], pair_dmas(b, t, u))
                for h in range(2):
                    pe.wait_ge(max_red, g * (2 * NQ) + 2 * i + h - 1 + RED_CREDIT)
                    mm = nc.tensor.matmul(max_ps[:, half_cols(h)], q_hh[u][:, tile_cols(i)], k_hl[u][:, half_cols(h)],
                                          start=True, stop=True)
                    mm.then_inc(max_mm, 1)

            def max_row(g):
                pe.wait_ge(neg_ok, g + 1)
                for q in range(NQ):
                    mm = nc.tensor.matmul(max_ps[0:1, tile_cols(q)], neg_max[:, q:q + 1], ident_bf[:], start=True, stop=True)
                mm.then_inc(crow_mm, 1)

            def scores(g, u, j):
                if j == 0:
                    pe.wait_ge(crow_ok, g + 1)
                pe.wait_ge(exp_ok, g * NQ + j - 1 + EXP_CREDIT)
                for h in range(2):
                    nc.tensor.matmul(st_ps[j % 2][:, half_cols(h)], k_hl[u][:, tile_cols(j)], q_hh[u][:, half_cols(h)],
                                     start=True, stop=False)
                for h in range(2):
                    mm = nc.tensor.matmul(st_ps[j % 2][:, half_cols(h)], k_h1[u][:, tile_cols(j)], q_lc[u][:, half_cols(h)],
                                          start=False, stop=True)
                mm.then_inc(st_mm, 1)

            def weighted(b, t, u, q, tail=False):
                g = b * H + t
                bank = (pv_ps, ms_ps)[(q // 2) % 2] if tail else pv_ps
                if q == 0:
                    pe.wait_ge(plo_dve, b * BD + t * LD + LD + len(lows_of(t)[0]))
                    pe.wait_ge(plo_pool, b * BP + t * LP + LP + len(lows_of(t)[1]))
                    pe.wait_ge(v3_ok, b * NV + NV + V3_CREDIT)
                if is_at(t, 0) and q == 0:
                    pe.wait_ge(lg_ok, b + 1)
                if q % 2 == 0 and tail and q == 2:
                    pe.wait_ge(low_ok, (b + 1) * (H * 4) + 1)
                elif q % 2 == 0:
                    pe.wait_ge(pv_ev, g * 4 + q // 2 + (0 if tail and q else 1))
                o = bank[:, (q % 2) * VW:(q % 2) * VW + VHI]
                for kb in range(NQ):
                    v = v_all[:, kb, bass.ds(t, 1), :].rearrange("p o w -> p (o w)")
                    nc.tensor.matmul(o, p_hi[u][:, kb, tile_cols(q)], v[:, 0:VHI], start=(kb == 0), stop=False)
                    mm = nc.tensor.matmul(o[:, 0:VLO], p_lo[u][:, kb, tile_cols(q)], v[:, 0:VLO],
                                          start=False, stop=(kb == NQ - 1))
                if q % 2 == 1:
                    mm.then_inc(pv_mm, 1)

            def v_stage(b, before):
                pe.wait_ge(ht_in_ev, b * (2 * KT) + 2 * KT)
                pe.wait_ge(wv_ld, b * (16 * KT) + 16 * KT)
                if before is not None:
                    pe.wait_ge(ht_ev, before * NQ + NQ)
                for i in range(NV):
                    kb, hg = i // NG, i % NG
                    pe.wait_ge(v_sub, b * NV + i + 1)
                    for kt in range(KT):
                        mm = nc.tensor.matmul(st_ps[(i % 4) // 2][:, half_cols(i % 2)], h_t[:, kt, tile_cols(kb)],
                                              wv_sb[:, kt, hg * HG:(hg + 1) * HG, :].rearrange("p h n -> p (h n)"),
                                              start=(kt == 0), stop=(kt == KT - 1))
                    mm.then_inc(v_mm, 1)
                    if i in PROJECT_AT:
                        if before is not None and PROJECT_AT[i] == 0:
                            pe.wait_ge(gated, (before + 1) * NQ)
                        project(b, 0, 0, PROJECT_AT[i])
                    if i in FIRST_MAX_AT:
                        max_tile(b, 0, 0, FIRST_MAX_AT[i])
                    if before is not None and i in TURN_AT:
                        turn_h2(before, TURN_AT[i])
                    if before is not None and i == LOGITS_AT:
                        router_logits(before)

            def all_heads(b):
                project(b, 1, 1, 0)
                max_row(b * H)

                def head(t, u, first):
                    g = b * H + t
                    last = is_at(t, H - 1)
                    for j in range(NQ):
                        if j == 0 and not last:
                            project(b, t + 1, 1 - u, 1)
                        scores(g, u, j)
                        if j == NQ - 1 and not last and not is_at(t, H - 2):
                            project(b, t + 2, u, 0)
                        if j in MAX_BEFORE and not last:
                            max_tile(b, t + 1, 1 - u, MAX_BEFORE[j])
                        if j and not first:
                            weighted(b, t - 1, 1 - u, j - 1)
                        if j in MAX_AFTER and not last:
                            max_tile(b, t + 1, 1 - u, MAX_AFTER[j])
                    if not first:
                        weighted(b, t - 1, 1 - u, NQ - 1)
                    if not last:
                        max_row(g + 1)

                run_heads(pe, head)

            def boundary(b, more):
                for q in range(NQ):
                    weighted(b, H - 1, 1, q, True)

                def turn(q):
                    if q >= 2:
                        pe.wait_ge(ht_ev, b * NQ + q - 1)
                    if q == 0:
                        pe.wait_ge(exp_ok, (b + 1) * (H * NQ) + EXP_CREDIT)
                        pe.wait_ge(head_ok, (b + 1) * (H * 4) + HEAD_CREDIT)
                    for t in range(HT):
                        mm = nc.tensor.transpose(st_ps[q % 2][:, tile_cols(t)], heads[:, q, tile_cols(t)], ident[:])
                    mm.then_inc(ht_mm, 1)

                pe.wait_ge(wo_ld, b * 16 + 16)
                turn(0)
                pe.wait_ge(pv_ev, (b + 1) * (H * 4) + 1)
                for q in range(NQ):
                    if q < NQ - 1:
                        turn(q + 1)
                    pe.wait_ge(ht_ev, b * NQ + q + 1)
                    if q >= 2:
                        pe.wait_ge(gated, b * NQ + q - 1)
                    o_ps = (pv_ps if q % 2 == 0 else ms_ps)[:, 0:D]
                    for t in range(HT):
                        mm = nc.tensor.matmul(o_ps, heads_t[q % 2][:, t, :], wo_sb[:, t, :], start=(t == 0), stop=(t == HT - 1))
                    mm.then_inc(o_mm, 1)
                    if more and q in NORM_TURN_AT:
                        pe.wait_ge(crow_ok, (b + 1) * H)
                        for i in NORM_TURN_AT[q]:
                            turn_norm(b + 1, i)
                if more:
                    v_stage(b + 1, b)
                else:
                    pe.wait_ge(gated, (b + 1) * NQ)
                    for i in range(2 * KT):
                        turn_h2(b, i)
                    router_logits(b)

            for i in range(2 * KT):
                turn_norm(0, i)
            pe.wait_ge(mod_ok, 14)
            v_stage(0, None)
            with pe.Fori(0, B - 1) as b:
                all_heads(b)
                boundary(b, True)
            all_heads(B - 1)
            boundary(B - 1, False)


def ffn_phase(nc, k):
    B, P, D, E, F, NB = k["B"], k["P"], k["D"], k["E"], k["F"], k["NB"]
    KT, ST, FT, ROW, TK = k["KT"], k["ST"], k["FT"], k["ROW"], k["topk"]
    SLOT_LO, SLOT_HI = k["SLOT_LO"], k["SLOT_HI"]
    ident, logits = k["ident"], k["logits"]
    rows_dram, rows_blk, gate_dram, slots_dram, out_rows = k["rows_dram"], k["rows_blk"], k["gate_dram"], k["slots_dram"], k["out_rows"]
    w1, b1, w2, b2 = k["w1"], k["b1"], k["w2"], k["b2"]
    EB = E * NB
    TOP_BIT = 29
    NOWHERE = 4096.0
    LO_BITS = SLOT_LO.bit_length() - 1
    CHUNK = 16
    assert TK % PART == 0 and SLOT_HI * SLOT_LO == TK and SLOT_HI <= PART and 2 * TK < NOWHERE

    with ExitStack() as ctx:
        def sb(name, shape, dt):
            return ctx.enter_context(nc.sbuf_tensor(name, shape, dt))

        def ps(name, shape):
            return ctx.enter_context(nc.psum_tensor(name, shape, F32))

        def sem(name):
            return ctx.enter_context(nc.semaphore(name))

        token_max = sb("token_max", [PART, NB], F32)
        token_sum = sb("token_sum", [PART, NB], F32)
        scores = sb("scores", [PART, E, NB], F32)
        ones_bf = sb("ones_bf", [PART, PART], BF16)
        before_bf = sb("before_bf", [PART, PART], BF16)
        thr = sb("thr", [PART, E], I32)
        cand = sb("cand", [PART, E], I32)
        bit = sb("bit", [PART, E], I32)
        flag = sb("flag", [PART, E], I32)
        cnt = sb("cnt", [PART, E], F32)
        mask = sb("mask", [PART, 2, E, NB], BF16)
        tot = sb("tot", [PART, 2, EB], F32)
        incl = sb("incl", [PART, 2, EB], F32)
        carry = sb("carry", [PART, E, NB], F32)
        need = sb("need", [PART, E], F32)
        place = sb("place", [PART, EB], F32)
        take = sb("take", [PART, EB], F32)
        place_i = sb("place_i", [PART, EB], I32)
        part_i = sb("part_i", [PART, EB], I32)
        place_hi = sb("place_hi", [PART, EB], BF16)
        place_lo = sb("place_lo", [PART, EB], BF16)
        iota_i = sb("iota_i", [PART, NB + SLOT_LO], I32)
        iota_bf = sb("iota_bf", [PART, NB + SLOT_LO], BF16)
        row_i = sb("row_i", [PART, 1], I32)
        row_f = sb("row_f", [PART, 1], F32)
        hot_hi = sb("hot_hi", [PART, NB, SLOT_HI], BF16)
        hot_lo = sb("hot_lo", [PART, NB, SLOT_LO], BF16)
        hot_id = sb("hot_id", [PART, NB, 2, SLOT_LO], BF16)
        id_f = sb("id_f", [SLOT_HI, 2, SLOT_LO], F32)
        id_i = sb("id_i", [SLOT_HI, SLOT_LO], U32)
        slots = sb("slots", [PART, E, ST], U32)
        slot_batch = sb("slot_batch", [PART, E, ST], U32)
        w1_sb = sb("w1_sb", [PART, KT, F], F32)
        w2_sb = sb("w2_sb", [PART, FT, D], F32)
        w1_hi = [sb(f"w1_hi{u}", [PART, KT, F], F32R) for u in range(2)]
        w2_hi = [sb(f"w2_hi{u}", [PART, FT, D], F32R) for u in range(2)]
        w1_lo = [sb(f"w1_lo{u}", [PART, KT, F], F32R) for u in range(2)]
        w2_lo = [sb(f"w2_lo{u}", [PART, FT, D], F32R) for u in range(2)]
        b1_sb = [sb(f"b1_sb{u}", [PART, FT], F32) for u in range(2)]
        b2_sb = [sb(f"b2_sb{u}", [PART, D], F32) for u in range(2)]
        rows = [sb(f"rows{u}", [PART, ST, ROW], F32) for u in range(2)]
        gates = [sb(f"gates{u}", [PART, ST, D], F32) for u in range(2)]
        weight = [sb(f"weight{u}", [PART, ST], F32) for u in range(2)]
        rows_hi = sb("rows_hi", [PART, KT, TK], F32R)
        rows_lo = sb("rows_lo", [PART, KT, TK], F32R)
        hid = sb("hid", [PART, 2, TK], F32)
        hid_hi = sb("hid_hi", [PART, FT, TK], F32R)
        hid_lo = sb("hid_lo", [PART, FT, TK], F32R)
        y_t = sb("y_t", [PART, KT, TK], F32)
        contrib = [sb(f"contrib{u}", [PART, ST, D], F32) for u in range(2)]

        a_ps = [ps(f"a_ps{i}", [PART, HALF]) for i in range(4)]
        y_ps = [ps(f"y_ps{i}", [PART, HALF]) for i in range(2)]
        c_ps = ps("c_ps", [PART, HALF])
        z_ps = ps("z_ps", [PART, HALF])

        rt = sem("rt")
        sm_exp = sem("sm_exp")
        sc_ok = sem("sc_ok")
        sc_st = sem("sc_st")
        cst = sem("cst")
        bs = sem("bs")
        cnt_in = sem("cnt_in")
        cnt_mm = sem("cnt_mm")
        mask_ok = sem("mask_ok")
        rank_mm = sem("rank_mm")
        hot = sem("hot")
        hot_ok = sem("hot_ok")
        id_mm = sem("id_mm")
        id_cp = sem("id_cp")
        id_ok = sem("id_ok")
        id_st = sem("id_st")
        id_ld = [sem(f"id_ld{u}") for u in range(2)]
        sb_ok = sem("sb_ok")
        w_ld = sem("w_ld")
        b_ld = [sem(f"b_ld{u}") for u in range(2)]
        got = [sem(f"got{u}") for u in range(2)]
        g_cp = sem("g_cp")
        rt_mm = sem("rt_mm")
        rt_ev = sem("rt_ev")
        hid_mm = sem("hid_mm")
        hid_ok = sem("hid_ok")
        hid_hi_ok = sem("hid_hi_ok")
        hid_lo_ok = sem("hid_lo_ok")
        rt_lo_ok = sem("rt_lo_ok")
        w_hi_ok = sem("w_hi_ok")
        w_lo_ok = sem("w_lo_ok")
        yt_mm = sem("yt_mm")
        yt_ev = sem("yt_ev")
        y_mm = sem("y_mm")
        y_b = sem("y_b")
        y_ok = sem("y_ok")
        added = sem("added")
        contrib_free = sem("contrib_free")

        STEP_BS, STEP_HOT = 5, 3
        block = ctx.enter_context(nc.Block())

        @block.sync
        def _(sp):
            def load_layers(e):
                sp.dma_start(w1_sb[:], w1[bass.ds(e, 1)].rearrange("o (t p) f -> p (o t) f", p=PART)).then_inc(w_ld, 16)
                sp.dma_start(w2_sb[:], w2[bass.ds(e, 1)].rearrange("o (t p) d -> p (o t) d", p=PART)).then_inc(w_ld, 16)

            def load_biases(e, u):
                sp.dma_start(b1_sb[u][:], b1[bass.ds(e, 1)].rearrange("o (t p) -> p (o t)", p=PART),
                             allow_slow_non_contiguous=True).then_inc(b_ld[u], 16)
                sp.dma_start(b2_sb[u][:], b2[bass.ds(e, 1)].rearrange("o d -> (o d)").partition_broadcast(PART)).then_inc(b_ld[u], 16)

            load_layers(0)
            for e in range(2):
                load_biases(e, e)
            sp.wait_ge(sc_ok, 1)
            sp.dma_start(rows_blk[:, :, D:D + E], logits[:]).then_inc(sc_st, 16)

            def store_slots(e):
                sp.wait_ge(id_ok, e + 1)
                sp.dma_start(slots_dram[bass.ds(e, 1)].rearrange("o (h l) -> (o h) l", l=SLOT_LO), id_i[:]).then_inc(id_st, 16)

            def load_slots(e, u):
                sp.dma_start(slots[:, bass.ds(e, 1), :], slots_dram[bass.ds(e, 1)].rearrange("o (s p) -> p o s", p=PART),
                             allow_slow_non_contiguous=True).then_inc(id_ld[u], 16)

            sp.wait_ge(w_lo_ok, 2)
            load_layers(1)
            for e in range(2):
                store_slots(e)
                sp.wait_ge(id_st, 16 * (e + 1) + 1)
                load_slots(e, e)
            with sp.Fori(0, E // 2 - 1) as ep:
                for u in range(2):
                    e = ep * 2 + u
                    store_slots(e + 2)
                    sp.wait_ge(id_st, 16 * (e + 3) + 1)
                    load_slots(e + 2, u)
                    sp.wait_ge(w_lo_ok, e * 2 + 4)
                    load_layers(e + 2)
                    sp.wait_ge(y_ok, (e + 1) * ST)
                    load_biases(e + 2, u)
            sp.wait_ge(sc_st, 16)

        @block.gpsimd
        def _(pool):
            nc.gpsimd.iota(iota_i[:, 0:NB], [[1, NB]], base=0, channel_multiplier=0).then_inc(cst, 1)
            nc.gpsimd.iota(iota_i[:, NB:], [[1, SLOT_LO]], base=0, channel_multiplier=0).then_inc(cst, 1)
            nc.gpsimd.iota(row_i[:], [[0, 1]], base=0, channel_multiplier=1).then_inc(cst, 1)
            nc.gpsimd.memset(ones_bf[:], 1.0).then_inc(cst, 1)
            pool.wait_ge(cst, 4)
            nc.gpsimd.affine_select(out=before_bf[:], in_=ones_bf[:], compare_op=ALU.is_gt, fill=0.0, base=0,
                                    pattern=[[1, PART]], channel_multiplier=-1).then_inc(cst, 1)

            def gather(e, u):
                for s in range(ST):
                    nc.gpsimd.indirect_dma_start(
                        out=rows[u][:, s, :], out_offset=None, in_=rows_dram,
                        in_offset=bass.IndirectOffsetOnAxis(ap=slots[:, e, s:s + 1], axis=0)).then_inc(got[u], 16)
                    nc.gpsimd.indirect_dma_start(
                        out=gates[u][:, s, :], out_offset=None, in_=gate_dram,
                        in_offset=bass.IndirectOffsetOnAxis(ap=slot_batch[:, e, s:s + 1], axis=0)).then_inc(got[u], 16)

            def scatter(e, u):
                if e:
                    pool.wait_ge(added, e * (16 * ST))
                    pool.sem_inc(contrib_free, 1)
                for s in range(ST):
                    pool.wait_ge(y_ok, e * ST + s + 1)
                    nc.gpsimd.indirect_dma_start(
                        out=out_rows, out_offset=bass.IndirectOffsetOnAxis(ap=slots[:, e, s:s + 1], axis=0),
                        in_=contrib[u][:, s, :], in_offset=None, compute_op=ALU.add).then_inc(added, 16)

            for i, (raw, low, high) in enumerate(((w1_sb, w1_lo, w1_hi), (w2_sb, w2_lo, w2_hi))):
                pool.wait_ge(w_hi_ok, i + 1)
                nc.gpsimd.tensor_tensor(low[0][:], raw[:], high[0][:].bitcast(F32), ALU.subtract).then_inc(w_lo_ok, 1)
            pool.sem_inc(contrib_free, 2)
            pool.wait_ge(sc_st, 16)
            for e in range(2):
                pool.wait_ge(sb_ok, e + 1)
                gather(e, e)
            for e in range(E):
                scatter(e, e % 2)
                if e + 2 < E:
                    pool.wait_ge(sb_ok, e + 3)
                    gather(e + 2, e % 2)
            pool.wait_ge(added, E * (16 * ST))

        @block.scalar
        def _(act):
            act.wait_ge(rt, 2)
            nc.scalar.activation(logits[:], logits[:], ACT.Exp).then_inc(sm_exp, 1)

            def weights_high(e, u):
                act.wait_ge(w_ld, e * 32 + 32)
                nc.scalar.activation(w1_hi[u][:], w1_sb[:], ACT.Copy).then_inc(w_hi_ok, 1)
                nc.scalar.activation(w2_hi[u][:], w2_sb[:], ACT.Copy).then_inc(w_hi_ok, 1)

            def rows_high(e):
                for t in range(KT):
                    act.wait_ge(rt_mm, e * KT + t + 1)
                    nc.scalar.activation(rows_hi[:, t, :], a_ps[t][:, 0:TK], ACT.Copy).then_inc(rt_ev, 1)

            def experts(ep, more):
                for u in range(2):
                    e = ep * 2 + u
                    act.wait_ge(b_ld[u], (ep + 1) * 32)
                    for f in range(FT):
                        act.wait_ge(hid_mm, e * FT + f + 1)
                        act.wait_ge(hid_lo_ok, e * FT + f + 1)
                        nc.scalar.activation(hid[:, f % 2, :], a_ps[f % 4][:, 0:TK], ACT.Relu, bias=b1_sb[u][:, f:f + 1]).then_inc(hid_ok, 1)
                        act.wait_ge(hid_ok, e * FT + f + 1)
                        nc.scalar.activation(hid_hi[:, f, :], hid[:, f % 2, :], ACT.Copy).then_inc(hid_hi_ok, 1)
                    if more or u == 0:
                        weights_high(e + 1, 1 - u)
                    for t in range(KT):
                        act.wait_ge(yt_mm, e * KT + t + 1)
                        nc.scalar.activation(y_t[:, t, :], y_ps[t][:, 0:TK], ACT.Copy).then_inc(yt_ev, 1)
                    if more or u == 0:
                        rows_high(e + 1)

            weights_high(0, 0)
            rows_high(0)
            with act.Fori(0, E // 2 - 1) as ep:
                experts(ep, True)
            experts(E // 2 - 1, False)

        @block.vector
        def _(dve):
            n_rt = [0]

            def step(ins, wait=True):
                ins.then_inc(rt, 1)
                n_rt[0] += 1
                if wait:
                    dve.wait_ge(rt, n_rt[0])

            dve.sem_inc(hid_lo_ok, 2)
            dve.sem_inc(y_b, 2)
            dve.sem_inc(id_st, 1)
            step(nc.vector.tensor_reduce(token_max[:], logits[:], AX.X, ALU.max))
            step(nc.vector.tensor_tensor(logits[:], logits[:], token_max[:].unsqueeze(2).to_broadcast([PART, NB, E]), ALU.subtract), False)
            dve.wait_ge(sm_exp, 1)
            step(nc.vector.tensor_reduce(token_sum[:], logits[:], AX.X, ALU.add))
            step(nc.vector.reciprocal(token_sum[:], token_sum[:]))
            nc.vector.tensor_tensor(logits[:], logits[:], token_sum[:].unsqueeze(2).to_broadcast([PART, NB, E]), ALU.mult).then_inc(sc_ok, 1)
            dve.wait_ge(sc_ok, 1)
            step(nc.vector.tensor_copy(scores[:], logits[:].rearrange("p n e -> p e n")), False)
            dve.wait_ge(cst, 5)
            step(nc.vector.tensor_copy(iota_bf[:], iota_i[:]), False)
            step(nc.vector.tensor_copy(row_f[:], row_i[:]), False)
            step(nc.vector.memset(carry[:], 1.0))
            step(nc.vector.memset(carry[:, :, 0:1], 0.0), False)
            step(nc.vector.memset(thr[:], 0), False)
            step(nc.vector.memset(bit[:], 1 << TOP_BIT), False)
            step(nc.vector.memset(cand[:], 1 << TOP_BIT))

            with dve.Fori(0, TOP_BIT + 1) as i:
                nc.vector.tensor_tensor(mask[:, 0], scores[:], cand[:].bitcast(F32).unsqueeze(2).to_broadcast([PART, E, NB]),
                                        ALU.is_ge).then_inc(cnt_in, 1)
                dve.wait_ge(cnt_mm, i + 1)
                nc.vector.tensor_reduce(cnt[:], c_ps[:, 0:E * CHUNK].rearrange("p (e n) -> p e n", n=CHUNK), AX.X, ALU.add).then_inc(bs, 1)
                dve.wait_ge(bs, i * STEP_BS + 1)
                nc.vector.tensor_scalar(flag[:], cnt[:], float(TK), None, ALU.is_ge).then_inc(bs, 1)
                dve.wait_ge(bs, i * STEP_BS + 2)
                nc.vector.tensor_scalar(bit[:], bit[:], 1, None, ALU.logical_shift_right).then_inc(bs, 1)
                nc.vector.copy_predicated(thr[:], flag[:], cand[:]).then_inc(bs, 1)
                dve.wait_ge(bs, i * STEP_BS + 4)
                nc.vector.tensor_tensor(cand[:], thr[:], bit[:], ALU.bitwise_or).then_inc(bs, 1)
                dve.wait_ge(bs, i * STEP_BS + 5)

            thr_bc = thr[:].bitcast(F32).unsqueeze(2).to_broadcast([PART, E, NB])
            nc.vector.tensor_tensor(mask[:, 0], scores[:], thr_bc, ALU.is_gt).then_inc(mask_ok, 1)
            nc.vector.tensor_tensor(mask[:, 1], scores[:], thr_bc, ALU.is_equal).then_inc(mask_ok, 1)
            dve.wait_ge(rank_mm, 1)
            carry_f = carry[:].rearrange("p e n -> p (e n)")
            for m in range(2):
                step(nc.vector.tensor_copy(tot[:, m], a_ps[2 + m][:, 0:EB]), m == 1)
            for m in range(2):
                step(nc.vector.tensor_tensor_scan(incl[:, m], carry_f, tot[:, m], 0.0, ALU.mult, ALU.add), m == 1)
            step(nc.vector.tensor_scalar(need[:], incl[:, 0].rearrange("p (e n) -> p e n", n=NB)[:, :, NB - 1], -1.0, float(TK), ALU.mult, ALU.add), False)
            step(nc.vector.tensor_tensor(tot[:], incl[:], tot[:], ALU.subtract))
            for m in range(2):
                step(nc.vector.tensor_tensor(tot[:, m], tot[:, m], a_ps[m][:, 0:EB], ALU.add), m == 1)
            need_bc = need[:].unsqueeze(2).to_broadcast([PART, E, NB])

            def by_expert(ap):
                return ap.rearrange("p (e n) -> p e n", n=NB)

            step(nc.vector.tensor_tensor(by_expert(place[:]), by_expert(tot[:, 1]), need_bc, ALU.min), False)
            step(nc.vector.tensor_tensor(by_expert(take[:]), by_expert(tot[:, 1]), need_bc, ALU.is_lt))
            step(nc.vector.tensor_tensor(place[:], place[:], tot[:, 0], ALU.add), False)
            step(nc.vector.tensor_tensor(take[:], take[:], mask[:, 1].rearrange("p e n -> p (e n)"), ALU.mult))
            step(nc.vector.tensor_tensor(take[:], take[:], mask[:, 0].rearrange("p e n -> p (e n)"), ALU.add))
            step(nc.vector.scalar_tensor_tensor(out=place[:], in0=take[:], scalar=-NOWHERE, in1=place[:], op0=ALU.mult, op1=ALU.add))
            step(nc.vector.tensor_scalar(place_i[:], place[:], NOWHERE, None, ALU.add))
            step(nc.vector.tensor_scalar(part_i[:], place_i[:], LO_BITS, None, ALU.logical_shift_right))
            step(nc.vector.tensor_copy(place_hi[:], part_i[:]))
            step(nc.vector.tensor_scalar(part_i[:], place_i[:], SLOT_LO - 1, None, ALU.bitwise_and))
            step(nc.vector.tensor_copy(place_lo[:], part_i[:]))

            def one_hots(e):
                hi_e = place_hi[:, bass.ds(e * NB, NB)].unsqueeze(2).to_broadcast([PART, NB, SLOT_HI])
                lo_e = place_lo[:, bass.ds(e * NB, NB)].unsqueeze(2).to_broadcast([PART, NB, SLOT_LO])
                nc.vector.tensor_tensor(hot_hi[:], hi_e, iota_bf[:, NB:NB + SLOT_HI].unsqueeze(1).to_broadcast([PART, NB, SLOT_HI]),
                                        ALU.is_equal).then_inc(hot, 1)
                nc.vector.tensor_tensor(hot_lo[:], lo_e, iota_bf[:, NB:NB + SLOT_LO].unsqueeze(1).to_broadcast([PART, NB, SLOT_LO]),
                                        ALU.is_equal).then_inc(hot, 1)

            def weighted_one_hots(e):
                dve.wait_ge(hot, e * STEP_HOT + 2)
                nc.vector.tensor_tensor(hot_id[:, :, 0, :], hot_lo[:], iota_bf[:, 0:NB].unsqueeze(2).to_broadcast([PART, NB, SLOT_LO]),
                                        ALU.mult).then_inc(hot, 1)
                nc.vector.tensor_scalar(hot_id[:, :, 1, :], hot_lo[:], row_f[:, 0:1], None, ALU.mult).then_inc(hot_ok, 1)

            def token_ids(e):
                dve.wait_ge(id_mm, e + 1)
                nc.vector.tensor_copy(id_f[:], c_ps[0:SLOT_HI, 0:2 * SLOT_LO].rearrange("p (m l) -> p m l", m=2)).then_inc(id_cp, 1)
                dve.wait_ge(id_cp, e + 1)
                dve.wait_ge(id_st, e * 16 + 1)
                nc.vector.scalar_tensor_tensor(out=id_i[:], in0=id_f[:, 0], scalar=float(PART), in1=id_f[:, 1],
                                               op0=ALU.mult, op1=ALU.add).then_inc(id_ok, 1)

            def batch_of_slots(n, u):
                dve.wait_ge(id_ld[u], n * 16 + 16)
                e = n * 2 + u
                nc.vector.tensor_scalar(slot_batch[:, bass.ds(e, 1), :], slots[:, bass.ds(e, 1), :], P.bit_length() - 1, None,
                                        ALU.logical_shift_right).then_inc(sb_ok, 1)

            one_hots(0)
            weighted_one_hots(0)
            token_ids(0)
            one_hots(1)
            weighted_one_hots(1)
            batch_of_slots(0, 0)
            token_ids(1)

            def rows_low(e):
                for t in range(KT):
                    dve.wait_ge(rt_ev, e * KT + t + 1)
                    nc.vector.tensor_tensor(rows_lo[:, t, :], a_ps[t][:, 0:TK], rows_hi[:, t, :].bitcast(F32), ALU.subtract).then_inc(rt_lo_ok, 1)

            rows_low(0)

            def experts(ep, more):
                for u in range(2):
                    e = ep * 2 + u
                    dve.wait_ge(got[u], (ep + 1) * (32 * ST))
                    nc.vector.tensor_copy(weight[u][:], rows[u][:, :, bass.ds(e + D, 1)].rearrange("p s o -> p (s o)")).then_inc(g_cp, 1)
                    dve.wait_ge(g_cp, e + 1)
                    def hidden_low(f):
                        dve.wait_ge(hid_hi_ok, e * FT + f + 1)
                        nc.vector.tensor_tensor(hid_lo[:, f, :], hid[:, f % 2, :], hid_hi[:, f, :].bitcast(F32), ALU.subtract).then_inc(hid_lo_ok, 1)

                    for f in range(FT):
                        hidden_low(f)
                        if f == 4 and u == 0:
                            batch_of_slots(ep, 1)
                        if f == 4 and u == 1 and more:
                            batch_of_slots(ep + 1, 0)
                        if f == 5 and more:
                            one_hots(e + 2)
                    if more:
                        weighted_one_hots(e + 2)
                    if more or u == 0:
                        for i, (raw, low, high) in enumerate(((w1_sb, w1_lo, w1_hi), (w2_sb, w2_lo, w2_hi))):
                            dve.wait_ge(w_hi_ok, e * 2 + i + 3)
                            nc.vector.tensor_tensor(low[1 - u][:], raw[:], high[1 - u][:].bitcast(F32), ALU.subtract).then_inc(w_lo_ok, 1)
                    if more:
                        token_ids(e + 2)
                    if more or u == 0:
                        rows_low(e + 1)
                    dve.wait_ge(contrib_free, e + 1)
                    for s in range(ST):
                        n = e * ST + s
                        dve.wait_ge(y_mm, n + 1)
                        nc.vector.tensor_tensor(contrib[u][:, s, :], (z_ps, c_ps)[s % 2][:, 0:D], b2_sb[u][:], ALU.add).then_inc(y_b, 1)
                        dve.wait_ge(y_b, n + 3)
                        nc.vector.scalar_tensor_tensor(out=contrib[u][:, s, :], in0=contrib[u][:, s, :], scalar=weight[u][:, s:s + 1],
                                                       in1=gates[u][:, s, :], op0=ALU.mult, op1=ALU.mult).then_inc(y_ok, 1)

            with dve.Fori(0, E // 2 - 1) as ep:
                experts(ep, True)
            experts(E // 2 - 1, False)

        @block.tensor
        def _(pe):
            pe.wait_ge(cst, 5)
            with pe.Fori(0, TOP_BIT + 1) as i:
                pe.wait_ge(cnt_in, i + 1)
                for n in range(0, NB, CHUNK):
                    mm = nc.tensor.matmul(c_ps[:, 0:E * CHUNK], ones_bf[:], mask[:, 0, :, n:n + CHUNK],
                                          start=(n == 0), stop=(n == NB - CHUNK))
                mm.then_inc(cnt_mm, 1)
            pe.wait_ge(mask_ok, 2)
            for m in range(2):
                src = mask[:, m].rearrange("p e n -> p (e n)")
                nc.tensor.matmul(a_ps[m][:, 0:EB], before_bf[:], src, start=True, stop=True)
                mm = nc.tensor.matmul(a_ps[2 + m][:, 0:EB], ones_bf[:], src, start=True, stop=True)
            mm.then_inc(rank_mm, 1)
            def slot_tokens(e):
                pe.wait_ge(hot_ok, e + 1)
                for n in range(NB):
                    mm = nc.tensor.matmul(c_ps[0:SLOT_HI, 0:2 * SLOT_LO], hot_hi[:, n, :], hot_id[:, n].rearrange("p m l -> p (m l)"),
                                          start=(n == 0), stop=(n == NB - 1))
                mm.then_inc(id_mm, 1)

            def turn_rows(turn, u):
                pe.wait_ge(got[u], (turn + 1) * (32 * ST))
                for t in range(KT):
                    for s in range(ST):
                        mm = nc.tensor.transpose(a_ps[t][:, s * PART:(s + 1) * PART], rows[u][:, s, t * PART:(t + 1) * PART], ident[:])
                    mm.then_inc(rt_mm, 1)

            def experts(ep, more):
                for u in range(2):
                    e = ep * 2 + u
                    pe.wait_ge(w_lo_ok, e * 2 + 1)
                    pe.wait_ge(rt_lo_ok, e * KT + KT)
                    for f in range(FT):
                        if f >= 4:
                            pe.wait_ge(hid_ok, e * FT + f - 3)
                        for i, (w, r) in enumerate(((w1_hi[u], rows_hi), (w1_lo[u], rows_hi), (w1_hi[u], rows_lo))):
                            for t in range(KT):
                                mm = nc.tensor.matmul(a_ps[f % 4][:, 0:TK], w[:, t, f * PART:(f + 1) * PART], r[:, t, :],
                                                      start=(i == 0 and t == 0), stop=(i == 2 and t == KT - 1))
                        mm.then_inc(hid_mm, 1)
                    pe.wait_ge(w_lo_ok, e * 2 + 2)
                    for t in range(KT):
                        pe.wait_ge(yt_ev, e * KT + t + 1)
                        for f in range(FT):
                            if t == 0:
                                pe.wait_ge(hid_lo_ok, e * FT + f + 3)
                            for i, (w, h) in enumerate(((w2_hi[u], hid_hi), (w2_lo[u], hid_hi), (w2_hi[u], hid_lo))):
                                mm = nc.tensor.matmul(y_ps[t][:, 0:TK], w[:, f, t * PART:(t + 1) * PART], h[:, f, :],
                                                      start=(i == 0 and f == 0), stop=(i == 2 and f == FT - 1))
                        mm.then_inc(yt_mm, 1)
                    if more:
                        slot_tokens(e + 2)
                    if more or u == 0:
                        turn_rows(ep + u, 1 - u)
                    for s in range(ST):
                        if s == 0:
                            pe.wait_ge(yt_ev, e * KT + 2 * KT)
                        if s == 1 and more:
                            pe.wait_ge(id_cp, e + 3)
                        pe.wait_ge(y_b, e * ST + s + 1)
                        for t in range(KT):
                            mm = nc.tensor.transpose((z_ps, c_ps)[s % 2][:, t * PART:(t + 1) * PART],
                                                     y_t[:, t, s * PART:(s + 1) * PART], ident[:])
                        mm.then_inc(y_mm, 1)

            pe.sem_inc(yt_ev, KT)
            slot_tokens(0)
            slot_tokens(1)
            turn_rows(0, 0)
            with pe.Fori(0, E // 2 - 1) as ep:
                experts(ep, True)
            experts(E // 2 - 1, False)


_INS = ['L0_attn_inputs', 'L0_attn_w_qkv', 'L0_attn_w_o', 'L0_ffn_router_w', 'L0_ffn_router_b', 'L0_ffn_w1', 'L0_ffn_b1', 'L0_ffn_w2', 'L0_ffn_b2', 'L0_c', 'L0_wmod']
TOPK = 512


def kernel(**inputs):
    import numpy as _np
    import concourse.bacc as _bacc
    from concourse import mybir as _mybir
    from concourse.bass_utils import run_bass_kernel_spmd as _run

    nc = _bacc.Bacc("TRN2", target_bir_lowering=False, num_devices=1)
    arrays, args = {}, []
    for name in _INS:
        a = _np.ascontiguousarray(inputs[name])
        arrays[f"in_{name}_dram"] = a
        args.append(nc.dram_tensor(f"in_{name}_dram", a.shape, _mybir.dt.from_np(a.dtype), kind="ExternalInput").ap())
    shape = tuple(inputs['L0_attn_inputs'].shape)
    out = nc.dram_tensor("out_0_dram", shape, _mybir.dt.from_np(_np.dtype('float32')), kind="ExternalOutput").ap()
    build_kernel(nc, *args, out, TOPK)
    r = _run(nc, [arrays], core_ids=[0])
    return r.results[0]["out_0_dram"]
```
